# Optimizing a Trainium2 kernel written in Bass

```python
import numpy as np
import jax
import jax.numpy as jnp

def _softmax(x, axis=-1):
    return jax.nn.softmax(x, axis=axis)

def _gelu(x):
    return jax.nn.gelu(x, approximate=True)

def _silu(x):
    return jax.nn.silu(x)

def _sigmoid(x):
    return jax.nn.sigmoid(x)

def _layernorm(x, axis=-1, eps=1e-05):
    m = jnp.mean(x, axis=axis, keepdims=True)
    v = jnp.var(x, axis=axis, keepdims=True)
    return (x - m) / jnp.sqrt(v + eps)

def _scatter_add(tgt, idx, src, axis=0):
    return tgt.at[idx].add(src)

def _segment_sum(src, seg, n):
    return jax.ops.segment_sum(src, seg, n)
kernel_name = 'mk_adaln_ffn_d4_seqx_r8_114473'

def setup_inputs(seed: int=0):
    np.random.seed(seed)
    _w = jnp.asarray

    def _rec_inputs():
        import jax
        import jax.numpy as jnp
        _rk = jax.random.key(seed)
        x = -0.0003929 + 0.9999 * jax.random.normal(jax.random.fold_in(_rk, 1), (128, 32, 512), jnp.float32)
        _lenS = 32 - jax.random.randint(jax.random.fold_in(_rk, 7), (128,), 0, max(1, 32 // 4) + 1, jnp.int32)
        _lenS2 = 32 - jax.random.randint(jax.random.fold_in(_rk, 8), (128,), 0, max(1, 32 // 4) + 1, jnp.int32)
        cond_512 = 0.00782532 + 1.00527 * jax.random.normal(jax.random.fold_in(_rk, 11), (128, 64), jnp.float32)
        return (x, cond_512)
    x, cond_512 = _rec_inputs()

    def _L0_cond_setup():
        import jax, jax.numpy as jnp
        from jax import lax
        import numpy as np
        CIN, COUT, K, STYLE_DIM = (32, 32, 3, 64)
        N_LAYERS = 4
        TYPES = ('same', 'upsample', 'same', 'downsample')
        SCALE = 1.0 / float(np.sqrt(CIN * K ** 2))
        EPS = 1e-08
        _BK = np.array([1.0, 3.0, 3.0, 1.0], dtype=np.float32)
        BLUR_K = _BK / _BK.sum()

        def _blur(x, kern, pad):
            B, C, _ = x.shape
            xp = jnp.pad(x, ((0, 0), (0, 0), (pad[0], pad[1])))
            w = jnp.broadcast_to(kern.astype(x.dtype)[None, None, :], (C, 1, kern.shape[0]))
            return lax.conv_general_dilated(xp, w, (1,), 'VALID', feature_group_count=C, dimension_numbers=('NCH', 'OIH', 'NCH'))

        def _conv_same(x, w):
            p = (K - 1) // 2
            return lax.conv_general_dilated(x[None], w, (1,), [(p, p)], dimension_numbers=('NCH', 'OIH', 'NCH'))[0]

        def _conv_down(x, w):
            return lax.conv_general_dilated(x[None], w, (2,), 'VALID', dimension_numbers=('NCH', 'OIH', 'NCH'))[0]

        def _conv_up(x, w_t):
            return lax.conv_transpose(x[None], w_t, (2,), 'VALID', dimension_numbers=('NCH', 'IOH', 'NCH'), transpose_kernel=True)[0]

        def _layer(x, style, w, b, mw, mb, typ):
            s = style @ mw.T + mb
            weight = SCALE * w * s[:, None, :, None]
            demod = lax.rsqrt(jnp.sum(weight * weight, axis=(2, 3)) + EPS)
            weight = weight * demod[:, :, None, None]
            blur_k = jnp.asarray(BLUR_K)
            if typ == 'same':
                out = jax.vmap(_conv_same)(x, weight) + b[None, :, None]
            elif typ == 'upsample':
                out = jax.vmap(_conv_up)(x, weight.transpose(0, 2, 1, 3)) + b[None, :, None]
                out = _blur(out, 2.0 * blur_k, (1, 1))
            elif typ == 'downsample':
                xb = _blur(x, blur_k, (2, 2))
                out = jax.vmap(_conv_down)(xb, weight) + b[None, :, None]
            else:
                raise NotImplementedError(typ)
            return out
        key = jax.random.key(seed)
        ks = jax.random.split(key, 6)
        B, L = (16, 512)
        return {'x': jax.random.normal(ks[0], (B, CIN, L), dtype=jnp.float32), 'style': jax.random.normal(ks[1], (B, STYLE_DIM), dtype=jnp.float32), 'weights': jax.random.normal(ks[2], (N_LAYERS, COUT, CIN, K), dtype=jnp.float32), 'biases': jax.random.normal(ks[3], (N_LAYERS, COUT), dtype=jnp.float32) * 0.1, 'mod_w': jax.random.normal(ks[4], (N_LAYERS, CIN, STYLE_DIM), dtype=jnp.float32) / np.sqrt(STYLE_DIM), 'mod_b': 1.0 + 0.1 * jax.random.normal(ks[5], (N_LAYERS, CIN), dtype=jnp.float32)}
    _L0_cond_all = _L0_cond_setup()
    _L0_cond_in = {k: v for k, v in _L0_cond_all.items() if k in ('weights', 'biases', 'mod_w', 'mod_b')}
    del _L0_cond_all

    def _L0_ffn_setup():
        import jax, jax.numpy as jnp
        import numpy as np
        key = jax.random.key(seed)
        k = jax.random.split(key, 6)
        x = jax.random.normal(k[0], (4, 256, 512), jnp.float32)
        W = jax.random.normal(k[1], (512, 512), jnp.float32) * 0.02
        bias = jax.random.normal(k[2], (512,), jnp.float32) * 0.02
        A = jax.random.normal(k[3], (16, 16, 512), jnp.float32) * 0.02
        Bf = jax.random.normal(k[4], (16, 512, 16), jnp.float32) * 0.02
        coeffs = jax.random.uniform(k[5], (16,), jnp.float32)
        scales = jnp.full((16,), 0.5, jnp.float32)
        return {'x': x, 'W': W, 'bias': bias, 'A': A, 'Bf': Bf, 'coeffs': coeffs, 'scales': scales}
    _L0_ffn_all = _L0_ffn_setup()
    _L0_ffn_in = {k: v for k, v in _L0_ffn_all.items() if k in ('W', 'bias', 'A', 'Bf', 'coeffs', 'scales')}
    del _L0_ffn_all

    def _L1_cond_setup():
        import jax, jax.numpy as jnp
        from jax import lax
        import numpy as np
        CIN, COUT, K, STYLE_DIM = (32, 32, 3, 64)
        N_LAYERS = 4
        TYPES = ('same', 'upsample', 'same', 'downsample')
        SCALE = 1.0 / float(np.sqrt(CIN * K ** 2))
        EPS = 1e-08
        _BK = np.array([1.0, 3.0, 3.0, 1.0], dtype=np.float32)
        BLUR_K = _BK / _BK.sum()

        def _blur(x, kern, pad):
            B, C, _ = x.shape
            xp = jnp.pad(x, ((0, 0), (0, 0), (pad[0], pad[1])))
            w = jnp.broadcast_to(kern.astype(x.dtype)[None, None, :], (C, 1, kern.shape[0]))
            return lax.conv_general_dilated(xp, w, (1,), 'VALID', feature_group_count=C, dimension_numbers=('NCH', 'OIH', 'NCH'))

        def _conv_same(x, w):
            p = (K - 1) // 2
            return lax.conv_general_dilated(x[None], w, (1,), [(p, p)], dimension_numbers=('NCH', 'OIH', 'NCH'))[0]

        def _conv_down(x, w):
            return lax.conv_general_dilated(x[None], w, (2,), 'VALID', dimension_numbers=('NCH', 'OIH', 'NCH'))[0]

        def _conv_up(x, w_t):
            return lax.conv_transpose(x[None], w_t, (2,), 'VALID', dimension_numbers=('NCH', 'IOH', 'NCH'), transpose_kernel=True)[0]

        def _layer(x, style, w, b, mw, mb, typ):
            s = style @ mw.T + mb
            weight = SCALE * w * s[:, None, :, None]
            demod = lax.rsqrt(jnp.sum(weight * weight, axis=(2, 3)) + EPS)
            weight = weight * demod[:, :, None, None]
            blur_k = jnp.asarray(BLUR_K)
            if typ == 'same':
                out = jax.vmap(_conv_same)(x, weight) + b[None, :, None]
            elif typ == 'upsample':
                out = jax.vmap(_conv_up)(x, weight.transpose(0, 2, 1, 3)) + b[None, :, None]
                out = _blur(out, 2.0 * blur_k, (1, 1))
            elif typ == 'downsample':
                xb = _blur(x, blur_k, (2, 2))
                out = jax.vmap(_conv_down)(xb, weight) + b[None, :, None]
            else:
                raise NotImplementedError(typ)
            return out
        key = jax.random.key(seed)
        ks = jax.random.split(key, 6)
        B, L = (16, 512)
        return {'x': jax.random.normal(ks[0], (B, CIN, L), dtype=jnp.float32), 'style': jax.random.normal(ks[1], (B, STYLE_DIM), dtype=jnp.float32), 'weights': jax.random.normal(ks[2], (N_LAYERS, COUT, CIN, K), dtype=jnp.float32), 'biases': jax.random.normal(ks[3], (N_LAYERS, COUT), dtype=jnp.float32) * 0.1, 'mod_w': jax.random.normal(ks[4], (N_LAYERS, CIN, STYLE_DIM), dtype=jnp.float32) / np.sqrt(STYLE_DIM), 'mod_b': 1.0 + 0.1 * jax.random.normal(ks[5], (N_LAYERS, CIN), dtype=jnp.float32)}
    _L1_cond_all = _L1_cond_setup()
    _L1_cond_in = {k: v for k, v in _L1_cond_all.items() if k in ('weights', 'biases', 'mod_w', 'mod_b')}
    del _L1_cond_all

    def _L1_ffn_setup():
        import jax, jax.numpy as jnp
        import numpy as np
        B, S, D, O, E, R = (2, 512, 512, 512, 8, 16)
        TOP_K = 2
        SCALING = 32.0 / 16.0
        key = jax.random.key(seed)
        k = jax.random.split(key, 6)
        x = jax.random.normal(k[0], (B, S, D), dtype=jnp.float32)
        W_base = jax.random.normal(k[1], (O, D), dtype=jnp.float32) * 0.02
        b_base = jax.random.normal(k[2], (O,), dtype=jnp.float32) * 0.02
        W_router = jax.random.normal(k[3], (E, D), dtype=jnp.float32) * 0.01
        lora_A = jax.random.normal(k[4], (E, R, D), dtype=jnp.float32) * (1.0 / np.sqrt(D))
        lora_B = jax.random.normal(k[5], (E, O, R), dtype=jnp.float32) * 0.02
        return {'x': x, 'W_base': W_base, 'b_base': b_base, 'W_router': W_router, 'lora_A': lora_A, 'lora_B': lora_B}
    _L1_ffn_all = _L1_ffn_setup()
    _L1_ffn_in = {k: v for k, v in _L1_ffn_all.items() if k in ('W_base', 'b_base', 'W_router', 'lora_A', 'lora_B')}
    del _L1_ffn_all

    def _L2_cond_setup():
        import jax, jax.numpy as jnp
        from jax import lax
        import numpy as np
        CIN, COUT, K, STYLE_DIM = (32, 32, 3, 64)
        N_LAYERS = 4
        TYPES = ('same', 'upsample', 'same', 'downsample')
        SCALE = 1.0 / float(np.sqrt(CIN * K ** 2))
        EPS = 1e-08
        _BK = np.array([1.0, 3.0, 3.0, 1.0], dtype=np.float32)
        BLUR_K = _BK / _BK.sum()

        def _blur(x, kern, pad):
            B, C, _ = x.shape
            xp = jnp.pad(x, ((0, 0), (0, 0), (pad[0], pad[1])))
            w = jnp.broadcast_to(kern.astype(x.dtype)[None, None, :], (C, 1, kern.shape[0]))
            return lax.conv_general_dilated(xp, w, (1,), 'VALID', feature_group_count=C, dimension_numbers=('NCH', 'OIH', 'NCH'))

        def _conv_same(x, w):
            p = (K - 1) // 2
            return lax.conv_general_dilated(x[None], w, (1,), [(p, p)], dimension_numbers=('NCH', 'OIH', 'NCH'))[0]

        def _conv_down(x, w):
            return lax.conv_general_dilated(x[None], w, (2,), 'VALID', dimension_numbers=('NCH', 'OIH', 'NCH'))[0]

        def _conv_up(x, w_t):
            return lax.conv_transpose(x[None], w_t, (2,), 'VALID', dimension_numbers=('NCH', 'IOH', 'NCH'), transpose_kernel=True)[0]

        def _layer(x, style, w, b, mw, mb, typ):
            s = style @ mw.T + mb
            weight = SCALE * w * s[:, None, :, None]
            demod = lax.rsqrt(jnp.sum(weight * weight, axis=(2, 3)) + EPS)
            weight = weight * demod[:, :, None, None]
            blur_k = jnp.asarray(BLUR_K)
            if typ == 'same':
                out = jax.vmap(_conv_same)(x, weight) + b[None, :, None]
            elif typ == 'upsample':
                out = jax.vmap(_conv_up)(x, weight.transpose(0, 2, 1, 3)) + b[None, :, None]
                out = _blur(out, 2.0 * blur_k, (1, 1))
            elif typ == 'downsample':
                xb = _blur(x, blur_k, (2, 2))
                out = jax.vmap(_conv_down)(xb, weight) + b[None, :, None]
            else:
                raise NotImplementedError(typ)
            return out
        key = jax.random.key(seed)
        ks = jax.random.split(key, 6)
        B, L = (16, 512)
        return {'x': jax.random.normal(ks[0], (B, CIN, L), dtype=jnp.float32), 'style': jax.random.normal(ks[1], (B, STYLE_DIM), dtype=jnp.float32), 'weights': jax.random.normal(ks[2], (N_LAYERS, COUT, CIN, K), dtype=jnp.float32), 'biases': jax.random.normal(ks[3], (N_LAYERS, COUT), dtype=jnp.float32) * 0.1, 'mod_w': jax.random.normal(ks[4], (N_LAYERS, CIN, STYLE_DIM), dtype=jnp.float32) / np.sqrt(STYLE_DIM), 'mod_b': 1.0 + 0.1 * jax.random.normal(ks[5], (N_LAYERS, CIN), dtype=jnp.float32)}
    _L2_cond_all = _L2_cond_setup()
    _L2_cond_in = {k: v for k, v in _L2_cond_all.items() if k in ('weights', 'biases', 'mod_w', 'mod_b')}
    del _L2_cond_all

    def _L2_ffn_setup():
        import jax, jax.numpy as jnp
        import numpy as np
        B, T, D_IN, D_OUT = (8, 256, 512, 512)
        N_LORAS, RANK = (16, 32)
        SCALING = 1.0
        key = jax.random.key(seed)
        ks = jax.random.split(key, 8)
        std = 1.0 / D_IN ** 0.5
        x = jax.random.normal(ks[0], (B, T, D_IN), dtype=jnp.float32)
        idx = jax.random.randint(ks[1], (B,), 0, N_LORAS)
        gate = jax.nn.one_hot(idx, N_LORAS, dtype=jnp.float32)
        kernel = jax.random.normal(ks[2], (D_IN, D_OUT), dtype=jnp.float32) * std
        bias = jnp.zeros((D_OUT,), dtype=jnp.float32)
        lora_A = jax.random.normal(ks[3], (N_LORAS, RANK, D_IN), dtype=jnp.float32) * std
        lora_B = jax.random.normal(ks[4], (N_LORAS, D_OUT, RANK), dtype=jnp.float32) * 0.01
        lora_A_shared = jax.random.normal(ks[5], (RANK, D_IN), dtype=jnp.float32) * std
        lora_B_shared = jax.random.normal(ks[6], (D_OUT, RANK), dtype=jnp.float32) * 0.01
        return {'x': x, 'gate': gate, 'kernel': kernel, 'bias': bias, 'lora_A': lora_A, 'lora_B': lora_B, 'lora_A_shared': lora_A_shared, 'lora_B_shared': lora_B_shared}
    _L2_ffn_all = _L2_ffn_setup()
    _L2_ffn_in = {k: v for k, v in _L2_ffn_all.items() if k in ('gate', 'kernel', 'bias', 'lora_A', 'lora_B', 'lora_A_shared', 'lora_B_shared')}
    del _L2_ffn_all

    def _L3_cond_setup():
        import jax, jax.numpy as jnp
        from jax import lax
        import numpy as np
        CIN, COUT, K, STYLE_DIM = (32, 32, 3, 64)
        N_LAYERS = 4
        TYPES = ('same', 'upsample', 'same', 'downsample')
        SCALE = 1.0 / float(np.sqrt(CIN * K ** 2))
        EPS = 1e-08
        _BK = np.array([1.0, 3.0, 3.0, 1.0], dtype=np.float32)
        BLUR_K = _BK / _BK.sum()

        def _blur(x, kern, pad):
            B, C, _ = x.shape
            xp = jnp.pad(x, ((0, 0), (0, 0), (pad[0], pad[1])))
            w = jnp.broadcast_to(kern.astype(x.dtype)[None, None, :], (C, 1, kern.shape[0]))
            return lax.conv_general_dilated(xp, w, (1,), 'VALID', feature_group_count=C, dimension_numbers=('NCH', 'OIH', 'NCH'))

        def _conv_same(x, w):
            p = (K - 1) // 2
            return lax.conv_general_dilated(x[None], w, (1,), [(p, p)], dimension_numbers=('NCH', 'OIH', 'NCH'))[0]

        def _conv_down(x, w):
            return lax.conv_general_dilated(x[None], w, (2,), 'VALID', dimension_numbers=('NCH', 'OIH', 'NCH'))[0]

        def _conv_up(x, w_t):
            return lax.conv_transpose(x[None], w_t, (2,), 'VALID', dimension_numbers=('NCH', 'IOH', 'NCH'), transpose_kernel=True)[0]

        def _layer(x, style, w, b, mw, mb, typ):
            s = style @ mw.T + mb
            weight = SCALE * w * s[:, None, :, None]
            demod = lax.rsqrt(jnp.sum(weight * weight, axis=(2, 3)) + EPS)
            weight = weight * demod[:, :, None, None]
            blur_k = jnp.asarray(BLUR_K)
            if typ == 'same':
                out = jax.vmap(_conv_same)(x, weight) + b[None, :, None]
            elif typ == 'upsample':
                out = jax.vmap(_conv_up)(x, weight.transpose(0, 2, 1, 3)) + b[None, :, None]
                out = _blur(out, 2.0 * blur_k, (1, 1))
            elif typ == 'downsample':
                xb = _blur(x, blur_k, (2, 2))
                out = jax.vmap(_conv_down)(xb, weight) + b[None, :, None]
            else:
                raise NotImplementedError(typ)
            return out
        key = jax.random.key(seed)
        ks = jax.random.split(key, 6)
        B, L = (16, 512)
        return {'x': jax.random.normal(ks[0], (B, CIN, L), dtype=jnp.float32), 'style': jax.random.normal(ks[1], (B, STYLE_DIM), dtype=jnp.float32), 'weights': jax.random.normal(ks[2], (N_LAYERS, COUT, CIN, K), dtype=jnp.float32), 'biases': jax.random.normal(ks[3], (N_LAYERS, COUT), dtype=jnp.float32) * 0.1, 'mod_w': jax.random.normal(ks[4], (N_LAYERS, CIN, STYLE_DIM), dtype=jnp.float32) / np.sqrt(STYLE_DIM), 'mod_b': 1.0 + 0.1 * jax.random.normal(ks[5], (N_LAYERS, CIN), dtype=jnp.float32)}
    _L3_cond_all = _L3_cond_setup()
    _L3_cond_in = {k: v for k, v in _L3_cond_all.items() if k in ('weights', 'biases', 'mod_w', 'mod_b')}
    del _L3_cond_all

    def _L3_ffn_setup():
        import jax, jax.numpy as jnp
        import numpy as np
        NUM_EXPERTS = 4
        HIDDEN = 512
        RANK = 8
        ALPHA = 8.0
        SCALE = ALPHA / RANK
        key = jax.random.key(seed)
        ks = jax.random.split(key, 6)
        B, T, H, E, R = (4, 512, HIDDEN, NUM_EXPERTS, RANK)
        x = jax.random.normal(ks[0], (B, T, H), dtype=jnp.float32)
        W_up = jax.random.normal(ks[1], (H, H), dtype=jnp.float32) / np.sqrt(H)
        gate_w = jax.random.normal(ks[2], (E, H), dtype=jnp.float32) / np.sqrt(H)
        expert_bias = jnp.zeros((E,), dtype=jnp.float32)
        lora_A = jax.random.normal(ks[3], (E, R, H), dtype=jnp.float32) / np.sqrt(H)
        lora_B = jax.random.normal(ks[4], (E, H, R), dtype=jnp.float32) * 0.01
        return {'x': x, 'W_up': W_up, 'gate_w': gate_w, 'expert_bias': expert_bias, 'lora_A': lora_A, 'lora_B': lora_B}
    _L3_ffn_all = _L3_ffn_setup()
    _L3_ffn_in = {k: v for k, v in _L3_ffn_all.items() if k in ('W_up', 'gate_w', 'expert_bias', 'lora_A', 'lora_B')}
    del _L3_ffn_all
    return {'x': x, 'cond_512': cond_512, 'L0_cond_weights': _L0_cond_in['weights'], 'L0_cond_biases': _L0_cond_in['biases'], 'L0_cond_mod_w': _L0_cond_in['mod_w'], 'L0_cond_mod_b': _L0_cond_in['mod_b'], 'L0_ffn_W': _L0_ffn_in['W'], 'L0_ffn_bias': _L0_ffn_in['bias'], 'L0_ffn_A': _L0_ffn_in['A'], 'L0_ffn_Bf': _L0_ffn_in['Bf'], 'L0_ffn_coeffs': _L0_ffn_in['coeffs'], 'L0_ffn_scales': _L0_ffn_in['scales'], 'L1_cond_weights': _L1_cond_in['weights'], 'L1_cond_biases': _L1_cond_in['biases'], 'L1_cond_mod_w': _L1_cond_in['mod_w'], 'L1_cond_mod_b': _L1_cond_in['mod_b'], 'L1_ffn_W_base': _L1_ffn_in['W_base'], 'L1_ffn_b_base': _L1_ffn_in['b_base'], 'L1_ffn_W_router': _L1_ffn_in['W_router'], 'L1_ffn_lora_A': _L1_ffn_in['lora_A'], 'L1_ffn_lora_B': _L1_ffn_in['lora_B'], 'L2_cond_weights': _L2_cond_in['weights'], 'L2_cond_biases': _L2_cond_in['biases'], 'L2_cond_mod_w': _L2_cond_in['mod_w'], 'L2_cond_mod_b': _L2_cond_in['mod_b'], 'L2_ffn_gate': _L2_ffn_in['gate'], 'L2_ffn_kernel': _L2_ffn_in['kernel'], 'L2_ffn_bias': _L2_ffn_in['bias'], 'L2_ffn_lora_A': _L2_ffn_in['lora_A'], 'L2_ffn_lora_B': _L2_ffn_in['lora_B'], 'L2_ffn_lora_A_shared': _L2_ffn_in['lora_A_shared'], 'L2_ffn_lora_B_shared': _L2_ffn_in['lora_B_shared'], 'L3_cond_weights': _L3_cond_in['weights'], 'L3_cond_biases': _L3_cond_in['biases'], 'L3_cond_mod_w': _L3_cond_in['mod_w'], 'L3_cond_mod_b': _L3_cond_in['mod_b'], 'L3_ffn_W_up': _L3_ffn_in['W_up'], 'L3_ffn_gate_w': _L3_ffn_in['gate_w'], 'L3_ffn_expert_bias': _L3_ffn_in['expert_bias'], 'L3_ffn_lora_A': _L3_ffn_in['lora_A'], 'L3_ffn_lora_B': _L3_ffn_in['lora_B']}

def reference(x, cond_512, L0_cond_weights, L0_cond_biases, L0_cond_mod_w, L0_cond_mod_b, L0_ffn_W, L0_ffn_bias, L0_ffn_A, L0_ffn_Bf, L0_ffn_coeffs, L0_ffn_scales, L1_cond_weights, L1_cond_biases, L1_cond_mod_w, L1_cond_mod_b, L1_ffn_W_base, L1_ffn_b_base, L1_ffn_W_router, L1_ffn_lora_A, L1_ffn_lora_B, L2_cond_weights, L2_cond_biases, L2_cond_mod_w, L2_cond_mod_b, L2_ffn_gate, L2_ffn_kernel, L2_ffn_bias, L2_ffn_lora_A, L2_ffn_lora_B, L2_ffn_lora_A_shared, L2_ffn_lora_B_shared, L3_cond_weights, L3_cond_biases, L3_cond_mod_w, L3_cond_mod_b, L3_ffn_W_up, L3_ffn_gate_w, L3_ffn_expert_bias, L3_ffn_lora_A, L3_ffn_lora_B):
    import jax
    import jax.numpy as jnp

    def _L0_cond_ref(x, style, weights, biases, mod_w, mod_b):
        import jax, jax.numpy as jnp
        from jax import lax
        import numpy as np
        CIN, COUT, K, STYLE_DIM = (32, 32, 3, 64)
        N_LAYERS = 4
        TYPES = ('same', 'upsample', 'same', 'downsample')
        SCALE = 1.0 / float(np.sqrt(CIN * K ** 2))
        EPS = 1e-08
        _BK = np.array([1.0, 3.0, 3.0, 1.0], dtype=np.float32)
        BLUR_K = _BK / _BK.sum()

        def _blur(x, kern, pad):
            B, C, _ = x.shape
            xp = jnp.pad(x, ((0, 0), (0, 0), (pad[0], pad[1])))
            w = jnp.broadcast_to(kern.astype(x.dtype)[None, None, :], (C, 1, kern.shape[0]))
            return lax.conv_general_dilated(xp, w, (1,), 'VALID', feature_group_count=C, dimension_numbers=('NCH', 'OIH', 'NCH'))

        def _conv_same(x, w):
            p = (K - 1) // 2
            return lax.conv_general_dilated(x[None], w, (1,), [(p, p)], dimension_numbers=('NCH', 'OIH', 'NCH'))[0]

        def _conv_down(x, w):
            return lax.conv_general_dilated(x[None], w, (2,), 'VALID', dimension_numbers=('NCH', 'OIH', 'NCH'))[0]

        def _conv_up(x, w_t):
            return lax.conv_transpose(x[None], w_t, (2,), 'VALID', dimension_numbers=('NCH', 'IOH', 'NCH'), transpose_kernel=True)[0]

        def _layer(x, style, w, b, mw, mb, typ):
            s = style @ mw.T + mb
            weight = SCALE * w * s[:, None, :, None]
            demod = lax.rsqrt(jnp.sum(weight * weight, axis=(2, 3)) + EPS)
            weight = weight * demod[:, :, None, None]
            blur_k = jnp.asarray(BLUR_K)
            if typ == 'same':
                out = jax.vmap(_conv_same)(x, weight) + b[None, :, None]
            elif typ == 'upsample':
                out = jax.vmap(_conv_up)(x, weight.transpose(0, 2, 1, 3)) + b[None, :, None]
                out = _blur(out, 2.0 * blur_k, (1, 1))
            elif typ == 'downsample':
                xb = _blur(x, blur_k, (2, 2))
                out = jax.vmap(_conv_down)(xb, weight) + b[None, :, None]
            else:
                raise NotImplementedError(typ)
            return out
        out = x
        for i, typ in enumerate(TYPES):
            out = _layer(out, style, weights[i], biases[i], mod_w[i], mod_b[i], typ)
        return out

    def _L0_ffn_ref(x, W, bias, A, Bf, coeffs, scales):
        import jax, jax.numpy as jnp
        import numpy as np
        out = jnp.einsum('bsd,od->bso', x, W) + bias
        xa = jnp.einsum('bsd,erd->ebsr', x, A)
        w = coeffs * scales
        upd = jnp.einsum('ebsr,eor,e->bso', xa, Bf, w)
        return out + upd

    def _L1_cond_ref(x, style, weights, biases, mod_w, mod_b):
        import jax, jax.numpy as jnp
        from jax import lax
        import numpy as np
        CIN, COUT, K, STYLE_DIM = (32, 32, 3, 64)
        N_LAYERS = 4
        TYPES = ('same', 'upsample', 'same', 'downsample')
        SCALE = 1.0 / float(np.sqrt(CIN * K ** 2))
        EPS = 1e-08
        _BK = np.array([1.0, 3.0, 3.0, 1.0], dtype=np.float32)
        BLUR_K = _BK / _BK.sum()

        def _blur(x, kern, pad):
            B, C, _ = x.shape
            xp = jnp.pad(x, ((0, 0), (0, 0), (pad[0], pad[1])))
            w = jnp.broadcast_to(kern.astype(x.dtype)[None, None, :], (C, 1, kern.shape[0]))
            return lax.conv_general_dilated(xp, w, (1,), 'VALID', feature_group_count=C, dimension_numbers=('NCH', 'OIH', 'NCH'))

        def _conv_same(x, w):
            p = (K - 1) // 2
            return lax.conv_general_dilated(x[None], w, (1,), [(p, p)], dimension_numbers=('NCH', 'OIH', 'NCH'))[0]

        def _conv_down(x, w):
            return lax.conv_general_dilated(x[None], w, (2,), 'VALID', dimension_numbers=('NCH', 'OIH', 'NCH'))[0]

        def _conv_up(x, w_t):
            return lax.conv_transpose(x[None], w_t, (2,), 'VALID', dimension_numbers=('NCH', 'IOH', 'NCH'), transpose_kernel=True)[0]

        def _layer(x, style, w, b, mw, mb, typ):
            s = style @ mw.T + mb
            weight = SCALE * w * s[:, None, :, None]
            demod = lax.rsqrt(jnp.sum(weight * weight, axis=(2, 3)) + EPS)
            weight = weight * demod[:, :, None, None]
            blur_k = jnp.asarray(BLUR_K)
            if typ == 'same':
                out = jax.vmap(_conv_same)(x, weight) + b[None, :, None]
            elif typ == 'upsample':
                out = jax.vmap(_conv_up)(x, weight.transpose(0, 2, 1, 3)) + b[None, :, None]
                out = _blur(out, 2.0 * blur_k, (1, 1))
            elif typ == 'downsample':
                xb = _blur(x, blur_k, (2, 2))
                out = jax.vmap(_conv_down)(xb, weight) + b[None, :, None]
            else:
                raise NotImplementedError(typ)
            return out
        out = x
        for i, typ in enumerate(TYPES):
            out = _layer(out, style, weights[i], biases[i], mod_w[i], mod_b[i], typ)
        return out

    def _L1_ffn_ref(x, W_base, b_base, W_router, lora_A, lora_B):
        import jax, jax.numpy as jnp
        import numpy as np
        B, S, D, O, E, R = (2, 512, 512, 512, 8, 16)
        TOP_K = 2
        SCALING = 32.0 / 16.0
        d = x.shape[-1]
        n_experts = W_router.shape[0]
        xf = x.reshape(-1, d)
        logits = xf @ W_router.T
        probs = jax.nn.softmax(logits, axis=-1)
        topk_p, topk_i = jax.lax.top_k(probs, TOP_K)
        topk_p = topk_p / jnp.sum(topk_p, axis=-1, keepdims=True)
        w = jnp.sum(jax.nn.one_hot(topk_i, n_experts, dtype=xf.dtype) * topk_p[..., None], axis=1)
        h = jnp.einsum('td,erd->ter', xf, lora_A)
        lora_out = jnp.einsum('ter,eor,te->to', h, lora_B, w) * SCALING
        base = x @ W_base.T + b_base
        return base + lora_out.reshape(x.shape[:-1] + (W_base.shape[0],))

    def _L2_cond_ref(x, style, weights, biases, mod_w, mod_b):
        import jax, jax.numpy as jnp
        from jax import lax
        import numpy as np
        CIN, COUT, K, STYLE_DIM = (32, 32, 3, 64)
        N_LAYERS = 4
        TYPES = ('same', 'upsample', 'same', 'downsample')
        SCALE = 1.0 / float(np.sqrt(CIN * K ** 2))
        EPS = 1e-08
        _BK = np.array([1.0, 3.0, 3.0, 1.0], dtype=np.float32)
        BLUR_K = _BK / _BK.sum()

        def _blur(x, kern, pad):
            B, C, _ = x.shape
            xp = jnp.pad(x, ((0, 0), (0, 0), (pad[0], pad[1])))
            w = jnp.broadcast_to(kern.astype(x.dtype)[None, None, :], (C, 1, kern.shape[0]))
            return lax.conv_general_dilated(xp, w, (1,), 'VALID', feature_group_count=C, dimension_numbers=('NCH', 'OIH', 'NCH'))

        def _conv_same(x, w):
            p = (K - 1) // 2
            return lax.conv_general_dilated(x[None], w, (1,), [(p, p)], dimension_numbers=('NCH', 'OIH', 'NCH'))[0]

        def _conv_down(x, w):
            return lax.conv_general_dilated(x[None], w, (2,), 'VALID', dimension_numbers=('NCH', 'OIH', 'NCH'))[0]

        def _conv_up(x, w_t):
            return lax.conv_transpose(x[None], w_t, (2,), 'VALID', dimension_numbers=('NCH', 'IOH', 'NCH'), transpose_kernel=True)[0]

        def _layer(x, style, w, b, mw, mb, typ):
            s = style @ mw.T + mb
            weight = SCALE * w * s[:, None, :, None]
            demod = lax.rsqrt(jnp.sum(weight * weight, axis=(2, 3)) + EPS)
            weight = weight * demod[:, :, None, None]
            blur_k = jnp.asarray(BLUR_K)
            if typ == 'same':
                out = jax.vmap(_conv_same)(x, weight) + b[None, :, None]
            elif typ == 'upsample':
                out = jax.vmap(_conv_up)(x, weight.transpose(0, 2, 1, 3)) + b[None, :, None]
                out = _blur(out, 2.0 * blur_k, (1, 1))
            elif typ == 'downsample':
                xb = _blur(x, blur_k, (2, 2))
                out = jax.vmap(_conv_down)(xb, weight) + b[None, :, None]
            else:
                raise NotImplementedError(typ)
            return out
        out = x
        for i, typ in enumerate(TYPES):
            out = _layer(out, style, weights[i], biases[i], mod_w[i], mod_b[i], typ)
        return out

    def _L2_ffn_ref(x, gate, kernel, bias, lora_A, lora_B, lora_A_shared, lora_B_shared):
        import jax, jax.numpy as jnp
        import numpy as np
        B, T, D_IN, D_OUT = (8, 256, 512, 512)
        N_LORAS, RANK = (16, 32)
        SCALING = 1.0
        base_out = jnp.matmul(x, kernel) + bias
        b = gate.shape[0]
        x_flat = x.reshape(b, -1, x.shape[-1])
        A_eff = jnp.einsum('bn,nri->bri', gate, lora_A)
        B_eff = jnp.einsum('bn,nor->bor', gate, lora_B)
        Ax = jnp.einsum('bri,bti->btr', A_eff, x_flat)
        delta_flat = jnp.einsum('bor,btr->bto', B_eff, Ax)
        Ax_s = jnp.einsum('ri,bti->btr', lora_A_shared, x_flat)
        delta_flat = delta_flat + jnp.einsum('or,btr->bto', lora_B_shared, Ax_s)
        delta = delta_flat.reshape(x.shape[:-1] + (kernel.shape[-1],))
        return base_out + (SCALING * delta).astype(base_out.dtype)

    def _L3_cond_ref(x, style, weights, biases, mod_w, mod_b):
        import jax, jax.numpy as jnp
        from jax import lax
        import numpy as np
        CIN, COUT, K, STYLE_DIM = (32, 32, 3, 64)
        N_LAYERS = 4
        TYPES = ('same', 'upsample', 'same', 'downsample')
        SCALE = 1.0 / float(np.sqrt(CIN * K ** 2))
        EPS = 1e-08
        _BK = np.array([1.0, 3.0, 3.0, 1.0], dtype=np.float32)
        BLUR_K = _BK / _BK.sum()

        def _blur(x, kern, pad):
            B, C, _ = x.shape
            xp = jnp.pad(x, ((0, 0), (0, 0), (pad[0], pad[1])))
            w = jnp.broadcast_to(kern.astype(x.dtype)[None, None, :], (C, 1, kern.shape[0]))
            return lax.conv_general_dilated(xp, w, (1,), 'VALID', feature_group_count=C, dimension_numbers=('NCH', 'OIH', 'NCH'))

        def _conv_same(x, w):
            p = (K - 1) // 2
            return lax.conv_general_dilated(x[None], w, (1,), [(p, p)], dimension_numbers=('NCH', 'OIH', 'NCH'))[0]

        def _conv_down(x, w):
            return lax.conv_general_dilated(x[None], w, (2,), 'VALID', dimension_numbers=('NCH', 'OIH', 'NCH'))[0]

        def _conv_up(x, w_t):
            return lax.conv_transpose(x[None], w_t, (2,), 'VALID', dimension_numbers=('NCH', 'IOH', 'NCH'), transpose_kernel=True)[0]

        def _layer(x, style, w, b, mw, mb, typ):
            s = style @ mw.T + mb
            weight = SCALE * w * s[:, None, :, None]
            demod = lax.rsqrt(jnp.sum(weight * weight, axis=(2, 3)) + EPS)
            weight = weight * demod[:, :, None, None]
            blur_k = jnp.asarray(BLUR_K)
            if typ == 'same':
                out = jax.vmap(_conv_same)(x, weight) + b[None, :, None]
            elif typ == 'upsample':
                out = jax.vmap(_conv_up)(x, weight.transpose(0, 2, 1, 3)) + b[None, :, None]
                out = _blur(out, 2.0 * blur_k, (1, 1))
            elif typ == 'downsample':
                xb = _blur(x, blur_k, (2, 2))
                out = jax.vmap(_conv_down)(xb, weight) + b[None, :, None]
            else:
                raise NotImplementedError(typ)
            return out
        out = x
        for i, typ in enumerate(TYPES):
            out = _layer(out, style, weights[i], biases[i], mod_w[i], mod_b[i], typ)
        return out

    def _L3_ffn_ref(x, W_up, gate_w, expert_bias, lora_A, lora_B):
        import jax, jax.numpy as jnp
        import numpy as np
        NUM_EXPERTS = 4
        HIDDEN = 512
        RANK = 8
        ALPHA = 8.0
        SCALE = ALPHA / RANK
        B, T, H = x.shape
        E = gate_w.shape[0]
        x_flat = x.reshape(-1, H)
        logits = x_flat @ gate_w.T + expert_bias
        top1 = jnp.argmax(logits, axis=-1)
        one_hot = jax.nn.one_hot(top1, E, dtype=x_flat.dtype)
        base_out = jnp.einsum('bth,oh->bto', x, W_up)
        z = jnp.einsum('nh,erh->ner', x_flat, lora_A)
        d = jnp.einsum('ner,ehr->neh', z, lora_B) * SCALE
        delta = jnp.einsum('neh,ne->nh', d, one_hot)
        return base_out + delta.reshape(B, T, H)
    x = x + _L0_ffn_ref(_L0_cond_ref(x, cond_512, L0_cond_weights, L0_cond_biases, L0_cond_mod_w, L0_cond_mod_b), L0_ffn_W, L0_ffn_bias, L0_ffn_A, L0_ffn_Bf, L0_ffn_coeffs, L0_ffn_scales)
    x = x + _L1_ffn_ref(_L1_cond_ref(x, cond_512, L1_cond_weights, L1_cond_biases, L1_cond_mod_w, L1_cond_mod_b), L1_ffn_W_base, L1_ffn_b_base, L1_ffn_W_router, L1_ffn_lora_A, L1_ffn_lora_B)
    x = x + _L2_ffn_ref(_L2_cond_ref(x, cond_512, L2_cond_weights, L2_cond_biases, L2_cond_mod_w, L2_cond_mod_b), L2_ffn_gate, L2_ffn_kernel, L2_ffn_bias, L2_ffn_lora_A, L2_ffn_lora_B, L2_ffn_lora_A_shared, L2_ffn_lora_B_shared)
    x = x + _L3_ffn_ref(_L3_cond_ref(x, cond_512, L3_cond_weights, L3_cond_biases, L3_cond_mod_w, L3_cond_mod_b), L3_ffn_W_up, L3_ffn_gate_w, L3_ffn_expert_bias, L3_ffn_lora_A, L3_ffn_lora_B)
    return x

_drawn_inputs = setup_inputs


def setup_inputs(seed=0):
    import zlib

    import numpy as np

    out = dict(_drawn_inputs(seed))
    spreads = {'L0_ffn_scales': (0.5, 0.6), 'L2_ffn_bias': (0.0, 0.1), 'L3_ffn_expert_bias': (0.0, 0.8)}
    factors = {'L0_ffn_bias': 3.273,
     'L0_ffn_coeffs': 4.269,
     'L1_ffn_b_base': 3.973,
     'L3_ffn_gate_w': 4.651,
     'L3_ffn_lora_A': 3.909,
     'L3_ffn_lora_B': 3.929}
    for name, (base, spread) in spreads.items():
        noise = np.random.default_rng([zlib.crc32(name.encode()), seed]).standard_normal(out[name].shape)
        drawn = base * np.exp(spread * noise) if base else spread * noise
        out[name] = jnp.asarray(drawn.astype(out[name].dtype))
    for name, factor in factors.items():
        out[name] = (out[name] * factor).astype(out[name].dtype)
    return out
```

```python
from contextlib import ExitStack

import numpy as np
import concourse.bass as bass
from concourse import mybir

SAMPLES, CH, LEN = 128, 32, 512
LAYERS, CONVS, TAPS, STYLE = 4, 4, 3, 64
P = 128
PH = P // CH
Q = LEN // PH
TILE = PH
TILES = 4
GROUP = TILE * TILES
ITERS = SAMPLES // (2 * GROUP)
PAIR = 2 * GROUP
HALO = Q + 2
E1, R1 = 8, 16
N2, R2 = 16, 32
E3, R3 = 4, 8
SCALE = 1.0 / float(np.sqrt(CH * TAPS ** 2))
EPS = 1e-08
LORA1_SCALE = 2.0
LOWEST = -3.0e38

F32 = mybir.dt.float32
ALU = mybir.AluOpType
ACT = mybir.ActivationFunctionType
AX = mybir.AxisListType

HI_A = (0, 1, 2, 3)
HI_B = (5, 4, 7, 6)
LO = (0, 1, 2, 3)

BLOCKS = (
    [(0, LO, 0, o) for o in LO] + [(0, LO, -1, 0), (0, LO, 1, 3)]
    + [(1, LO, 0, o) for o in HI_A] + [(1, LO, 0, o) for o in HI_B]
    + [(1, LO, -1, 0), (1, LO, -1, 1)] + [(1, LO, 1, 7), (1, LO, 1, 6)]
    + [(2, HI_A, 0, o) for o in HI_A] + [(2, HI_B, 0, o) for o in HI_B]
    + [(2, HI_B, -1, 0), (2, HI_B, 0, 3), (2, HI_A, 0, 4), (2, HI_A, 1, 7)]
    + [(3, HI_A, 0, 0), (3, HI_A, 0, 1), (3, HI_A, 0, 2), (3, HI_A, 1, 3)]
    + [(3, HI_B, -1, 0), (3, HI_B, 0, 1), (3, HI_B, 0, 2), (3, HI_B, 0, 3)]
)
NB = len(BLOCKS)
FIRST_BLOCK = [next(i for i, b in enumerate(BLOCKS) if b[0] == k) for k in range(CONVS)] + [NB]
C0_MID, C0_LEFT, C0_RIGHT = 0, 4, 5
UP_A, UP_B, UP_LEFT, UP_RIGHT = 6, 10, 14, 16
C2_A, C2_B, C2_SIDES = 18, 22, 26
DN = 30

T_A, T_B, T_S, T_DA, T_DB = 0, 512, 896, 1024, 1152
T_COLS = 1280


def block_coefficients():
    blur = np.array([1.0, 3.0, 3.0, 1.0]) / 8.0
    out = np.zeros((PH, TAPS, NB), np.float32)
    for n, (conv, rows, shift, o) in enumerate(BLOCKS):
        for g, row in enumerate(rows):
            for t in range(TAPS):
                if conv == 0:
                    c = 1.0 if row + 4 * shift - o + 1 == t else 0.0
                elif conv == 1:
                    j = 2 * (row + 4 * shift) + t - o + 1
                    c = 2.0 * blur[j] if 0 <= j < 4 else 0.0
                elif conv == 2:
                    c = 1.0 if row + 8 * shift - o + 1 == t else 0.0
                else:
                    j = row + 8 * shift - 2 * o - t + 2
                    c = blur[j] if 0 <= j < 4 else 0.0
                out[g, t, n] = c
    return out


def setup_program(nc, ctx, io, keep, scratch):

    def sb(name, shape, dt=F32):
        return ctx.enter_context(nc.sbuf_tensor(name, shape, dt))

    def sem(name):
        return ctx.enter_context(nc.semaphore(name))

    LK = LAYERS * CONVS
    cw = sb("cw", [P, LAYERS, CONVS, TAPS, CH])
    coef = sb("coef", [P, TAPS, NB])
    tmp_dve = sb("tmp_dve", [P, LAYERS, 12, CH])
    tmp_pool = sb("tmp_pool", [P, LAYERS, 12, CH])
    cond_t = sb("cond_t", [STYLE, SAMPLES])
    mw = sb("mw", [STYLE, LK, P])
    mb = sb("mb", [P, LK])
    cb = sb("cb", [P, LK])
    wq = sb("wq", [CH, LK, TAPS, CH])
    wsq = sb("wsq", [CH, LK, CH])
    qrep = sb("qrep", [CH, LK, PH, CH])
    s_all = sb("s_all", [P, LAYERS, CONVS, SAMPLES])
    s_sq = sb("s_sq", [CH, LAYERS, CONVS, SAMPLES])
    var = sb("var", [P, LAYERS, CONVS, SAMPLES])
    root = sb("root", [P, LAYERS, CONVS, SAMPLES])
    demod = sb("demod", [P, LAYERS, CONVS, SAMPLES])
    tab = sb("tab_all", [P, ITERS, T_COLS])
    a0 = sb("a0", [P, 2, LEN])
    b0 = sb("b0", [P, 2, LEN])
    coeffs = sb("coeffs_rep", [P, 2])
    scales = sb("scales_rep", [P, 2])
    mix = sb("mix", [P, 2])
    a2 = sb("a2", [P, 4, LEN])
    b2 = sb("b2", [P, 4, LEN])
    gate_t = sb("gate_t", [P, 4, 8])
    delta = sb("delta", [P, R2])
    gmat = sb("gmat", [P, 4, 8, R2])
    a2eff = sb("a2eff", [P, 8, PH, R2])
    b2eff = sb("b2eff", [P, 2, LEN])

    ps = [ctx.enter_context(nc.psum_tensor(f"setup_ps{i}", [P, 512], F32)) for i in range(8)]

    loads = {}

    def load(eng, name, dst, src):
        loads[name] = sem(f"ld_{name}")
        eng.dma_start(dst, src).then_inc(loads[name], 16)

    for name in ("cond", "mw", "mb", "cb", "wq", "cw", "coef", "w0", "a0", "b0", "coeffs", "scales",
                 "a2", "b2", "gate", "delta"):
        loads[name] = sem(f"ld_{name}")
    s_kept = sem("s_kept")
    s_style = sem("s_style")
    s_mod = sem("s_mod")
    s_square = sem("s_square")
    s_q = sem("s_q")
    s_var = sem("s_var")
    s_v = sem("s_v")
    s_root = sem("s_root")
    s_dve = sem("s_dve")
    s_tab = sem("s_tab")
    s_pool = sem("s_pool")
    s_shared = sem("s_shared")
    s_mix = sem("s_mix")
    s_w0 = sem("s_w0")
    s_gm = sem("s_gm")
    s_a2 = sem("s_a2")
    s_a2e = sem("s_a2e")
    s_b2 = sem("s_b2")
    s_b2e = sem("s_b2e")
    s_scr = [sem(f"s_scr{i}") for i in range(4)]

    def blocks_of(eng, queue, k, tmp, done, base):
        lo, hi = FIRST_BLOCK[k], FIRST_BLOCK[k + 1]
        n = hi - lo
        out = keep["wc"][:, :, lo * CH:hi * CH].rearrange("p l (n c) -> p l n c", c=CH)
        part = tmp[:, :, 0:n]

        def tap(t):
            return cw[:, :, k, t].unsqueeze(2).broadcast_to((P, LAYERS, n, CH))

        def factor(t):
            return coef[:, t, lo:hi].unsqueeze(1).unsqueeze(3).broadcast_to((P, LAYERS, n, CH))

        if base:
            queue.wait_ge(done, base)
        eng.tensor_tensor(out, tap(0), factor(0), ALU.mult).then_inc(done, 1)
        for t in (1, 2):
            eng.tensor_tensor(part, tap(t), factor(t), ALU.mult).then_inc(done, 1)
            queue.wait_ge(done, base + 2 * t)
            eng.tensor_tensor(out, out, part, ALU.add).then_inc(done, 1)
            queue.wait_ge(done, base + 2 * t + 1)

    with nc.Block() as block:

        @block.sync
        def _(sp):
            for name, dst, src in (
                ("cond", cond_t[:], io["cond_t"]), ("mw", mw[:], io["mw"]), ("mb", mb[:], io["mb"]),
                ("wq", wq[:], io["wq"]), ("cb", cb[:], io["cb"]),
                ("coeffs", coeffs[:], io["coeffs"]), ("scales", scales[:], io["scales"]),
                ("b0", b0[:], io["b0"]), ("a0", a0[:], io["a0"]),
                ("w0", keep["w"][:, 0], io["w"][:, 0]),
                ("gate", gate_t[:], io["gate_t"]), ("delta", delta[:], io["delta"]),
                ("a2", a2[:], io["a2"]), ("b2", b2[:], io["b2"]),
            ):
                sp.dma_start(dst, src).then_inc(loads[name], 16)
            sp.wait_ge(s_tab, 1)
            sp.dma_start(scratch["tab"].rearrange("i p c -> p i c"), tab[:]).then_inc(s_scr[0], 16)
            sp.wait_ge(s_a2e, 4)
            sp.dma_start(scratch["a2"], a2eff[:]).then_inc(s_scr[1], 16)
            sp.wait_ge(s_b2e, 2)
            for h in range(2):
                sp.dma_start(scratch["b2"][4 * h:4 * h + 4].rearrange("b r n -> (b r) n"),
                             b2eff[:, h]).then_inc(s_scr[2 + h], 16)
            for h in range(4):
                sp.wait_ge(s_scr[h], 16)

        @block.scalar
        def _(act):
            act.dma_start(cw[:], io["cw"]).then_inc(loads["cw"], 16)
            act.dma_start(coef[:], io["coef"]).then_inc(loads["coef"], 16)
            n = 0
            for dst, src in (
                (keep["ident"][:], io["ident"]), (keep["iota"][:], io["iota"]),
                (keep["ob"][:], io["ob"]),
                (keep["w"][:, 1:4], io["w"][:, 1:4]),
                (keep["wr1"][:], io["wr1"]), (keep["a1"][:], io["a1"]), (keep["b1"][:], io["b1"]),
                (keep["wg3"][:], io["wg3"]), (keep["eb3"][:], io["eb3"]), (keep["cb3"][:], io["cb3"]),
                (keep["a3"][:], io["a3"]),
            ):
                act.dma_start(dst, src).then_inc(s_kept, 16)
                n += 1
            act.wait_ge(loads["mb"], 16)
            for l in range(LAYERS):
                act.wait_ge(s_style, l + 1)
                for k in range(CONVS):
                    lk = CONVS * l + k
                    nc.scalar.activation(s_all[:, l, k], ps[l][:, k * P:(k + 1) * P], ACT.Identity,
                                         bias=mb[:, lk:lk + 1]).then_inc(s_mod, 1)
                act.wait_ge(s_mod, CONVS * (l + 1))
                nc.scalar.activation(s_sq[:, l], s_all[0:CH, l], ACT.Square).then_inc(s_square, 1)
            for l in range(LAYERS):
                act.wait_ge(s_v, l + 1)
                nc.scalar.activation(root[:, l], var[:, l], ACT.Sqrt).then_inc(s_root, 1)
            act.wait_ge(s_kept, 16 * n)

        @block.gpsimd
        def _(pool):
            nc.gpsimd.memset(keep["b2"][:], 0.0).then_inc(s_pool, 1)
            nc.gpsimd.memset(keep["b3"][:], 0.0).then_inc(s_pool, 1)
            pool.wait_ge(s_pool, 2)
            for g in range(2):
                pool.dma_start(keep["b2"][R2:2 * R2, g], io["bs2"]).then_inc(s_shared, 16)
                pool.dma_start(keep["a2"][:, g, :, R2:2 * R2], io["as2"]).then_inc(s_shared, 16)
            pool.dma_start(keep["b3"][0:E3 * R3], io["b3"]).then_inc(s_shared, 16)
            pool.wait_ge(loads["cw"], 16)
            pool.wait_ge(loads["coef"], 16)
            blocks_of(nc.gpsimd, pool, 2, tmp_pool, s_pool, 2)
            blocks_of(nc.gpsimd, pool, 3, tmp_pool, s_pool, 2 + 5)
            pool.wait_ge(s_shared, 16 * 5)

        @block.vector
        def _(dve):
            v = nc.vector
            steps = 0

            def then(ins):
                nonlocal steps
                steps += 1
                ins.then_inc(s_dve, 1)
                dve.wait_ge(s_dve, steps)

            dve.wait_ge(loads["wq"], 16)
            then(v.tensor_tensor(wq[:], wq[:], wq[:], ALU.mult))
            then(v.tensor_tensor(wsq[:], wq[:, :, 0], wq[:, :, 1], ALU.add))
            then(v.tensor_tensor(wsq[:], wsq[:], wq[:, :, 2], ALU.add))
            for r in range(PH):
                v.tensor_copy(qrep[:, :, r], wsq[:]).then_inc(s_q, 1)
            dve.wait_ge(loads["cw"], 16)
            dve.wait_ge(loads["coef"], 16)
            blocks_of(v, dve, 0, tmp_dve, s_dve, steps)
            steps += 5
            blocks_of(v, dve, 1, tmp_dve, s_dve, steps)
            steps += 5
            dve.wait_ge(loads["coeffs"], 16)
            dve.wait_ge(loads["scales"], 16)
            dve.wait_ge(loads["b0"], 16)
            then(v.tensor_tensor(mix[:], coeffs[:], scales[:], ALU.mult))
            for kk in range(2):
                v.tensor_scalar(b0[:, kk], b0[:, kk], mix[:, kk:kk + 1], None, ALU.mult).then_inc(s_mix, 1)
            dve.wait_ge(loads["gate"], 16)
            dve.wait_ge(loads["delta"], 16)
            v.tensor_tensor(gmat[:], gate_t[:].unsqueeze(3).broadcast_to((P, 4, 8, R2)),
                            delta[:].unsqueeze(1).unsqueeze(1).broadcast_to((P, 4, 8, R2)),
                            ALU.mult).then_inc(s_gm, 1)
            for l in range(LAYERS):
                dve.wait_ge(s_var, l + 1)
                v.tensor_scalar(var[:, l], ps[4 + l % 2][:].rearrange("p (k b) -> p k b", k=CONVS),
                                SCALE * SCALE, EPS, ALU.mult, ALU.add).then_inc(s_v, 1)
            dve.wait_ge(loads["w0"], 16)
            for p in range(PH):
                dve.wait_ge(s_w0, p + 1)
                w0p = keep["w"][:, 0, p]
                then(v.tensor_tensor(w0p, ps[p][:], w0p, ALU.add))
            dve.wait_ge(s_root, LAYERS)
            then(v.reciprocal(demod[:], root[:]))
            then(v.tensor_tensor(root[:], demod[:], demod[:], ALU.mult))
            then(v.tensor_tensor(root[:], root[:], var[:], ALU.mult))
            then(v.tensor_scalar(root[:], root[:], -0.5, 1.5, ALU.mult, ALU.add))
            then(v.tensor_tensor(demod[:], demod[:], root[:], ALU.mult))
            dve.wait_ge(s_mod, LK)
            dve.wait_ge(loads["cb"], 16)

            def of(x, k):
                return x[:, :, k].rearrange("p l (i b) -> p i l b", i=ITERS)

            def table(at, k=None):
                n = CONVS if at == T_A else CONVS - 1
                if k is None:
                    return tab[:, :, at:at + LAYERS * PAIR].rearrange("p i (l b) -> p i l b", l=LAYERS)
                return tab[:, :, at:at + LAYERS * n * PAIR].rearrange(
                    "p i (l k b) -> p i l k b", l=LAYERS, k=n)[:, :, :, k]

            for k, left, right in ((0, demod, of(demod, 1)), (1, s_all, of(s_all, 2)), (2, demod, of(s_all, 3))):
                for i in range(ITERS):
                    v.tensor_tensor(table(T_A, k)[:, i], of(left, k)[:, i], right[:, i], ALU.mult)
            for i in range(ITERS):
                v.tensor_copy(table(T_A, 3)[:, i], of(demod, 3)[:, i])
                last = v.tensor_copy(table(T_S)[:, i], of(s_all, 0)[:, i])
            then(last)
            v.tensor_scalar(tab[:, :, T_A:T_B], tab[:, :, T_A:T_B], SCALE, None, ALU.mult)
            v.memset(tab[:, :, T_DA:T_COLS], 0.0)
            for l in range(LAYERS):
                for k, right in ((0, demod), (1, s_all), (2, s_all)):
                    bias = cb[:, CONVS * l + k:CONVS * l + k + 1]
                    last = v.tensor_scalar(table(T_B, k)[:, :, l], right[:, l, k + 1].rearrange("p (i b) -> p i b", i=ITERS),
                                    bias, 2.0 if k == 1 else 1.0, ALU.mult, ALU.mult)
            then(last)
            for i in range(ITERS):
                v.tensor_scalar(table(T_DA)[0:CH, i], table(T_B, 1)[0:CH, i], -0.125, None, ALU.mult)
                last = v.tensor_scalar(table(T_DB)[2 * CH:3 * CH, i], table(T_B, 1)[2 * CH:3 * CH, i], -0.125,
                                       None, ALU.mult)
            last.then_inc(s_tab, 1)
            for p in range(PH):
                dve.wait_ge(s_a2, p + 1)
                v.tensor_copy(a2eff[:, :, p], ps[p][:, 0:256].rearrange("p (b r) -> p b r", r=R2)).then_inc(s_a2e, 1)
            for h in range(2):
                dve.wait_ge(s_b2, h + 1)
                v.tensor_copy(b2eff[:, h], ps[6 + h][:]).then_inc(s_b2e, 1)

        @block.tensor
        def _(pe):
            pe.wait_ge(loads["cond"], 16)
            pe.wait_ge(loads["mw"], 16)
            for l in range(LAYERS):
                for k in range(CONVS):
                    last = pe.matmul(ps[l][:, k * P:(k + 1) * P], mw[:, CONVS * l + k], cond_t[:],
                                     start=True, stop=True)
                last.then_inc(s_style, 1)
            pe.wait_ge(s_q, PH)
            for l in range(LAYERS):
                pe.wait_ge(s_square, l + 1)
                if l >= 2:
                    pe.wait_ge(s_v, l - 1)
                for k in range(CONVS):
                    last = pe.matmul(ps[4 + l % 2][:, k * P:(k + 1) * P],
                                     qrep[:, CONVS * l + k].rearrange("c r o -> c (r o)"),
                                     s_sq[:, l, k], start=True, stop=True)
                last.then_inc(s_var, 1)
            pe.wait_ge(s_mix, 2)
            pe.wait_ge(loads["a0"], 16)
            for p in range(PH):
                for kk in range(2):
                    last = pe.matmul(ps[p][:], a0[:, kk, p * Q:(p + 1) * Q], b0[:, kk], start=(kk == 0), stop=(kk == 1))
                last.then_inc(s_w0, 1)
            pe.wait_ge(s_gm, 1)
            pe.wait_ge(loads["a2"], 16)
            pe.wait_ge(loads["b2"], 16)
            g2 = gmat[:].rearrange("p k b r -> p k (b r)")
            for h in range(2):
                for kk in range(4):
                    last = pe.matmul(ps[6 + h][:], g2[:, kk, h * P:(h + 1) * P], b2[:, kk], start=(kk == 0), stop=(kk == 3))
                last.then_inc(s_b2, 1)
            for p in range(PH):
                if p == 0:
                    pe.wait_ge(s_root, LAYERS)
                    pe.wait_ge(s_tab, 1)
                for kk in range(4):
                    last = pe.matmul(ps[p][:, 0:256], a2[:, kk, p * Q:(p + 1) * Q], g2[:, kk], start=(kk == 0), stop=(kk == 3))
                last.then_inc(s_a2, 1)


def main_program(nc, ctx, io, keep, scratch):
    def sb(name, shape, dt=F32):
        return ctx.enter_context(nc.sbuf_tensor(name, shape, dt))

    def sem(name):
        sems.append(ctx.enter_context(nc.semaphore(name)))
        return sems[-1]

    sems = []
    x = [sb(f"x{g}", [P, GROUP, Q]) for g in range(2)]
    tab = sb("tab", [P, T_COLS])
    y3 = [sb(f"y3_{u}", [P, TILE, Q]) for u in range(2)]
    y3t = sb("y3t", [P, PH, GROUP * CH])
    out_t = sb("out_t", [P, GROUP, PH, CH])
    h_sb = sb("h_sb", [P, GROUP * CH])
    hm1 = sb("hm1", [P, GROUP * CH])
    hm = {1: hm1, 2: sb("hm2", [P, GROUP * CH]), 3: sb("hm3", [P, GROUP * CH])}
    wexp = sb("wexp", [P, TILES, P])
    lg = sb("lg", [P, TILES, 8])
    r_a = sb("r_a", [P, TILES, 8])
    r_b = sb("r_b", [P, TILES, 8])
    oh = sb("oh", [P, TILES, 8])
    oh2 = sb("oh2", [P, TILES, 8])
    ex = sb("ex", [P, TILES, 8])
    m1 = sb("m1", [P, TILES])
    m2 = sb("m2", [P, TILES])
    ix = sb("ix", [P, TILES])
    den = sb("den", [P, TILES])
    xs = [sb(f"xs{g}", [P, GROUP, HALO]) for g in range(2)]
    y0 = [sb(f"y0_{u}", [P, TILE, HALO]) for u in range(2)]
    y1 = [sb(f"y1_{u}", [P, 2, TILE, HALO]) for u in range(2)]
    y2 = [sb(f"y2_{u}", [P, 2, TILE, HALO]) for u in range(2)]
    wc, w, ident = keep["wc"], keep["w"], keep["ident"]

    conv_ps = [[ctx.enter_context(nc.psum_tensor(f"conv{u}{h}", [P, TILE, Q], F32)) for h in range(2)]
               for u in range(2)]
    tr_ps = ctx.enter_context(nc.psum_tensor("tr_ps", [P, TILE, PH, CH], F32))
    back_ps = ctx.enter_context(nc.psum_tensor("back_ps", [P, TILE, Q], F32))
    lin_ps = [ctx.enter_context(nc.psum_tensor(f"lin{h}", [P, 512], F32)) for h in range(2)]
    logit_ps = back_ps[:].rearrange("p b q -> p (b q)")

    x_loaded = [[sem(f"x_loaded{g}{t}") for t in range(TILES)] for g in range(2)]
    tab_loaded = sem("tab_loaded")
    a2_loaded = sem("a2_loaded")
    b2_loaded = sem("b2_loaded")
    stored = sem("stored")
    xs_ready = sem("xs_ready")
    c0_done, up_done, c2_done, dn_done, tr_done = (sem(n) for n in ("c0_done", "up_done", "c2_done", "dn_done", "tr_done"))
    y0_ready, y1a_ready, y1b_ready, y2a_ready, y2b_ready, y3_ready, y3t_ready = (
        sem(n) for n in ("y0_ready", "y1a_ready", "y1b_ready", "y2a_ready", "y2b_ready", "y3_ready", "y3t_ready"))
    lin_done, out_ready, back_done, x_ready = (sem(n) for n in ("lin_done", "out_ready", "back_done", "x_ready"))
    logits_done, h_done, h_ready, exp_in, exp_done, gates_ready, wexp_ready, wt_done, hm_ready, rchain = (
        sem(n) for n in ("logits_done", "h_done", "h_ready", "exp_in", "exp_done", "gates_ready", "wexp_ready",
                         "wt_done", "hm_ready", "rchain"))

    PHASES = 2 * LAYERS

    def before(n, layers):
        return sum(1 for m in range(n) if m // 2 in layers)

    def loop_body(it):
        with nc.Block() as block:

            @block.sync
            def _(sp):
                sp.dma_start(tab[:], scratch["tab"][it]).then_inc(tab_loaded, 16)
                for g in range(2):
                    for t in range(TILES):
                        sp.dma_start(x[g][:, TILE * t:TILE * (t + 1)],
                                     io["x"][2 * it + g][:, TILE * t:TILE * (t + 1)]).then_inc(x_loaded[g][t], 16)
                for g in range(2):
                    sp.dma_start(keep["a2"][:, g, :, 0:R2], scratch["a2"][:, 2 * it + g]).then_inc(a2_loaded, 16)
                    sp.dma_start(keep["b2"][0:R2, g], scratch["b2"][2 * it + g]).then_inc(b2_loaded, 16)
                for g in range(2):
                    n = PHASES - 2 + g
                    for t in range(TILES):
                        sp.wait_ge(x_ready, TILES * n + t + 1)
                        sp.dma_start(io["out"][2 * it + g][:, TILE * t:TILE * (t + 1)],
                                     x[g][:, TILE * t:TILE * (t + 1)]).then_inc(stored, 16)
                sp.wait_ge(stored, 16 * 2 * TILES)
                sp.wait_ge(tab_loaded, 16)
                sp.wait_ge(a2_loaded, 32)
                sp.wait_ge(b2_loaded, 32)

            @block.gpsimd
            def _(pool):
                def scale_x(g, l, t):
                    lo = T_S + PAIR * l + GROUP * g + TILE * t
                    nc.gpsimd.tensor_tensor(
                        xs[g][:, TILE * t:TILE * (t + 1), 1:Q + 1], x[g][:, TILE * t:TILE * (t + 1)],
                        tab[:, lo:lo + TILE].unsqueeze(2).broadcast_to((P, TILE, Q)), ALU.mult).then_inc(xs_ready, 1)

                pool.wait_ge(tab_loaded, 16)
                for g in range(2):
                    for t in range(TILES):
                        pool.wait_ge(x_loaded[g][t], 16)
                        scale_x(g, 0, t)
                for n in range(PHASES):
                    l, g = n // 2, n % 2
                    if l in (1, 3):
                        e, r = (E1, R1) if l == 1 else (E3, R3)
                        pool.wait_ge(gates_ready, before(n, (1, 3)) + 1)
                        nc.gpsimd.tensor_copy(
                            wexp[:, :, 0:e * r].rearrange("p t (e r) -> p t e r", r=r),
                            oh[:, :, 0:e].unsqueeze(3).broadcast_to((P, TILES, e, r))).then_inc(wexp_ready, 1)
                    if l < LAYERS - 1:
                        for t in range(TILES):
                            pool.wait_ge(x_ready, TILES * n + t + 1)
                            scale_x(g, l + 1, t)

            @block.scalar
            def _(act):
                a = nc.scalar

                def factors(l, k, n, t, b):
                    col = PAIR * (CONVS * l + k) + GROUP * (n % 2) + TILE * t + b
                    bcol = PAIR * ((CONVS - 1) * l + k) + GROUP * (n % 2) + TILE * t + b
                    return tab[:, T_A + col:T_A + col + 1], tab[:, T_B + bcol:T_B + bcol + 1]

                def half(n, t, k, y, done, ready):
                    act.wait_ge(done, TILES * n + t + 1)
                    for b in range(TILE):
                        s, c = factors(n // 2, k, n, t, b)
                        ins = a.activation(y[t % 2][:, 0, b, 1:Q + 1], conv_ps[t % 2][0][:, b], ACT.Identity,
                                           bias=c, scale=s)
                    ins.then_inc(ready, 1)

                def turned(n, t):
                    act.wait_ge(tr_done, TILES * n + t + 1)
                    cols = y3t[:, :, P * t:P * (t + 1)].rearrange("q p (b c) -> q p b c", c=CH)
                    a.activation(cols, tr_ps[:].rearrange("q b p c -> q p b c"), ACT.Copy).then_inc(y3t_ready, 1)

                def adapter(n):
                    l = n // 2
                    if l in (1, 2, 3):
                        rows = (0, E1 * R1, 2 * R2, E3 * R3)[l]
                        act.wait_ge(h_done, before(n, (1, 2, 3)) + 1)
                        dst = hm[2] if l == 2 else h_sb
                        a.activation(dst[0:rows], lin_ps[0][0:rows], ACT.Copy).then_inc(h_ready, 1)
                    if l == 1:
                        act.wait_ge(exp_in, before(n, (1,)) + 1)
                        a.activation(ex[:], r_a[:], ACT.Exp).then_inc(exp_done, 1)

                def linear_out(n):
                    l = n // 2
                    for p in range(PH):
                        act.wait_ge(lin_done, PH * n + p + 1)
                        src = lin_ps[p % 2][:].rearrange("q (b c) -> q b c", c=CH)
                        if l < 3:
                            ins = a.activation(out_t[:, :, p], src, ACT.Identity,
                                               bias=keep["ob"][:, PH * l + p:PH * l + p + 1])
                        else:
                            ins = a.activation(out_t[:, :, p], src, ACT.Copy)
                        ins.then_inc(out_ready, 1)

                act.wait_ge(tab_loaded, 16)
                for n in range(PHASES + 1):
                    m = n - 1
                    if m >= 0:
                        turned(m, 2)
                        turned(m, 3)
                    if n < PHASES:
                        half(n, 0, 1, y1, up_done, y1a_ready)
                        half(n, 1, 1, y1, up_done, y1a_ready)
                    if m >= 0:
                        adapter(m)
                    if n < PHASES:
                        half(n, 0, 2, y2, c2_done, y2a_ready)
                        half(n, 1, 2, y2, c2_done, y2a_ready)
                    if m >= 0:
                        linear_out(m)
                    if n < PHASES:
                        turned(n, 0)
                        turned(n, 1)
                        half(n, 2, 1, y1, up_done, y1a_ready)
                        half(n, 3, 1, y1, up_done, y1a_ready)
                        half(n, 2, 2, y2, c2_done, y2a_ready)
                        half(n, 3, 2, y2, c2_done, y2a_ready)

            @block.vector
            def _(dve):
                v = nc.vector
                steps = 0

                def then(ins):
                    nonlocal steps
                    steps += 1
                    ins.then_inc(rchain, 1)
                    dve.wait_ge(rchain, steps)

                def evacuate(n, t, k, dst, src, done, ready):
                    l = n // 2
                    dve.wait_ge(done, TILES * n + t + 1)
                    for b in range(TILE):
                        col = PAIR * (CONVS * l + k) + GROUP * (n % 2) + TILE * t + b
                        bcol = PAIR * ((CONVS - 1) * l + k) + GROUP * (n % 2) + TILE * t + b
                        c = tab[:, T_B + bcol:T_B + bcol + 1] if k < 3 else keep["cb3"][:, l:l + 1]
                        ins = v.tensor_scalar(dst[:, b], src[:, b], tab[:, T_A + col:T_A + col + 1], c,
                                              ALU.mult, ALU.add)
                    ins.then_inc(ready, 1)

                def first(n, t):
                    evacuate(n, t, 0, y0[t % 2][:, :, 1:Q + 1], conv_ps[t % 2][0], c0_done, y0_ready)

                def up(n, t):
                    evacuate(n, t, 1, y1[t % 2][:, 1, :, 1:Q + 1], conv_ps[t % 2][1], up_done, y1b_ready)

                def third(n, t):
                    evacuate(n, t, 2, y2[t % 2][:, 1, :, 1:Q + 1], conv_ps[t % 2][1], c2_done, y2b_ready)

                def down(n, t):
                    evacuate(n, t, 3, y3[t % 2][:], conv_ps[t % 2][0], dn_done, y3_ready)

                def residual(n, t):
                    dve.wait_ge(back_done, TILES * n + t + 1)
                    xt = x[n % 2][:, TILE * t:TILE * (t + 1)]
                    v.tensor_tensor(xt, back_ps[:], xt, ALU.add).then_inc(x_ready, 1)

                def wide(small, e):
                    return small[:].unsqueeze(2).broadcast_to((P, TILES, e))

                def best(scores, e, mask, top):
                    iota = keep["iota"][:, 0:e].unsqueeze(1).broadcast_to((P, TILES, e))
                    then(v.tensor_reduce(top[:], scores, AX.X, ALU.max))
                    then(v.tensor_tensor(r_b[:, :, 0:e], scores, wide(top, e), ALU.is_equal))
                    then(v.tensor_tensor(r_b[:, :, 0:e], r_b[:, :, 0:e], iota, ALU.mult))
                    then(v.tensor_reduce(ix[:], r_b[:, :, 0:e], AX.X, ALU.min))
                    then(v.tensor_tensor(mask[:, :, 0:e], wide(ix, e), iota, ALU.is_equal))

                def route(n):
                    l = n // 2
                    if l not in (1, 3):
                        return
                    e = E1 if l == 1 else E3
                    dve.wait_ge(logits_done, before(n, (1, 3)) + 1)
                    src = logit_ps[:, 0:TILES * 8].rearrange("p (t e) -> p t e", e=8)[:, :, 0:e]
                    if before(n, (1, 3)):
                        dve.wait_ge(wexp_ready, before(n, (1, 3)))
                    if l == 3:
                        then(v.tensor_tensor(lg[:, :, 0:e], src,
                                             keep["eb3"][:].unsqueeze(1).broadcast_to((P, TILES, e)), ALU.add))
                        best(lg[:, :, 0:e], e, oh2, m1)
                        v.tensor_copy(oh[:, :, 0:e], oh2[:, :, 0:e]).then_inc(gates_ready, 1)
                        return
                    then(v.tensor_copy(lg[:], src))
                    best(lg[:], e, oh, m1)
                    v.tensor_tensor(r_a[:], lg[:], wide(m1, e), ALU.subtract).then_inc(exp_in, 1)
                    then(v.scalar_tensor_tensor(out=lg[:], in0=oh[:], scalar=LOWEST, in1=lg[:], op0=ALU.mult, op1=ALU.add))
                    best(lg[:], e, oh2, m2)
                    then(v.tensor_tensor(oh[:], oh[:], oh2[:], ALU.add))
                    dve.wait_ge(exp_done, before(n, (1,)) + 1)
                    then(v.tensor_tensor(oh[:], oh[:], ex[:], ALU.mult))
                    then(v.tensor_reduce(den[:], oh[:], AX.X, ALU.add))
                    then(v.reciprocal(den[:], den[:]))
                    then(v.tensor_tensor(oh[:], oh[:], wide(den, e), ALU.mult))
                    v.tensor_scalar(oh[:], oh[:], LORA1_SCALE, None, ALU.mult).then_inc(gates_ready, 1)

                def masked(n):
                    l = n // 2
                    if l not in (1, 3):
                        return
                    rows = E1 * R1 if l == 1 else E3 * R3
                    dve.wait_ge(wt_done, before(n, (1, 3)) + 1)
                    dve.wait_ge(h_ready, before(n, (1, 2, 3)) + 1)
                    v.tensor_tensor(hm[l][0:rows], lin_ps[1][0:rows], h_sb[0:rows], ALU.mult).then_inc(hm_ready, 1)

                dve.wait_ge(tab_loaded, 16)
                for n in range(PHASES + 1):
                    m = n - 1
                    if n < PHASES:
                        first(n, 0)
                        first(n, 1)
                        up(n, 0)
                        up(n, 1)
                    if m >= 0:
                        route(m)
                    if n < PHASES:
                        third(n, 0)
                        third(n, 1)
                    if m >= 0:
                        masked(m)
                    for t in range(TILES):
                        if n < PHASES:
                            (down if t < 2 else first)(n, t)
                        if m >= 0:
                            residual(m, t)
                    if n < PHASES:
                        up(n, 2)
                        up(n, 3)
                        third(n, 2)
                        third(n, 3)
                        down(n, 2)
                        down(n, 3)

            @block.tensor
            def _(pe):
                def mm(out, l, first_block, blocks, rhs, start, stop):
                    return pe.matmul(out, wc[:, l, first_block * CH:(first_block + blocks) * CH], rhs,
                                     start=start, stop=stop, skip_group_check=True)

                def conv0(n, t):
                    l, u, tau = n // 2, t % 2, TILES * n + t
                    pe.wait_ge(xs_ready, tau + 1)
                    if tau >= 2:
                        pe.wait_ge(y3_ready, tau - 1)
                    xt = xs[n % 2][:, TILE * t:TILE * (t + 1)]
                    ps = conv_ps[u][0]
                    mm(ps[:], l, C0_MID, 4, xt[:, :, 1:Q + 1], True, False)
                    mm(ps[0:CH], l, C0_LEFT, 1, xt[:, :, 0:Q], False, True)
                    mm(ps[3 * CH:P], l, C0_RIGHT, 1, xt[:, :, 2:Q + 2], False, True).then_inc(c0_done, 1)

                def conv_up(n, t):
                    l, u, tau = n // 2, t % 2, TILES * n + t
                    pe.wait_ge(y0_ready, tau + 1)
                    y = y0[u]
                    mm(conv_ps[u][0][:], l, UP_A, 4, y[:, :, 1:Q + 1], True, False)
                    mm(conv_ps[u][1][:], l, UP_B, 4, y[:, :, 1:Q + 1], True, False)
                    mm(conv_ps[u][0][0:2 * CH], l, UP_LEFT, 2, y[:, :, 0:Q], False, True)
                    mm(conv_ps[u][1][2 * CH:P], l, UP_RIGHT, 2, y[:, :, 2:Q + 2], False, True).then_inc(up_done, 1)

                def conv2(n, t):
                    l, u, tau = n // 2, t % 2, TILES * n + t
                    pe.wait_ge(y1a_ready, tau + 1)
                    pe.wait_ge(y1b_ready, tau + 1)
                    ya, yb = y1[u][:, 0], y1[u][:, 1]
                    pa, pb = conv_ps[u]
                    at = PAIR * l + GROUP * (n % 2) + TILE * t
                    mm(pa[:], l, C2_A, 4, ya[:, :, 1:Q + 1], True, False)
                    mm(pa[:, :, 0], l, C2_A, 4, tab[:, T_DA + at:T_DA + at + TILE], False, False)
                    mm(pb[:], l, C2_B, 4, yb[:, :, 1:Q + 1], True, False)
                    mm(pb[:, :, Q - 1], l, C2_B, 4, tab[:, T_DB + at:T_DB + at + TILE], False, False)
                    mm(pa[0:CH], l, C2_SIDES, 1, yb[:, :, 0:Q], False, True)
                    mm(pa[3 * CH:P], l, C2_SIDES + 1, 1, yb[:, :, 1:Q + 1], False, True)
                    mm(pb[CH:2 * CH], l, C2_SIDES + 2, 1, ya[:, :, 1:Q + 1], False, True)
                    mm(pb[2 * CH:3 * CH], l, C2_SIDES + 3, 1, ya[:, :, 2:Q + 2], False, True).then_inc(c2_done, 1)

                def conv_down(n, t):
                    l, u, tau = n // 2, t % 2, TILES * n + t
                    pe.wait_ge(y2a_ready, tau + 1)
                    pe.wait_ge(y2b_ready, tau + 1)
                    ya, yb = y2[u][:, 0], y2[u][:, 1]
                    ps = conv_ps[u][0]
                    for o in LO:
                        mm(ps[CH * o:CH * (o + 1)], l, DN + o, 1, ya[:, :, 1:Q + 1] if o < 3 else ya[:, :, 2:Q + 2], True, False)
                    for o in LO:
                        ins = mm(ps[CH * o:CH * (o + 1)], l, DN + 4 + o, 1, yb[:, :, 0:Q] if o == 0 else yb[:, :, 1:Q + 1], False, True)
                    ins.then_inc(dn_done, 1)

                def turn(n, t):
                    tau = TILES * n + t
                    pe.wait_ge(y3_ready, tau + 1)
                    if tau:
                        pe.wait_ge(y3t_ready, tau)
                    for b in range(TILE):
                        ins = pe.transpose(tr_ps[:, b].rearrange("q p c -> q (p c)"), y3[t % 2][:, b], ident[:])
                    ins.then_inc(tr_done, 1)

                def adapter(n):
                    l, g = n // 2, n % 2
                    if l == 0:
                        return
                    pe.wait_ge(y3t_ready, TILES * (n + 1))
                    if l in (1, 3):
                        e, wl = (E1, keep["wr1"]) if l == 1 else (E3, keep["wg3"])
                        pe.wait_ge(x_ready, TILES * n)
                        for t in range(TILES):
                            for p in range(PH):
                                ins = pe.matmul(logit_ps[:, 8 * t:8 * t + e], y3t[:, p, P * t:P * (t + 1)], wl[:, p],
                                                start=(p == 0), stop=(p == PH - 1))
                        ins.then_inc(logits_done, 1)
                    pe.wait_ge(out_ready, PH * n - 1)
                    if l == 2:
                        pe.wait_ge(a2_loaded, 32)
                    for p in range(PH):
                        a_l = (None, keep["a1"][:, p], keep["a2"][:, g, p], keep["a3"][:, p])[l]
                        rows = (0, E1 * R1, 2 * R2, E3 * R3)[l]
                        ins = pe.matmul(lin_ps[0][0:rows], a_l, y3t[:, p], start=(p == 0), stop=(p == PH - 1))
                    ins.then_inc(h_done, 1)

                def gates_turned(n):
                    l = n // 2
                    if l not in (1, 3):
                        return
                    rows = E1 * R1 if l == 1 else E3 * R3
                    pe.wait_ge(wexp_ready, before(n, (1, 3)) + 1)
                    pe.wait_ge(out_ready, PH * n)
                    for t in range(TILES):
                        ins = pe.transpose(lin_ps[1][0:rows, P * t:P * (t + 1)], wexp[:, t, 0:rows], ident[:])
                    ins.then_inc(wt_done, 1)

                def linear(n):
                    l, g = n // 2, n % 2
                    pe.wait_ge(y3t_ready, TILES * (n + 1))
                    if l:
                        pe.wait_ge(h_ready, before(n, (1, 2, 3)) + 1)
                    if l == 2:
                        pe.wait_ge(b2_loaded, 32)
                    b_l = (None, keep["b1"], keep["b2"][:, g], keep["b3"])[l]
                    for p in range(PH):
                        if PH * n + p >= 2:
                            pe.wait_ge(out_ready, PH * n + p - 1)
                        ps = lin_ps[p % 2]
                        for k in range(PH):
                            ins = pe.matmul(ps[:], w[:, l, k, p * Q:(p + 1) * Q], y3t[:, k], start=(k == 0), stop=(k == PH - 1 and l == 0))
                        if l:
                            if l in (1, 3) and p == 0:
                                pe.wait_ge(hm_ready, before(n, (1, 3)) + 1)
                            ins = pe.matmul(ps[:], b_l[:, p * Q:(p + 1) * Q], hm[l][:], start=False, stop=True)
                        ins.then_inc(lin_done, 1)

                def turn_back(n, t):
                    if t == 0:
                        pe.wait_ge(out_ready, PH * (n + 1))
                    if TILES * n + t:
                        pe.wait_ge(x_ready, TILES * n + t)
                    for b in range(TILE):
                        ins = pe.transpose(back_ps[:, b], out_t[:, TILE * t + b].rearrange("q p c -> q (p c)"), ident[:])
                    ins.then_inc(back_done, 1)

                pe.wait_ge(tab_loaded, 16)
                for n in range(PHASES + 1):
                    m = n - 1
                    for t in range(2):
                        if n < PHASES:
                            conv0(n, t)
                        if m >= 0:
                            turn(m, 2 + t)
                    if n < PHASES:
                        conv_up(n, 0)
                        conv_up(n, 1)
                    if m >= 0:
                        adapter(m)
                    if n < PHASES:
                        conv2(n, 0)
                        conv2(n, 1)
                    if m >= 0:
                        gates_turned(m)
                        linear(m)
                    for t in range(TILES):
                        if n < PHASES:
                            (conv_down if t < 2 else conv0)(n, t)
                            if t >= 2:
                                turn(n, t - 2)
                        if m >= 0:
                            turn_back(m, t)
                    if n < PHASES:
                        conv_up(n, 2)
                        conv_up(n, 3)
                        conv2(n, 2)
                        conv2(n, 3)
                        conv_down(n, 2)
                        conv_down(n, 3)

        nums = [s.num for s in sems]
        nc.gpsimd.sem_clear(range(min(nums), max(nums) + 1))
        nc.all_engine_barrier()

    with nc.Block() as block:

        @block.vector
        def _(dve):
            for g in range(2):
                for y in (xs[g], y0[g]):
                    nc.vector.memset(y[:, :, 0:HALO:HALO - 1], 0.0)
                for y in (y1[g], y2[g]):
                    nc.vector.memset(y[:, :, :, 0:HALO:HALO - 1], 0.0)
            nc.vector.memset(hm[2][:], 0.0)
            nc.vector.memset(hm[3][:], 0.0)

    with nc.Fori(0, ITERS) as it:
        loop_body(it)


def build(nc, io):
    with ExitStack() as ctx:
        def sb(name, shape, dt=F32):
            return ctx.enter_context(nc.sbuf_tensor(name, shape, dt))

        keep = {
            "wc": sb("wc", [P, LAYERS, NB * CH]),
            "w": sb("w_lin", [P, LAYERS, PH, LEN]),
            "ob": sb("ob", [P, 3 * PH]),
            "ident": sb("ident", [P, P]),
            "iota": sb("iota", [P, 8]),
            "wr1": sb("wr1", [P, PH, E1]),
            "a1": sb("a1", [P, PH, E1 * R1]),
            "b1": sb("b1", [P, LEN]),
            "a2": sb("a2_cur", [P, 2, PH, 2 * R2]),
            "b2": sb("b2_cur", [P, 2, LEN]),
            "wg3": sb("wg3", [P, PH, E3]),
            "eb3": sb("eb3", [P, E3]),
            "cb3": sb("cb3", [P, LAYERS]),
            "a3": sb("a3", [P, PH, E3 * R3]),
            "b3": sb("b3", [P, LEN]),
        }
        scratch = {
            "tab": nc.dram_tensor("tab_scratch", [ITERS, P, T_COLS], F32).ap(),
            "a2": nc.dram_tensor("a2_scratch", [P, 8, PH, R2], F32).ap(),
            "b2": nc.dram_tensor("b2_scratch", [8, R2, LEN], F32).ap(),
        }
        with ExitStack() as inner:
            setup_program(nc, inner, io, keep, scratch)
        with ExitStack() as inner:
            main_program(nc, inner, io, keep, scratch)


def host_layout(i):
    c = np.ascontiguousarray

    def cols(a):
        return c(a.reshape(a.shape[:-1] + (Q, PH)).swapaxes(-1, -2).reshape(a.shape))

    def rows(a):
        return c(a.reshape((Q, PH) + a.shape[1:]))

    def rep(a):
        return c(np.tile(a, (PH,) + (1,) * (a.ndim - 1)))

    def every(a):
        return c(np.tile(a[None], (P, 1)))

    cw_oikt = np.stack([i[f"L{l}_cond_weights"] for l in range(LAYERS)])
    cw_in = cw_oikt.transpose(3, 0, 1, 4, 2).copy()
    cw_in[:, :, 1] = cw_oikt[:, 1].transpose(1, 0, 3, 2)
    mod_w = np.stack([i[f"L{l}_cond_mod_w"] for l in range(LAYERS)])
    mod_b = np.stack([i[f"L{l}_cond_mod_b"] for l in range(LAYERS)])
    bias = np.stack([i[f"L{l}_cond_biases"] for l in range(LAYERS)])
    lk = LAYERS * CONVS
    w_do = [i["L0_ffn_W"].T, i["L1_ffn_W_base"].T, i["L2_ffn_kernel"], i["L3_ffn_W_up"].T]
    w = np.stack([rows(cols(c(m))) for m in w_do], axis=1)
    ob = np.stack([rows(i[k]) for k in ("L0_ffn_bias", "L1_ffn_b_base", "L2_ffn_bias")], axis=1)
    a0 = cols(i["L0_ffn_A"].reshape(256, LEN)).reshape(2, P, LEN).transpose(1, 0, 2)
    b0 = cols(c(i["L0_ffn_Bf"].transpose(0, 2, 1)).reshape(256, LEN)).reshape(2, P, LEN).transpose(1, 0, 2)
    a2 = cols(i["L2_ffn_lora_A"].reshape(512, LEN)).reshape(4, P, LEN).transpose(1, 0, 2)
    b2 = cols(c(i["L2_ffn_lora_B"].transpose(0, 2, 1)).reshape(512, LEN)).reshape(4, P, LEN).transpose(1, 0, 2)
    x = i["x"].reshape(2 * ITERS, GROUP, CH, Q, PH).transpose(0, 4, 2, 1, 3).reshape(2 * ITERS, P, GROUP, Q)
    return {k: c(a) for k, a in {
        "x": x,
        "cond_t": i["cond_512"].T,
        "mw": np.tile(mod_w.transpose(3, 0, 1, 2).reshape(STYLE, lk, CH), (1, 1, PH)),
        "mb": rep(mod_b.transpose(2, 0, 1).reshape(CH, lk)),
        "cb": rep(bias.transpose(2, 0, 1).reshape(CH, lk)),
        "cb3": rep(bias[:, 3].T),
        "wq": cw_oikt.transpose(3, 0, 1, 4, 2).reshape(CH, lk, TAPS, CH),
        "cw": rep(cw_in),
        "coef": np.repeat(block_coefficients(), CH, axis=0),
        "w": w, "ob": ob.reshape(P, 3 * PH),
        "a0": a0, "b0": b0,
        "coeffs": np.repeat(i["L0_ffn_coeffs"], 16).reshape(2, P).T,
        "scales": np.repeat(i["L0_ffn_scales"], 16).reshape(2, P).T,
        "ident": np.eye(P, dtype=np.float32),
        "iota": np.tile(np.arange(8, dtype=np.float32) - 8.0, (P, 1)),
        "wr1": rows(i["L1_ffn_W_router"].T),
        "a1": rows(i["L1_ffn_lora_A"].reshape(E1 * R1, LEN).T),
        "b1": cols(c(i["L1_ffn_lora_B"].transpose(0, 2, 1)).reshape(E1 * R1, LEN)),
        "a2": a2, "b2": b2,
        "gate_t": np.repeat(i["L2_ffn_gate"].T, R2, axis=0).reshape(4, P, 8).transpose(1, 0, 2),
        "delta": np.tile(np.eye(R2, dtype=np.float32), (PH, 1)),
        "as2": rows(i["L2_ffn_lora_A_shared"].T),
        "bs2": cols(c(i["L2_ffn_lora_B_shared"].T)),
        "wg3": rows(i["L3_ffn_gate_w"].T),
        "eb3": every(i["L3_ffn_expert_bias"]),
        "a3": rows(i["L3_ffn_lora_A"].reshape(E3 * R3, LEN).T),
        "b3": cols(c(i["L3_ffn_lora_B"].transpose(0, 2, 1)).reshape(E3 * R3, LEN)),
    }.items()}


def kernel(**inputs):
    import concourse.bacc as bacc
    from concourse.bass_utils import run_bass_kernel_spmd

    arrays = host_layout({k: np.asarray(v) for k, v in inputs.items()})
    nc = bacc.Bacc("TRN2", target_bir_lowering=False, num_devices=1)
    io = {k: nc.dram_tensor(f"in_{k}", a.shape, mybir.dt.from_np(a.dtype), kind="ExternalInput").ap()
          for k, a in arrays.items()}
    io["out"] = nc.dram_tensor("out_x", arrays["x"].shape, F32, kind="ExternalOutput").ap()
    build(nc, io)
    r = run_bass_kernel_spmd(nc, [{f"in_{k}": a for k, a in arrays.items()}], core_ids=[0])
    y = r.results[0]["out_x"].reshape(2 * ITERS, PH, CH, GROUP, Q)
    return np.ascontiguousarray(y.transpose(0, 3, 2, 4, 1)).reshape(SAMPLES, CH, LEN)
```

```python
from contextlib import ExitStack

import numpy as np
import concourse.bass as bass
from concourse import mybir

SAMPLES, CH, LEN = 128, 32, 512
LAYERS, CONVS, TAPS, STYLE = 4, 4, 3, 64
P = 128
PH = P // CH
Q = LEN // PH
TILE = PH
TILES = 4
GROUP = TILE * TILES
ITERS = SAMPLES // (2 * GROUP)
PAIR = 2 * GROUP
HALO = Q + 2
E1, R1 = 8, 16
N2, R2 = 16, 32
E3, R3 = 4, 8
SCALE = 1.0 / float(np.sqrt(CH * TAPS ** 2))
EPS = 1e-08
Z1 = E1 * R1 + E1
Z23 = 2 * R2
LORA1_SCALE = 2.0
LOWEST = -3.0e38

F32 = mybir.dt.float32
F32R = mybir.dt.float32r
PASSES = ((0, 0), (0, 1), (1, 0))
ALU = mybir.AluOpType
ACT = mybir.ActivationFunctionType
AX = mybir.AxisListType

HI_A = (0, 1, 2, 3)
HI_B = (5, 4, 7, 6)
LO = (0, 1, 2, 3)

LO_ODD = (1, 0, 3, 2)

PLACED = (
    [(0, LO, 0, o) for o in LO] + [(0, LO, -1, 0), (0, LO, 1, 3)] + [(0, LO, 0, o) for o in LO_ODD]
    + [(2, HI_A, 0, o) for o in HI_A] + [(2, HI_B, 0, o) for o in HI_B]
    + [(2, HI_B, -1, 0), (2, HI_B, 0, 3), (2, HI_A, 0, 4), (2, HI_A, 1, 7)]
)
MIXED = (
    [(1, LO, 0, o) for o in HI_A] + [(1, LO, 0, o) for o in HI_B]
    + [(1, LO, -1, 0), (1, LO, -1, 1)] + [(1, LO, 1, 7), (1, LO, 1, 6)]
    + [(3, HI_A, 0, 0), (3, HI_A, 0, 1), (3, HI_A, 0, 2), (3, HI_A, 1, 3)]
    + [(3, HI_B, -1, 0), (3, HI_B, 0, 1), (3, HI_B, 0, 2), (3, HI_B, 0, 3)]
)
NP, NM = len(PLACED), len(MIXED)
C0_MID, C0_LEFT, C0_RIGHT = (0, 6), 4, 5
C2_A, C2_B, C2_SIDES = 10, 14, 18
NUP = sum(1 for b in MIXED if b[0] == 1)
UP_A, UP_B, UP_LEFT, UP_RIGHT = 0, 4, 8, 10
DN = NUP
UP_ODD = NM

T_A, T_B, T_S, T_D = 0, CONVS, 2 * CONVS - 1, 2 * CONVS
KINDS = T_D + 1


def table_column(layer, kind, sample):
    return PAIR * (KINDS * layer + kind) + sample



def block_coefficients(blocks):
    blur = np.array([1.0, 3.0, 3.0, 1.0]) / 8.0
    out = np.zeros((PH, TAPS, len(blocks)), np.float32)
    for n, (conv, rows, shift, o) in enumerate(blocks):
        for g, row in enumerate(rows):
            for t in range(TAPS):
                if conv == 0:
                    c = 1.0 if row + 4 * shift - o + 1 == t else 0.0
                elif conv == 1:
                    j = 2 * (row + 4 * shift) + t - o + 1
                    c = 2.0 * blur[j] if 0 <= j < 4 else 0.0
                elif conv == 2:
                    c = 1.0 if row + 8 * shift - o + 1 == t else 0.0
                else:
                    j = row + 8 * shift - 2 * o - t + 2
                    c = blur[j] if 0 <= j < 4 else 0.0
                out[g, t, n] = c
    return out


def blocks_of(nc, eng, queue, keep, cw, coef, conv, lo, hi, tmp, done, base):
    n = hi - lo
    out = keep["wm"][:, :, lo * CH:hi * CH].rearrange("p l (n c) -> p l n c", c=CH)
    part = tmp[:, :, 0:n]

    def tap(t):
        return cw[:, :, conv, t].unsqueeze(2).broadcast_to((P, LAYERS, n, CH))

    def factor(t):
        return coef[:, t, lo:hi].unsqueeze(1).unsqueeze(3).broadcast_to((P, LAYERS, n, CH))

    eng.tensor_tensor(out, tap(0), factor(0), ALU.mult).then_inc(done, 1)
    for t in (1, 2):
        eng.tensor_tensor(part, tap(t), factor(t), ALU.mult).then_inc(done, 1)
        queue.wait_ge(done, base + 2 * t)
        eng.tensor_tensor(out, out, part, ALU.add).then_inc(done, 1)
        queue.wait_ge(done, base + 2 * t + 1)


def setup_program(nc, ctx, io, keep, scratch):

    def sb(name, shape, dt=F32):
        return ctx.enter_context(nc.sbuf_tensor(name, shape, dt))

    def sem(name):
        return ctx.enter_context(nc.semaphore(name))

    cond_t = sb("cond_t", [STYLE, SAMPLES])
    mod_w = sb("mod_w", [STYLE, CONVS, P])
    mod_b = sb("mod_b", [P, CONVS])
    conv_b = sb("conv_b", [P, CONVS])
    wq = sb("wq", [P, CONVS, TAPS, P])
    mod, mod_sq, var, demod = (sb(n, [P, CONVS, SAMPLES]) for n in ("mod", "mod_sq", "var", "demod"))
    root = mod_sq
    table = sb("table", [P, ITERS, KINDS, PAIR])
    raw = [sb(f"w_raw{i}", [P, PH, LEN]) for i in range(3)]
    a2, b2 = raw[1], raw[2]
    a0 = sb("a0", [P, 2, LEN])
    b0 = sb("b0", [P, 2, LEN])
    coeffs = sb("coeffs_rep", [P, 2])
    scales = sb("scales_rep", [P, 2])
    mix = sb("mix", [P, 2])
    cw = sb("cw", [P, LAYERS, 2, TAPS, CH])
    coef = sb("coef", [P, TAPS, NM])
    tmp_dve = sb("tmp_dve", [P, LAYERS, NUP, CH])
    tmp_pool = sb("tmp_pool", [P, LAYERS, NM - NUP, CH])
    a1 = sb("a1_raw", [P, PH, Z1])
    b1 = sb("b1_raw", [P, LEN])
    a3 = sb("a3_raw", [P, PH, Z23])
    b3 = sb("b3_raw", [P, LEN])
    as2 = sb("as2_raw", [P, PH, R2])
    bs2 = sb("bs2_raw", [2 * R2, LEN])
    gate_t = sb("gate_t", [P, 4, 8])
    delta = sb("delta", [P, R2])
    gmat = sb("gmat", [P, 4, 8, R2])
    a2eff = [a0[:].rearrange("p k n -> p (k n)").rearrange("p (b i r) -> p b i r", i=PH, r=R2).bitcast(F32R),
             sb("a2eff_lo", [P, 8, PH, R2], F32R)[:]]
    b2eff = [b0[:].bitcast(F32R), sb("b2eff_lo", [P, 2, LEN], F32R)[:]]
    ps = [ctx.enter_context(nc.psum_tensor(f"w_ps{i}", [P, 512], F32)) for i in range(6)]
    mod_ps = ctx.enter_context(nc.psum_tensor("mod_ps", [P, CONVS, SAMPLES], F32))
    var_ps = ctx.enter_context(nc.psum_tensor("var_ps", [P, CONVS, SAMPLES], F32))

    names = ("cond_t", "mod_w", "mod_b", "conv_b", "wq", "coeffs", "scales", "b0", "a0", "w0", "w1", "w2", "w3",
             "gate", "delta", "a2", "b2", "cw", "coef", "a1", "b1", "a3", "b3", "as2", "bs2")
    loaded = {n: sem(f"ld_{n}") for n in names}
    kept = sem("kept")
    mod_done, mod_ready, square_ready, wq_ready, var_done, var_ready, root_ready, chain, table_ready = (
        sem(n) for n in ("mod_done", "mod_ready", "square_ready", "wq_ready", "var_done", "var_ready",
                         "root_ready", "chain", "table_ready"))
    table_out = sem("table_out")
    zeroed = sem("zeroed")
    b3_zero = sem("b3_zero")
    mix_done = sem("mix_done")
    b0_ready = sem("b0_ready")
    w0_done = sem("w0_done")
    w0_ready = sem("w0_ready")
    gm_ready = sem("gm_ready")
    a2_done = sem("a2_done")
    b2_done = sem("b2_done")
    a2_hi, a2_lo, b2_hi, b2_lo = (sem(n) for n in ("a2_hi", "a2_lo", "b2_hi", "b2_lo"))
    w_hi, w_lo = sem("w_hi"), sem("w_lo")
    small_hi, small_lo = sem("small_hi"), sem("small_lo")
    blocks_dve, blocks_pool = sem("blocks_dve"), sem("blocks_pool")
    scratch_out = [sem(f"scratch_out{i}") for i in range(6)]

    S = slice(R2, 2 * R2)
    small = [
        ("a1", a1[:], [(keep["a1"][i][:]) for i in range(2)]),
        ("b1", b1[:], [(keep["b1"][i][:]) for i in range(2)]),
        ("a3", a3[:], [(keep["a3"][i][:]) for i in range(2)]),
        ("b3", b3[:], [(keep["b3"][i][:]) for i in range(2)]),
        ("as2", as2[:], [(keep["a2"][i][:, 0, :, S]) for i in range(2)]),
        ("as2", as2[:], [(keep["a2"][i][:, 1, :, S]) for i in range(2)]),
        ("bs2", bs2[S], [(keep["b2"][i][S, 0]) for i in range(2)]),
        ("bs2", bs2[S], [(keep["b2"][i][S, 1]) for i in range(2)]),
    ]

    with nc.Block() as block:

        @block.sync
        def _(sp):
            for name, dst, src in (
                ("cond_t", cond_t[:], io["cond_t"]), ("mod_w", mod_w[:], io["mod_w"]),
                ("cw", cw[:], io["cw"]), ("wq", wq[:], io["wq"]),
                ("coeffs", coeffs[:], io["coeffs"]), ("scales", scales[:], io["scales"]),
                ("b0", b0[:], io["b0"]), ("a0", a0[:], io["a0"]),
                ("w0", raw[0][:], io["w"][:, 0]), ("a2", a2[:], io["a2"]), ("b2", b2[:], io["b2"]),
            ):
                sp.dma_start(dst, src).then_inc(loaded[name], 16)
            sp.wait_ge(table_ready, 1)
            for l in range(LAYERS):
                sp.dma_start(scratch["tab"][:, :, l].rearrange("i c k b -> c i k b"),
                             table[CH * l:CH * (l + 1)]).then_inc(table_out, 16)
            for l in (1, 2, 3):
                if l == 1:
                    sp.wait_ge(w_lo, 1)
                elif l == 2:
                    sp.wait_ge(a2_done, PH)
                    sp.wait_ge(b2_done, 2)
                sp.dma_start(raw[l - 1][:], io["w"][:, l]).then_inc(loaded[f"w{l}"], 16)
            for i, done in ((0, a2_hi), (1, a2_lo)):
                sp.wait_ge(done, PH)
                sp.dma_start(scratch["a2"][i], a2eff[i].bitcast(F32)).then_inc(scratch_out[i], 16)
            for i, done in ((0, b2_hi), (1, b2_lo)):
                sp.wait_ge(done, 2)
                for h in range(2):
                    sp.dma_start(scratch["b2"][i, 4 * h:4 * h + 4].rearrange("b r n -> (b r) n"),
                                 b2eff[i][:, h].bitcast(F32)).then_inc(scratch_out[2 + 2 * i + h], 16)
            for s in scratch_out:
                sp.wait_ge(s, 16)
            sp.wait_ge(table_out, 16 * LAYERS)

        @block.scalar
        def _(act):
            a = nc.scalar
            for name, dst, src in (
                ("coef", coef[:], io["coef"]), ("mod_b", mod_b[:], io["mod_b"]), ("conv_b", conv_b[:], io["conv_b"]),
                ("gate", gate_t[:], io["gate_t"]), ("delta", delta[:], io["delta"]),
                ("a1", a1[:], io["a1"]), ("b1", b1[:], io["b1"]), ("a3", a3[:], io["a3"]),
                ("as2", as2[:], io["as2"]), ("bs2", bs2[S], io["bs2"]),
            ):
                act.dma_start(dst, src).then_inc(loaded[name], 16)
            act.wait_ge(b3_zero, 1)
            act.dma_start(b3[0:E3 * R3], io["b3"]).then_inc(loaded["b3"], 16)
            n = 0
            for dst, src in (
                (keep["wp"][:], io["wp"]), (keep["ident"][:], io["ident"]), (keep["iota"][:], io["iota"]),
                (keep["ob"][:], io["ob"]), (keep["eb3"][:], io["eb3"]), (keep["cb3"][:], io["cb3"]),
            ):
                act.dma_start(dst, src).then_inc(kept, 16)
                n += 1
            act.wait_ge(loaded["mod_b"], 16)
            act.wait_ge(mod_done, 1)
            for k in range(CONVS):
                a.activation(mod[:, k], mod_ps[:, k], ACT.Identity, bias=mod_b[:, k:k + 1]).then_inc(mod_ready, 1)
            act.wait_ge(mod_ready, CONVS)
            a.activation(mod_sq[:], mod[:], ACT.Square).then_inc(square_ready, 1)
            act.wait_ge(var_ready, 1)
            a.activation(root[:], var[:], ACT.Sqrt).then_inc(root_ready, 1)

            def layer_hi(l):
                act.wait_ge(loaded[f"w{l}"], 16)
                if l == 0:
                    act.wait_ge(w0_ready, PH)
                a.activation(keep["w"][0][:, l], raw[max(l - 1, 0)][:], ACT.Copy).then_inc(w_hi, 1)

            layer_hi(0)
            for p in range(PH):
                act.wait_ge(a2_done, p + 1)
                a.activation(a2eff[0][:, :, p], ps[p][:, 0:256].rearrange("p (b r) -> p b r", r=R2),
                             ACT.Copy).then_inc(a2_hi, 1)
            for h in range(2):
                act.wait_ge(b2_done, h + 1)
                a.activation(b2eff[0][:, h], ps[4 + h][:], ACT.Copy).then_inc(b2_hi, 1)
            for l in (1, 2, 3):
                layer_hi(l)
            act.wait_ge(zeroed, 2)
            for name, v, pair in small:
                act.wait_ge(loaded[name], 16)
                a.activation(pair[0], v, ACT.Copy).then_inc(small_hi, 1)
            act.wait_ge(blocks_dve, 5)
            for g, row in enumerate(LO_ODD):
                a.activation(keep["wm"][CH * g:CH * (g + 1), :, UP_ODD * CH:(UP_ODD + NUP) * CH],
                             keep["wm"][CH * row:CH * (row + 1), :, 0:NUP * CH], ACT.Copy)
            act.wait_ge(kept, 16 * n)

        @block.gpsimd
        def _(pool):
            nc.gpsimd.memset(b3[:], 0.0).then_inc(b3_zero, 1)
            for i in range(2):
                nc.gpsimd.memset(keep["b2"][i][:].bitcast(F32), 0.0).then_inc(zeroed, 1)
            pool.wait_ge(loaded["cw"], 16)
            pool.wait_ge(loaded["coef"], 16)
            blocks_of(nc, nc.gpsimd, pool, keep, cw, coef, 1, NUP, NM, tmp_pool, blocks_pool, 0)
            for l in range(LAYERS):
                pool.wait_ge(w_hi, l + 1)
                nc.gpsimd.tensor_tensor(keep["w"][1][:, l], raw[max(l - 1, 0)][:],
                                        keep["w"][0][:, l].bitcast(F32), ALU.subtract).then_inc(w_lo, 1)

        @block.vector
        def _(dve):
            v = nc.vector
            steps = 0

            def then(ins):
                nonlocal steps
                steps += 1
                ins.then_inc(chain, 1)
                dve.wait_ge(chain, steps)

            dve.wait_ge(loaded["wq"], 16)
            then(v.tensor_tensor(wq[:], wq[:], wq[:], ALU.mult))
            then(v.tensor_tensor(wq[:, :, 0], wq[:, :, 0], wq[:, :, 1], ALU.add))
            v.tensor_tensor(wq[:, :, 0], wq[:, :, 0], wq[:, :, 2], ALU.add).then_inc(wq_ready, 1)
            dve.wait_ge(loaded["coeffs"], 16)
            dve.wait_ge(loaded["scales"], 16)
            dve.wait_ge(loaded["b0"], 16)
            v.tensor_tensor(mix[:], coeffs[:], scales[:], ALU.mult).then_inc(mix_done, 1)
            dve.wait_ge(mix_done, 1)
            for kk in range(2):
                v.tensor_scalar(b0[:, kk], b0[:, kk], mix[:, kk:kk + 1], None, ALU.mult).then_inc(b0_ready, 1)
            dve.wait_ge(var_done, 1)
            v.tensor_scalar(var[:], var_ps[:], SCALE * SCALE, EPS, ALU.mult, ALU.add).then_inc(var_ready, 1)
            dve.wait_ge(loaded["gate"], 16)
            dve.wait_ge(loaded["delta"], 16)
            v.tensor_tensor(gmat[:], gate_t[:].unsqueeze(3).broadcast_to((P, 4, 8, R2)),
                            delta[:].unsqueeze(1).unsqueeze(1).broadcast_to((P, 4, 8, R2)),
                            ALU.mult).then_inc(gm_ready, 1)
            dve.wait_ge(root_ready, 1)
            then(v.reciprocal(demod[:], root[:]))
            then(v.tensor_tensor(root[:], demod[:], demod[:], ALU.mult))
            then(v.tensor_tensor(root[:], root[:], var[:], ALU.mult))
            then(v.tensor_scalar(root[:], root[:], -0.5, 1.5, ALU.mult, ALU.add))
            then(v.tensor_tensor(demod[:], demod[:], root[:], ALU.mult))
            dve.wait_ge(mod_ready, CONVS)

            def of(x, k):
                return x[:, k].rearrange("p (i b) -> p i b", i=ITERS)

            for k, left, right in ((0, demod, demod), (1, mod, mod), (2, demod, mod)):
                v.scalar_tensor_tensor(out=table[:, :, T_A + k], in0=of(left, k), scalar=SCALE, in1=of(right, k + 1),
                                       op0=ALU.mult, op1=ALU.mult)
            v.tensor_scalar(table[:, :, T_A + 3], of(demod, 3), SCALE, None, ALU.mult)
            dve.wait_ge(loaded["conv_b"], 16)
            for kind, k, right, c in ((T_B, 0, demod, 1.0), (T_B + 1, 1, mod, 2.0), (T_B + 2, 2, mod, 1.0),
                                      (T_D, 1, mod, -0.25)):
                v.tensor_scalar(table[:, :, kind], of(right, k + 1), conv_b[:, k:k + 1], c, ALU.mult, ALU.mult)
            v.tensor_copy(table[:, :, T_S], of(mod, 0)).then_inc(table_ready, 1)
            dve.wait_ge(loaded["w0"], 16)
            for p in range(PH):
                dve.wait_ge(w0_done, p + 1)
                v.tensor_tensor(raw[0][:, p], ps[p][:], raw[0][:, p], ALU.add).then_inc(w0_ready, 1)
            dve.wait_ge(loaded["cw"], 16)
            dve.wait_ge(loaded["coef"], 16)
            blocks_of(nc, v, dve, keep, cw, coef, 0, 0, NUP, tmp_dve, blocks_dve, 0)
            for p in range(PH):
                dve.wait_ge(a2_hi, p + 1)
                v.tensor_tensor(a2eff[1][:, :, p], ps[p][:, 0:256].rearrange("p (b r) -> p b r", r=R2),
                                a2eff[0][:, :, p].bitcast(F32), ALU.subtract).then_inc(a2_lo, 1)
            for h in range(2):
                dve.wait_ge(b2_hi, h + 1)
                v.tensor_tensor(b2eff[1][:, h], ps[4 + h][:], b2eff[0][:, h].bitcast(F32),
                                ALU.subtract).then_inc(b2_lo, 1)
            for k, (name, x, pair) in enumerate(small):
                dve.wait_ge(small_hi, k + 1)
                v.tensor_tensor(pair[1], x, pair[0].bitcast(F32), ALU.subtract).then_inc(small_lo, 1)

        @block.tensor
        def _(pe):
            pe.wait_ge(loaded["cond_t"], 16)
            pe.wait_ge(loaded["mod_w"], 16)
            for k in range(CONVS):
                last = pe.matmul(mod_ps[:, k], mod_w[:, k], cond_t[:], start=True, stop=True)
            last.then_inc(mod_done, 1)
            pe.wait_ge(wq_ready, 1)
            pe.wait_ge(square_ready, 1)
            for k in range(CONVS):
                last = pe.matmul(var_ps[:, k], wq[:, k, 0], mod_sq[:, k], start=True, stop=True)
            last.then_inc(var_done, 1)
            pe.wait_ge(b0_ready, 2)
            pe.wait_ge(loaded["a0"], 16)
            for p in range(PH):
                for kk in range(2):
                    last = pe.matmul(ps[p][:], a0[:, kk, p * Q:(p + 1) * Q], b0[:, kk], start=(kk == 0), stop=(kk == 1))
                last.then_inc(w0_done, 1)
            pe.wait_ge(gm_ready, 1)
            pe.wait_ge(loaded["a2"], 16)
            pe.wait_ge(loaded["b2"], 16)
            g2 = gmat[:].rearrange("p k b r -> p k (b r)")
            for h in range(2):
                for kk in range(4):
                    last = pe.matmul(ps[4 + h][:], g2[:, kk, h * P:(h + 1) * P], b2[:, kk], start=(kk == 0), stop=(kk == 3))
                last.then_inc(b2_done, 1)
            for p in range(PH):
                pe.wait_ge(w0_ready, p + 1)
                for kk in range(4):
                    last = pe.matmul(ps[p][:, 0:256], a2[:, kk, p * Q:(p + 1) * Q], g2[:, kk], start=(kk == 0), stop=(kk == 3))
                last.then_inc(a2_done, 1)


def main_program(nc, ctx, io, keep, scratch):
    def sb(name, shape, dt=F32):
        return ctx.enter_context(nc.sbuf_tensor(name, shape, dt))

    def sem(name):
        return ctx.enter_context(nc.semaphore(name))

    x = [sb(f"x{g}", [P, GROUP, Q]) for g in range(2)]
    tab = sb("tab", [P, LAYERS * KINDS * PAIR])
    y3 = [sb(f"y3_{u}", [P, TILE, Q]) for u in range(2)]
    y3t = [sb(f"y3t_{part}", [P, PH, GROUP * CH], F32R) for part in ("hi", "lo")]
    out_t = sb("out_t", [P, GROUP, PH, CH])
    z_raw = sb("z_raw", [P, GROUP * CH])
    logits = sb("logits", [E1, GROUP * CH])
    z = sb("z", [P, TILES, P])
    zt = [sb(f"zt_{part}", [P, GROUP * CH], F32R) for part in ("hi", "lo")]
    lg = sb("lg", [P, TILES, 8])
    r_a = sb("r_a", [P, TILES, 8])
    r_b = sb("r_b", [P, TILES, 8])
    oh = sb("oh", [P, TILES, 8])
    oh2 = sb("oh2", [P, TILES, 8])
    ex = sb("ex", [P, TILES, 8])
    m1 = sb("m1", [P, TILES])
    m2 = sb("m2", [P, TILES])
    ix = sb("ix", [P, TILES])
    den = sb("den", [P, TILES])
    xs = [sb(f"xs{t}", [P, TILE, HALO]) for t in range(TILES)]
    y0 = [sb(f"y0_{u}", [P, TILE, HALO]) for u in range(2)]
    y1 = [sb(f"y1_{u}", [P, 2, TILE, HALO]) for u in range(2)]
    y2 = [sb(f"y2_{u}", [P, 2, TILE, HALO]) for u in range(2)]
    w, ident = keep["w"], keep["ident"]

    conv_ps = [[ctx.enter_context(nc.psum_tensor(f"conv{u}{h}", [P, TILE, Q], F32)) for h in range(2)]
               for u in range(2)]
    tr_ps = ctx.enter_context(nc.psum_tensor("tr_ps", [P, TILE, PH, CH], F32))
    back_ps = ctx.enter_context(nc.psum_tensor("back_ps", [P, TILE, Q], F32))
    lin_ps = [ctx.enter_context(nc.psum_tensor(f"lin{h}", [P, 512], F32)) for h in range(2)]
    zt_ps = back_ps[:].rearrange("p b q -> p (b q)")

    z_ps, logit_ps = lin_ps

    x_loaded = [[sem(f"x_loaded{g}{t}") for t in range(TILES)] for g in range(2)]
    tab_loaded = [sem(f"tab_loaded{l}") for l in range(LAYERS)]
    a2_loaded = sem("a2_loaded")
    b2_loaded = sem("b2_loaded")
    stored = [[sem(f"stored{g}{t}") for t in range(TILES)] for g in range(2)]
    halos_zero = sem("halos_zero")
    xs_ready = sem("xs_ready")
    c0_done, up_done, c2_done, dn_done, tr_done = (sem(n) for n in ("c0_done", "up_done", "c2_done", "dn_done", "tr_done"))
    y0_ready, y1a_raw, y1b_raw, y1_ready, y2a_ready, y2b_ready, y3_ready, y3t_ready = (
        sem(n) for n in ("y0_ready", "y1a_raw", "y1b_raw", "y1_ready", "y2a_ready", "y2b_ready", "y3_ready",
                         "y3t_ready"))
    lin_done, out_ready, back_done, x_ready = (sem(n) for n in ("lin_done", "out_ready", "back_done", "x_ready"))
    z_done, z_raw_ready, z_turned, exp_in, exp_done, z_ready, zt_done, zt_hi, zt_ready, rchain, y3t_hi = (
        sem(n) for n in ("z_done", "z_raw_ready", "z_turned", "exp_in", "exp_done", "z_ready", "zt_done", "zt_hi",
                         "zt_ready", "rchain", "y3t_hi"))

    PHASES = 2 * LAYERS
    GATE_STEPS = {1: 17, 3: 6}

    def turned_cols(part, t):
        return y3t[part][:, :, P * t:P * (t + 1)].rearrange("q p (b c) -> q p b c", c=CH)

    COUNT = TILES * PHASES
    TAB_DMAS, ADAPTER_DMAS = PH, 4

    FIRST = [(n, True, n > 0) for n in range(PHASES)]
    STEADY = [(n, True, True) for n in range(PHASES)]
    LAST = [(0, False, True)]

    def layer(n):
        return n % PHASES // 2

    def adapters_before(it, n, layers):
        return it * 2 * len(layers) + (sum(1 for i in range(n) if layer(i) in layers) if n >= 0
                                       else -1 if layer(n) in layers else 0)

    def gate_steps_before(it, n):
        return it * 2 * sum(GATE_STEPS.values()) + (sum(GATE_STEPS.get(layer(i), 0) for i in range(n)) if n >= 0
                                                    else -GATE_STEPS[layer(n)])

    with nc.Block() as block:

        @block.sync
        def _(sp):
            def load_table(it, l):
                for g in range(PH):
                    at = table_column(l, 0, 0)
                    sp.dma_start(tab[CH * g:CH * (g + 1), at:at + KINDS * PAIR],
                                 scratch["tab"][it][:, l].rearrange("c k b -> c (k b)")).then_inc(tab_loaded[l], 16)

            def load_x(it, g, t):
                sp.dma_start(x[g][:, TILE * t:TILE * (t + 1)],
                             io["x"][2 * it + g][:, TILE * t:TILE * (t + 1)]).then_inc(x_loaded[g][t], 16)

            def load_adapters(it):
                for i in range(2):
                    for g in range(2):
                        sp.dma_start(keep["a2"][i][:, g, :, 0:R2].bitcast(F32),
                                     scratch["a2"][i][:, 2 * it + g]).then_inc(a2_loaded, 16)
                        sp.dma_start(keep["b2"][i][0:R2, g].bitcast(F32),
                                     scratch["b2"][i][2 * it + g]).then_inc(b2_loaded, 16)

            def store(it, g, t):
                sp.wait_ge(x_ready, it * COUNT + TILES * (PHASES - 2 + g) + t + 1)
                sp.dma_start(io["out"][2 * it + g][:, TILE * t:TILE * (t + 1)],
                             x[g][:, TILE * t:TILE * (t + 1)]).then_inc(stored[g][t], 16)

            load_table(0, 0)
            for g in range(2):
                for t in range(TILES):
                    load_x(0, g, t)
            for l in range(1, LAYERS):
                load_table(0, l)
            load_adapters(0)
            with sp.Fori(1, ITERS) as it:
                last = it - 1
                for l in range(LAYERS):
                    if l < LAYERS - 1:
                        sp.wait_ge(y3_ready, last * COUNT + TILES * 2 * (l + 1))
                        load_table(it, l)
                    if l == 2:
                        sp.wait_ge(lin_done, last * COUNT + PH * 2 * (l + 1))
                        load_adapters(it)
                for g in range(2):
                    for t in range(TILES):
                        store(last, g, t)
                    for t in range(TILES):
                        sp.wait_ge(stored[g][t], it * 16)
                        load_x(it, g, t)
                    if g == 0:
                        sp.wait_ge(y3_ready, it * COUNT)
                        load_table(it, LAYERS - 1)
            for g in range(2):
                for t in range(TILES):
                    store(ITERS - 1, g, t)
            for g in range(2):
                for t in range(TILES):
                    sp.wait_ge(stored[g][t], ITERS * 16)

        @block.gpsimd
        def _(pool):
            def scale_x(it, n, t):
                l, g = layer(n), n % 2
                if n or type(it) is not int:
                    pool.wait_ge(c0_done, it * COUNT + TILES * (n - 1) + t + 1)
                lo = table_column(l, T_S, GROUP * g + TILE * t)
                nc.gpsimd.tensor_tensor(
                    xs[t][:, :, 1:Q + 1], x[g][:, TILE * t:TILE * (t + 1)],
                    tab[:, lo:lo + TILE].unsqueeze(2).broadcast_to((P, TILE, Q)), ALU.mult).then_inc(xs_ready, 1)

            def iteration(it):
                for n in range(PHASES):
                    if n % 2 == 0:
                        pool.wait_ge(tab_loaded[layer(n)], (it + 1) * (16 * TAB_DMAS))
                    for t in range(TILES):
                        if n < 2:
                            pool.wait_ge(x_loaded[n][t], (it + 1) * 16)
                        else:
                            pool.wait_ge(x_ready, it * COUNT + TILES * (n - 2) + t + 1)
                        scale_x(it, n, t)

            iteration(0)
            with pool.Fori(1, ITERS) as it:
                iteration(it)

        @block.scalar
        def _(act):
            a = nc.scalar

            def iteration(it, phases):
                start = it * COUNT
                later = not (isinstance(it, int) and it == 0)

                def tiles(n, t):
                    return start + TILES * n + t

                def products(n, p):
                    return start + PH * n + p

                def factors(l, k, n, t, b):
                    sample = GROUP * (n % 2) + TILE * t + b
                    at, bias_at = table_column(l, T_A + k, sample), table_column(l, T_B + k, sample)
                    return tab[:, at:at + 1], tab[:, bias_at:bias_at + 1]

                def half(n, t, k, y, done, ready):
                    act.wait_ge(done, tiles(n, t + 1))
                    for b in range(TILE):
                        s, c = factors(layer(n), k, n, t, b)
                        ins = a.activation(y[t % 2][:, 0, b, 1:Q + 1], conv_ps[t % 2][0][:, b], ACT.Identity,
                                           bias=c, scale=s)
                    ins.then_inc(ready, 1)

                def up(n, t):
                    half(n, t, 1, y1, up_done, y1a_raw)

                def third(n, t):
                    half(n, t, 2, y2, c2_done, y2a_ready)

                def first(n, t):
                    act.wait_ge(c0_done, tiles(n, t + 1))
                    for b in range(TILE):
                        s, c = factors(layer(n), 0, n, t, b)
                        ins = a.activation(y0[t % 2][:, b, 1:Q + 1], conv_ps[t % 2][1][:, b], ACT.Identity,
                                           bias=c, scale=s)
                    ins.then_inc(y0_ready, 1)

                def turned(n, t):
                    act.wait_ge(tr_done, tiles(n, t + 1))
                    a.activation(turned_cols(0, t), tr_ps[:].rearrange("q b p c -> q p b c"), ACT.Copy).then_inc(y3t_hi, 1)

                def adapter(n):
                    l = layer(n)
                    if l:
                        act.wait_ge(z_done, adapters_before(it, n, (1, 2, 3)) + 1)
                    if l == 1:
                        a.activation(z_raw[:], z_ps[:], ACT.Copy)
                        a.activation(logits[:], logit_ps[0:E1], ACT.Copy).then_inc(z_raw_ready, 1)
                    elif l == 2:
                        a.activation(zt[0][0:Z23], z_ps[0:Z23], ACT.Copy).then_inc(zt_hi, 1)
                    elif l == 3:
                        a.activation(z_raw[0:Z23], z_ps[0:Z23], ACT.Copy).then_inc(z_raw_ready, 1)

                def exponentials(n):
                    if layer(n) == 1:
                        act.wait_ge(exp_in, adapters_before(it, n, (1,)) + 1)
                        a.activation(ex[:], r_a[:], ACT.Exp).then_inc(exp_done, 1)

                def adapter_turned(n):
                    if layer(n) in (1, 3):
                        rows = E1 * R1 if layer(n) == 1 else E3 * R3
                        act.wait_ge(zt_done, adapters_before(it, n, (1, 3)) + 1)
                        a.activation(zt[0][0:rows], zt_ps[0:rows], ACT.Copy).then_inc(zt_hi, 1)

                def linear_out(n):
                    l = layer(n)
                    for p in range(PH):
                        act.wait_ge(lin_done, products(n, p + 1))
                        src = lin_ps[p % 2][:].rearrange("q (b c) -> q b c", c=CH)
                        if l < 3:
                            ins = a.activation(out_t[:, :, p], src, ACT.Identity,
                                               bias=keep["ob"][:, PH * l + p:PH * l + p + 1])
                        else:
                            ins = a.activation(out_t[:, :, p], src, ACT.Copy)
                        ins.then_inc(out_ready, 1)

                for n, convolve, linear in phases:
                    m = n - 1
                    if convolve:
                        if n % 2 == 0:
                            act.wait_ge(tab_loaded[layer(n)], (it + 1) * (16 * TAB_DMAS))
                        first(n, 0)
                        first(n, 1)
                    for t in range(2):
                        if linear:
                            turned(m, 2 + t)
                        if convolve:
                            up(n, t)
                    if linear:
                        adapter(m)
                    if convolve:
                        third(n, 0)
                    if linear:
                        exponentials(m)
                    if convolve:
                        third(n, 1)
                    if linear:
                        adapter_turned(m)
                        linear_out(m)
                    if convolve:
                        first(n, 2)
                        first(n, 3)
                        for t in range(2):
                            turned(n, t)
                            up(n, 2 + t)
                        third(n, 2)
                        third(n, 3)

            iteration(0, FIRST)
            with act.Fori(1, ITERS) as it:
                iteration(it, STEADY)
            iteration(ITERS, LAST)

        @block.vector
        def _(dve):
            v = nc.vector
            for u in range(2):
                v.memset(y0[u][:, :, 0:HALO:HALO - 1], 0.0)
                for y in (y1[u], y2[u]):
                    v.memset(y[:, :, :, 0:HALO:HALO - 1], 0.0)
            for t in range(TILES):
                ins = v.memset(xs[t][:, :, 0:HALO:HALO - 1], 0.0)
            ins.then_inc(halos_zero, 1)
            def iteration(it, phases):
                start = it * COUNT
                later = not (isinstance(it, int) and it == 0)

                def tiles(n, t):
                    return start + TILES * n + t

                def products(n, p):
                    return start + PH * n + p

                steps, gates_start = 0, 0

                def then(ins):
                    nonlocal steps
                    steps += 1
                    ins.then_inc(rchain, 1)
                    dve.wait_ge(rchain, gates_start + steps)

                def evacuate(n, t, k, dst, src, done, ready):
                    l = layer(n)
                    dve.wait_ge(done, tiles(n, t + 1))
                    for b in range(TILE):
                        sample = GROUP * (n % 2) + TILE * t + b
                        at, bias_at = table_column(l, T_A + k, sample), table_column(l, T_B + k, sample)
                        c = tab[:, bias_at:bias_at + 1] if k < 3 else keep["cb3"][:, l:l + 1]
                        ins = v.tensor_scalar(dst[:, b], src[:, b], tab[:, at:at + 1], c,
                                              ALU.mult, ALU.add)
                    ins.then_inc(ready, 1)

                def up(n, t):
                    evacuate(n, t, 1, y1[t % 2][:, 1, :, 1:Q + 1], conv_ps[t % 2][1], up_done, y1b_raw)
                    at = table_column(layer(n), T_D, GROUP * (n % 2) + TILE * t)
                    for half, q, group, raw in ((0, 1, HI_A.index(0), y1a_raw), (1, Q, HI_B.index(7), y1b_raw)):
                        rows = slice(CH * group, CH * (group + 1))
                        end = y1[t % 2][rows, half, :, q]
                        dve.wait_ge(raw, tiles(n, t + 1))
                        ins = v.tensor_tensor(end, end, tab[rows, at:at + TILE], ALU.add)
                    ins.then_inc(y1_ready, 1)

                def third(n, t):
                    evacuate(n, t, 2, y2[t % 2][:, 1, :, 1:Q + 1], conv_ps[t % 2][1], c2_done, y2b_ready)

                def down(n, t):
                    evacuate(n, t, 3, y3[t % 2][:], conv_ps[t % 2][0], dn_done, y3_ready)

                def residual(n, t):
                    dve.wait_ge(back_done, tiles(n, t + 1))
                    xt = x[n % 2][:, TILE * t:TILE * (t + 1)]
                    v.tensor_tensor(xt, back_ps[:], xt, ALU.add).then_inc(x_ready, 1)

                def turned(n, t):
                    dve.wait_ge(y3t_hi, tiles(n, t + 1))
                    v.tensor_tensor(turned_cols(1, t), tr_ps[:].rearrange("q b p c -> q p b c"),
                                    turned_cols(0, t).bitcast(F32), ALU.subtract).then_inc(y3t_ready, 1)

                def wide(small, e):
                    return small[:].unsqueeze(2).broadcast_to((P, TILES, e))

                def best(scores, e, mask, top):
                    iota = keep["iota"][:, 0:e].unsqueeze(1).broadcast_to((P, TILES, e))
                    then(v.tensor_reduce(top[:], scores, AX.X, ALU.max))
                    then(v.tensor_tensor(r_b[:, :, 0:e], scores, wide(top, e), ALU.is_equal))
                    then(v.tensor_tensor(r_b[:, :, 0:e], r_b[:, :, 0:e], iota, ALU.mult))
                    then(v.tensor_reduce(ix[:], r_b[:, :, 0:e], AX.X, ALU.min))
                    then(v.tensor_tensor(mask[:, :, 0:e], wide(ix, e), iota, ALU.is_equal))

                def gated(n):
                    nonlocal steps, gates_start
                    l = layer(n)
                    if l not in (1, 3):
                        return
                    steps, gates_start = 0, gate_steps_before(it, n)
                    e, r = (E1, R1) if l == 1 else (E3, R3)
                    dve.wait_ge(z_turned, adapters_before(it, n, (1, 3)) + 1)
                    if l == 1:
                        then(v.tensor_copy(lg[:], logit_ps[:, 0:TILES * E1].rearrange("p (t e) -> p t e", e=E1)))
                    else:
                        then(v.tensor_tensor(lg[:, :, 0:e], z_ps[:].rearrange("p (t c) -> p t c", c=P)
                                             [:, :, e * r:e * r + e],
                                             keep["eb3"][:].unsqueeze(1).broadcast_to((P, TILES, e)), ALU.add))
                    best(lg[:, :, 0:e], e, oh, m1)
                    if l == 1:
                        v.tensor_tensor(r_a[:], lg[:], wide(m1, e), ALU.subtract).then_inc(exp_in, 1)
                        then(v.scalar_tensor_tensor(out=lg[:], in0=oh[:], scalar=LOWEST, in1=lg[:],
                                                    op0=ALU.mult, op1=ALU.add))
                        best(lg[:], e, oh2, m2)
                        then(v.tensor_tensor(oh[:], oh[:], oh2[:], ALU.add))
                        dve.wait_ge(exp_done, adapters_before(it, n, (1,)) + 1)
                        then(v.tensor_tensor(oh[:], oh[:], ex[:], ALU.mult))
                        then(v.tensor_reduce(den[:], oh[:], AX.X, ALU.add))
                        then(v.reciprocal(den[:], den[:]))
                        then(v.scalar_tensor_tensor(out=oh[:], in0=oh[:], scalar=LORA1_SCALE, in1=wide(den, e),
                                                    op0=ALU.mult, op1=ALU.mult))
                    assert steps == GATE_STEPS[l]
                    for t in range(TILES):
                        ins = v.tensor_tensor(
                            z[:, t, 0:e * r].rearrange("p (e r) -> p e r", r=r),
                            z_ps[:, P * t:P * t + e * r].rearrange("p (e r) -> p e r", r=r),
                            oh[:, t, 0:e].unsqueeze(2).broadcast_to((P, e, r)), ALU.mult)
                    ins.then_inc(z_ready, 1)

                def adapter_turned(n, layers):
                    l = layer(n)
                    if l in layers:
                        rows = (0, E1 * R1, Z23, E3 * R3)[l]
                        src = z_ps if l == 2 else zt_ps
                        dve.wait_ge(zt_hi, adapters_before(it, n, (1, 2, 3)) + 1)
                        v.tensor_tensor(zt[1][0:rows], src[0:rows], zt[0][0:rows].bitcast(F32),
                                        ALU.subtract).then_inc(zt_ready, 1)

                for n, convolve, linear in phases:
                    m = n - 1
                    if convolve and n % 2 == 0:
                        dve.wait_ge(tab_loaded[layer(n)], (it + 1) * (16 * TAB_DMAS))
                    if linear:
                        down(m, TILES - 1)
                    for t in range(2):
                        if linear:
                            turned(m, 2 + t)
                        if convolve:
                            up(n, t)
                    if linear:
                        adapter_turned(m, (2,))
                    if convolve:
                        third(n, 0)
                    if linear:
                        gated(m)
                    if convolve:
                        third(n, 1)
                        down(n, 0)
                    if linear:
                        adapter_turned(m, (1, 3))
                        residual(m, 0)
                    if convolve:
                        down(n, 1)
                    if linear:
                        residual(m, 1)
                    for t in range(2):
                        if convolve:
                            turned(n, t)
                            up(n, 2 + t)
                        if linear:
                            residual(m, 2 + t)
                    if convolve:
                        third(n, 2)
                        third(n, 3)
                        down(n, 2)

            iteration(0, FIRST)
            with dve.Fori(1, ITERS) as it:
                iteration(it, STEADY)
            iteration(ITERS, LAST)

        @block.tensor
        def _(pe):
            def iteration(it, phases):
                start = it * COUNT
                later = not (isinstance(it, int) and it == 0)

                def tiles(n, t):
                    return start + TILES * n + t

                def products(n, p):
                    return start + PH * n + p

                def mm(out, weights, l, first_block, blocks, rhs, start, stop):
                    return pe.matmul(out, weights[:, l, first_block * CH:(first_block + blocks) * CH], rhs,
                                     start=start, stop=stop, skip_group_check=True)

                wp, wm = keep["wp"], keep["wm"]

                def conv0_pair(n, t):
                    l = layer(n)
                    both = (t, t + 1)
                    for t in both:
                        u = t % 2
                        pe.wait_ge(xs_ready, tiles(n, t + 1))
                        if later or TILES * n + t >= 2:
                            pe.wait_ge(y2b_ready, tiles(n, t - 1))
                        mm(conv_ps[u][1][:], wp, l, C0_MID[u], 4, xs[t][:, :, 1:Q + 1], True, False)
                    for t in both:
                        u = t % 2
                        ps, xt = conv_ps[u][1], xs[t]
                        left, right = ((0, 3), (1, 2))[u]
                        mm(ps[left * CH:(left + 1) * CH], wp, l, C0_LEFT, 1, xt[:, :, 0:Q], False, True)
                        mm(ps[right * CH:(right + 1) * CH], wp, l, C0_RIGHT, 1, xt[:, :, 2:Q + 2],
                           False, True).then_inc(c0_done, 1)

                def conv_up(n, t):
                    l, u = layer(n), t % 2
                    pe.wait_ge(y0_ready, tiles(n, t + 1))
                    if later or TILES * n + t >= 2:
                        pe.wait_ge(y3_ready, tiles(n, t - 1))
                    y, at = y0[u], (0, UP_ODD)[u]
                    mm(conv_ps[u][0][:], wm, l, at + UP_A, 4, y[:, :, 1:Q + 1], True, False)
                    mm(conv_ps[u][1][:], wm, l, at + UP_B, 4, y[:, :, 1:Q + 1], True, False)
                    mm(conv_ps[u][0][0:2 * CH], wm, l, at + UP_LEFT, 2, y[:, :, 0:Q], False, True)
                    mm(conv_ps[u][1][2 * CH:P], wm, l, at + UP_RIGHT, 2, y[:, :, 2:Q + 2], False, True).then_inc(up_done, 1)

                def conv2(n, t):
                    l, u = layer(n), t % 2
                    pe.wait_ge(y1_ready, tiles(n, t + 1))
                    ya, yb = y1[u][:, 0], y1[u][:, 1]
                    pa, pb = conv_ps[u]
                    mm(pa[:], wp, l, C2_A, 4, ya[:, :, 1:Q + 1], True, False)
                    mm(pb[:], wp, l, C2_B, 4, yb[:, :, 1:Q + 1], True, False)
                    mm(pa[0:CH], wp, l, C2_SIDES, 1, yb[:, :, 0:Q], False, True)
                    mm(pa[3 * CH:P], wp, l, C2_SIDES + 1, 1, yb[:, :, 1:Q + 1], False, True)
                    mm(pb[CH:2 * CH], wp, l, C2_SIDES + 2, 1, ya[:, :, 1:Q + 1], False, True)
                    mm(pb[2 * CH:3 * CH], wp, l, C2_SIDES + 3, 1, ya[:, :, 2:Q + 2], False, True).then_inc(c2_done, 1)

                def conv_down(n, t):
                    l, u = layer(n), t % 2
                    pe.wait_ge(y2a_ready, tiles(n, t + 1))
                    pe.wait_ge(y2b_ready, tiles(n, t + 1))
                    ya, yb = y2[u][:, 0], y2[u][:, 1]
                    ps = conv_ps[u][0]
                    for o in LO:
                        mm(ps[CH * o:CH * (o + 1)], wm, l, DN + o, 1, ya[:, :, 1:Q + 1] if o < 3 else ya[:, :, 2:Q + 2], True, False)
                    for o in LO:
                        ins = mm(ps[CH * o:CH * (o + 1)], wm, l, DN + 4 + o, 1, yb[:, :, 0:Q] if o == 0 else yb[:, :, 1:Q + 1], False, True)
                    ins.then_inc(dn_done, 1)

                def turn(n, t):
                    pe.wait_ge(y3_ready, tiles(n, t + 1))
                    if later or TILES * n + t:
                        pe.wait_ge(y3t_ready, tiles(n, t))
                    for b in range(TILE):
                        ins = pe.transpose(tr_ps[:, b].rearrange("q p c -> q (p c)"), y3[t % 2][:, b], ident[:])
                    ins.then_inc(tr_done, 1)

                def adapter(n):
                    l, g = layer(n), n % 2
                    if l == 0:
                        return
                    pe.wait_ge(y3t_ready, tiles(n, TILES))
                    pe.wait_ge(out_ready, products(n, 0))
                    if l == 2:
                        pe.wait_ge(a2_loaded, (it + 1) * (16 * ADAPTER_DMAS))
                    a_l = (None, keep["a1"], [a[:, g] for a in keep["a2"]], keep["a3"])[l]
                    parts = [(z_ps, 0, P), (logit_ps, P, E1)] if l == 1 else [(z_ps, 0, Z23)]
                    for ps, col, rows in parts:
                        for p in range(PH):
                            for i, (ai, yi) in enumerate(PASSES):
                                ins = pe.matmul(ps[0:rows], a_l[ai][:, p, col:col + rows], y3t[yi][:, p],
                                                start=(p == 0 and i == 0), stop=(p == PH - 1 and i == 2))
                    ins.then_inc(z_done, 1)

                def to_tokens(n):
                    l = layer(n)
                    if l not in (1, 3):
                        return
                    pe.wait_ge(z_raw_ready, adapters_before(it, n, (1, 3)) + 1)
                    for t in range(TILES):
                        tokens = slice(P * t, P * (t + 1))
                        ins = pe.transpose(z_ps[:, tokens], z_raw[:, tokens], ident[:])
                        if l == 1:
                            ins = pe.transpose(logit_ps[:, E1 * t:E1 * (t + 1)], logits[:, tokens], ident[0:E1, 0:E1])
                    ins.then_inc(z_turned, 1)

                def adapter_turn(n):
                    l = layer(n)
                    if l not in (1, 3):
                        return
                    rows = E1 * R1 if l == 1 else E3 * R3
                    pe.wait_ge(z_ready, adapters_before(it, n, (1, 3)) + 1)
                    pe.wait_ge(x_ready, tiles(n, 0))
                    for t in range(TILES):
                        ins = pe.transpose(zt_ps[0:rows, P * t:P * (t + 1)], z[:, t, 0:rows], ident[:])
                    ins.then_inc(zt_done, 1)

                def linear_layer(n):
                    l, g = layer(n), n % 2
                    pe.wait_ge(y3t_ready, tiles(n, TILES))
                    if l == 2:
                        pe.wait_ge(b2_loaded, (it + 1) * (16 * ADAPTER_DMAS))
                        pe.wait_ge(zt_ready, adapters_before(it, n, (1, 2, 3)) + 1)
                    b_l = (None, keep["b1"], [b[:, g] for b in keep["b2"]], keep["b3"])[l]
                    for p in range(PH):
                        if later or PH * n + p >= 2:
                            pe.wait_ge(out_ready, products(n, p - 1))
                        ps = lin_ps[p % 2]
                        for k in range(PH):
                            for i, (wi, yi) in enumerate(PASSES):
                                ins = pe.matmul(ps[:], w[wi][:, l, k, p * Q:(p + 1) * Q], y3t[yi][:, k],
                                                start=(k == 0 and i == 0), stop=(k == PH - 1 and i == 2 and l == 0))
                        if l:
                            if p == 0 and l != 2:
                                pe.wait_ge(zt_ready, adapters_before(it, n, (1, 2, 3)) + 1)
                            for i, (bi, zi) in enumerate(PASSES):
                                ins = pe.matmul(ps[:], b_l[bi][:, p * Q:(p + 1) * Q], zt[zi][:], start=False, stop=(i == 2))
                        ins.then_inc(lin_done, 1)

                def turn_back(n, t):
                    if t == 0:
                        pe.wait_ge(out_ready, products(n, PH))
                    if later or TILES * n + t:
                        pe.wait_ge(x_ready, tiles(n, t))
                    for b in range(TILE):
                        ins = pe.transpose(back_ps[:, b], out_t[:, TILE * t + b].rearrange("q p c -> q (p c)"), ident[:])
                    ins.then_inc(back_done, 1)

                for n, convolve, linear in phases:
                    m = n - 1
                    if convolve:
                        conv0_pair(n, 0)
                    if linear:
                        conv_down(m, TILES - 1)
                    for t in range(2):
                        if linear:
                            turn(m, 2 + t)
                        if convolve:
                            conv_up(n, t)
                    if linear:
                        adapter(m)
                    if convolve:
                        conv2(n, 0)
                    if linear:
                        to_tokens(m)
                    if convolve:
                        conv2(n, 1)
                        conv_down(n, 0)
                    if linear:
                        adapter_turn(m)
                        linear_layer(m)
                    if convolve:
                        conv0_pair(n, 2)
                    if linear:
                        turn_back(m, 0)
                    if convolve:
                        conv_down(n, 1)
                    if linear:
                        turn_back(m, 1)
                    for t in range(2):
                        if convolve:
                            turn(n, t)
                            conv_up(n, 2 + t)
                        if linear:
                            turn_back(m, 2 + t)
                    if convolve:
                        conv2(n, 2)
                        conv2(n, 3)
                        conv_down(n, 2)

            pe.wait_ge(halos_zero, 1)
            iteration(0, FIRST)
            with pe.Fori(1, ITERS) as it:
                iteration(it, STEADY)
            iteration(ITERS, LAST)


def build(nc, io):
    with ExitStack() as ctx:
        def sb(name, shape, dt=F32):
            return ctx.enter_context(nc.sbuf_tensor(name, shape, dt))

        def pair(name, shape):
            return [sb(f"{name}_{part}", shape, F32R) for part in ("hi", "lo")]

        keep = {
            "wp": sb("w_placed", [P, LAYERS, NP * CH]),
            "wm": sb("w_mixed", [P, LAYERS, (NM + NUP) * CH]),
            "w": pair("w_lin", [P, LAYERS, PH, LEN]),
            "ob": sb("ob", [P, 3 * PH]),
            "ident": sb("ident", [P, P]),
            "iota": sb("iota", [P, 8]),
            "a1": pair("a1", [P, PH, Z1]),
            "b1": pair("b1", [P, LEN]),
            "a2": pair("a2_cur", [P, 2, PH, Z23]),
            "b2": pair("b2_cur", [P, 2, LEN]),
            "eb3": sb("eb3", [P, E3]),
            "cb3": sb("cb3", [P, LAYERS]),
            "a3": pair("a3", [P, PH, Z23]),
            "b3": pair("b3", [P, LEN]),
        }
        scratch = {
            "tab": nc.dram_tensor("tab_scratch", [ITERS, CH, LAYERS, KINDS, PAIR], F32).ap(),
            "a2": nc.dram_tensor("a2_scratch", [2, P, 8, PH, R2], F32).ap(),
            "b2": nc.dram_tensor("b2_scratch", [2, 8, R2, LEN], F32).ap(),
        }
        with ExitStack() as inner:
            setup_program(nc, inner, io, keep, scratch)
        with ExitStack() as inner:
            main_program(nc, inner, io, keep, scratch)


def placed_blocks(cw_in):
    where = block_coefficients(PLACED)
    out = np.zeros((PH, CH, LAYERS, NP, CH), np.float32)
    for g, t, n in zip(*np.nonzero(where)):
        out[g, :, :, n] = cw_in[:, :, PLACED[n][0], t]
    return out.reshape(P, LAYERS, NP * CH)


def host_layout(i):
    c = np.ascontiguousarray

    def cols(a):
        return c(a.reshape(a.shape[:-1] + (Q, PH)).swapaxes(-1, -2).reshape(a.shape))

    def rows(a):
        return c(a.reshape((Q, PH) + a.shape[1:]))

    def rep(a):
        return c(np.tile(a, (PH,) + (1,) * (a.ndim - 1)))

    def every(a):
        return c(np.tile(a[None], (P, 1)))

    cw_oikt = np.stack([i[f"L{l}_cond_weights"] for l in range(LAYERS)])
    cw_in = cw_oikt.transpose(3, 0, 1, 4, 2).copy()
    cw_in[:, :, 1] = cw_oikt[:, 1].transpose(1, 0, 3, 2)
    mod_w = np.stack([i[f"L{l}_cond_mod_w"] for l in range(LAYERS)])
    mod_b = np.stack([i[f"L{l}_cond_mod_b"] for l in range(LAYERS)])
    bias = np.stack([i[f"L{l}_cond_biases"] for l in range(LAYERS)])
    wq = np.zeros((LAYERS, CH, CONVS, TAPS, LAYERS, CH), np.float32)
    for l in range(LAYERS):
        wq[l, :, :, :, l] = cw_oikt[l].transpose(2, 0, 3, 1)
    w_do = [i["L0_ffn_W"].T, i["L1_ffn_W_base"].T, i["L2_ffn_kernel"], i["L3_ffn_W_up"].T]
    w = np.stack([rows(cols(c(m))) for m in w_do], axis=1)
    ob = np.stack([rows(i[k]) for k in ("L0_ffn_bias", "L1_ffn_b_base", "L2_ffn_bias")], axis=1)
    a0 = cols(i["L0_ffn_A"].reshape(256, LEN)).reshape(2, P, LEN).transpose(1, 0, 2)
    b0 = cols(c(i["L0_ffn_Bf"].transpose(0, 2, 1)).reshape(256, LEN)).reshape(2, P, LEN).transpose(1, 0, 2)
    a2 = cols(i["L2_ffn_lora_A"].reshape(512, LEN)).reshape(4, P, LEN).transpose(1, 0, 2)
    b2 = cols(c(i["L2_ffn_lora_B"].transpose(0, 2, 1)).reshape(512, LEN)).reshape(4, P, LEN).transpose(1, 0, 2)
    x = i["x"].reshape(2 * ITERS, GROUP, CH, Q, PH).transpose(0, 4, 2, 1, 3).reshape(2 * ITERS, P, GROUP, Q)
    return {k: c(a) for k, a in {
        "x": x,
        "cond_t": i["cond_512"].T,
        "mod_w": mod_w.transpose(3, 1, 0, 2).reshape(STYLE, CONVS, P),
        "mod_b": mod_b.transpose(0, 2, 1).reshape(P, CONVS),
        "conv_b": bias.transpose(0, 2, 1).reshape(P, CONVS),
        "cb3": rep(bias[:, 3].T),
        "wq": wq.reshape(P, CONVS, TAPS, P),
        "cw": rep(cw_in[:, :, 1::2]),
        "coef": np.repeat(block_coefficients(MIXED), CH, axis=0),
        "wp": placed_blocks(cw_in),
        "w": w, "ob": ob.reshape(P, 3 * PH),
        "a0": a0, "b0": b0,
        "coeffs": np.repeat(i["L0_ffn_coeffs"], 16).reshape(2, P).T,
        "scales": np.repeat(i["L0_ffn_scales"], 16).reshape(2, P).T,
        "ident": np.eye(P, dtype=np.float32),
        "iota": np.tile(np.arange(8, dtype=np.float32) - 8.0, (P, 1)),
        "a1": np.concatenate([rows(i["L1_ffn_lora_A"].reshape(E1 * R1, LEN).T), rows(i["L1_ffn_W_router"].T)], axis=2),
        "b1": cols(c(i["L1_ffn_lora_B"].transpose(0, 2, 1)).reshape(E1 * R1, LEN)),
        "a2": a2, "b2": b2,
        "gate_t": np.repeat(i["L2_ffn_gate"].T, R2, axis=0).reshape(4, P, 8).transpose(1, 0, 2),
        "delta": np.tile(np.eye(R2, dtype=np.float32), (PH, 1)),
        "as2": rows(i["L2_ffn_lora_A_shared"].T),
        "bs2": cols(c(i["L2_ffn_lora_B_shared"].T)),
        "eb3": every(i["L3_ffn_expert_bias"]),
        "a3": np.concatenate([rows(i["L3_ffn_lora_A"].reshape(E3 * R3, LEN).T), rows(i["L3_ffn_gate_w"].T),
                              np.zeros((Q, PH, Z23 - E3 * R3 - E3), np.float32)], axis=2),
        "b3": cols(c(i["L3_ffn_lora_B"].transpose(0, 2, 1)).reshape(E3 * R3, LEN)),
    }.items()}


def kernel(**inputs):
    import concourse.bacc as bacc
    from concourse.bass_utils import run_bass_kernel_spmd

    arrays = host_layout({k: np.asarray(v) for k, v in inputs.items()})
    nc = bacc.Bacc("TRN2", target_bir_lowering=False, num_devices=1)
    io = {k: nc.dram_tensor(f"in_{k}", a.shape, mybir.dt.from_np(a.dtype), kind="ExternalInput").ap()
          for k, a in arrays.items()}
    io["out"] = nc.dram_tensor("out_x", arrays["x"].shape, F32, kind="ExternalOutput").ap()
    build(nc, io)
    r = run_bass_kernel_spmd(nc, [{f"in_{k}": a for k, a in arrays.items()}], core_ids=[0])
    y = r.results[0]["out_x"].reshape(2 * ITERS, PH, CH, GROUP, Q)
    return np.ascontiguousarray(y.transpose(0, 3, 2, 4, 1)).reshape(SAMPLES, CH, LEN)
```

```python
from contextlib import ExitStack

import numpy as np
import concourse.bass as bass
from concourse import mybir

SAMPLES, CH, LEN = 128, 32, 512
LAYERS, CONVS, TAPS, STYLE = 4, 4, 3, 64
P = 128
PH = P // CH
Q = LEN // PH
TILE = PH
TILES = 4
GROUP = TILE * TILES
ITERS = SAMPLES // (2 * GROUP)
PAIR = 2 * GROUP
HALO = Q + 2
E1, R1 = 8, 16
R2 = 32
E3, R3 = 4, 8
SCALE = 1.0 / float(np.sqrt(CH * TAPS ** 2))
EPS = 1e-08
Z1 = E1 * R1 + E1
Z23 = 2 * R2
LORA1_SCALE = 2.0
LOWEST = -3.0e38

F32 = mybir.dt.float32
F32R = mybir.dt.float32r
PASSES = ((0, 0), (0, 1), (1, 0))
HIGH_INPUT, LOW_INPUT = ((0, 0), (1, 0)), ((0, 1),)
ALU = mybir.AluOpType
ACT = mybir.ActivationFunctionType
AX = mybir.AxisListType

HI_A = (0, 1, 2, 3)
HI_B = (5, 4, 7, 6)
LO = (0, 1, 2, 3)

LO_ODD = (1, 0, 3, 2)

PLACED = (
    [(0, LO, 0, o) for o in LO] + [(0, LO, -1, 0), (0, LO, 1, 3)] + [(0, LO, 0, o) for o in LO_ODD]
    + [(2, HI_A, 0, o) for o in HI_A] + [(2, HI_B, 0, o) for o in HI_B]
    + [(2, HI_B, -1, 0), (2, HI_B, 0, 3), (2, HI_A, 0, 4), (2, HI_A, 1, 7)]
)
MIXED = (
    [(1, LO, 0, o) for o in HI_A] + [(1, LO, 0, o) for o in HI_B]
    + [(1, LO, -1, 0), (1, LO, -1, 1)] + [(1, LO, 1, 7), (1, LO, 1, 6)]
    + [(3, HI_A, 0, 0), (3, HI_A, 0, 1), (3, HI_A, 0, 2), (3, HI_A, 1, 3)]
    + [(3, HI_B, -1, 0), (3, HI_B, 0, 1), (3, HI_B, 0, 2), (3, HI_B, 0, 3)]
)
NP, NM = len(PLACED), len(MIXED)
C0_MID, C0_LEFT, C0_RIGHT = (0, 6), 4, 5
C2_FIRST, C2_LAST = 10, 18
NC2 = C2_LAST - C2_FIRST
C2_SIDES = C2_FIRST
NUP = sum(1 for b in MIXED if b[0] == 1)
UP_MID = 8
UP_SIDES = NUP - UP_MID
HALF = 4
DN = UP_SIDES
SIDES = (0, DN + NM - NUP)

T_A, T_B, T_S, T_D = 0, CONVS, 2 * CONVS - 1, 2 * CONVS
KINDS = T_D + 1


def table_column(layer, kind, sample):
    return PAIR * (KINDS * layer + kind) + sample


def block_coefficients(blocks):
    blur = np.array([1.0, 3.0, 3.0, 1.0]) / 8.0
    out = np.zeros((PH, TAPS, len(blocks)), np.float32)
    for n, (conv, rows, shift, o) in enumerate(blocks):
        for g, row in enumerate(rows):
            for t in range(TAPS):
                if conv == 0:
                    c = 1.0 if row + 4 * shift - o + 1 == t else 0.0
                elif conv == 1:
                    j = 2 * (row + 4 * shift) + t - o + 1
                    c = 2.0 * blur[j] if 0 <= j < 4 else 0.0
                elif conv == 2:
                    c = 1.0 if row + 8 * shift - o + 1 == t else 0.0
                else:
                    j = row + 8 * shift - 2 * o - t + 2
                    c = blur[j] if 0 <= j < 4 else 0.0
                out[g, t, n] = c
    return out


def blocks_of(eng, queue, blocks, cw, coef, conv, lo, hi, tmp, done, base):
    n = hi - lo
    out = blocks.rearrange("p l (n c) -> p l n c", c=CH)
    part = tmp[:, :, 0:n]

    def tap(t):
        return cw[:, :, conv, t].unsqueeze(2).broadcast_to((P, LAYERS, n, CH))

    def factor(t):
        return coef[:, t, lo:hi].unsqueeze(1).unsqueeze(3).broadcast_to((P, LAYERS, n, CH))

    eng.tensor_tensor(out, tap(0), factor(0), ALU.mult).then_inc(done, 1)
    for t in (1, 2):
        eng.tensor_tensor(part, tap(t), factor(t), ALU.mult).then_inc(done, 1)
        queue.wait_ge(done, base + 2 * t)
        eng.tensor_tensor(out, out, part, ALU.add).then_inc(done, 1)
        queue.wait_ge(done, base + 2 * t + 1)


def setup_program(nc, ctx, io, keep, scratch):

    def sb(name, shape, dt=F32):
        return ctx.enter_context(nc.sbuf_tensor(name, shape, dt))

    def sem(name):
        return ctx.enter_context(nc.semaphore(name))

    cond_t = sb("cond_t", [STYLE, SAMPLES])
    mod_w = sb("mod_w", [STYLE, CONVS, P])
    mod_b = sb("mod_b", [P, CONVS])
    conv_b = sb("conv_b", [P, CONVS])
    wq = sb("wq", [P, CONVS, TAPS, P])
    mod, mod_sq, var, demod = (sb(n, [P, CONVS, SAMPLES]) for n in ("mod", "mod_sq", "var", "demod"))
    root = mod_sq
    table = sb("table", [P, ITERS, KINDS, PAIR])
    w0 = sb("w0", [P, PH, LEN])
    a2 = sb("a2", [P, 4, LEN])
    b2 = sb("b2", [P, 4, LEN])
    a0 = sb("a0", [P, 2, LEN])
    b0 = sb("b0", [P, 2, LEN])
    coeffs = sb("coeffs_rep", [P, 2])
    scales = sb("scales_rep", [P, 2])
    mix = sb("mix", [P, 2])
    cw = sb("cw", [P, LAYERS, 2, TAPS, CH])
    coef = sb("coef", [P, TAPS, NM])
    up_blocks = sb("up_blocks", [P, LAYERS, 2 * NUP * CH])
    c2_blocks = sb("c2_blocks", [P, LAYERS, NC2 * CH])
    tmp_dve = sb("tmp_dve", [P, LAYERS, NUP, CH])
    tmp_pool = sb("tmp_pool", [P, LAYERS, NM - NUP, CH])
    a1 = sb("a1_raw", [P, PH, Z1])
    b1 = sb("b1_raw", [P, LEN])
    a3 = sb("a3_raw", [P, PH, Z23])
    b3 = sb("b3_raw", [P, LEN])
    as2 = sb("as2_raw", [P, PH, R2])
    bs2 = sb("bs2_raw", [2 * R2, LEN])
    gate_t = sb("gate_t", [P, 4, 8])
    delta = sb("delta", [P, R2])
    gmat = sb("gmat", [P, 4, 8, R2])
    a2eff = [a0[:].rearrange("p k n -> p (k n)").rearrange("p (b i r) -> p b i r", i=PH, r=R2).bitcast(F32R),
             sb("a2eff_lo", [P, 8, PH, R2], F32R)[:]]
    b2eff = [b0[:].bitcast(F32R), sb("b2eff_lo", [P, 2, LEN], F32R)[:]]
    ps = [ctx.enter_context(nc.psum_tensor(f"w_ps{i}", [P, 512], F32)) for i in range(6)]
    mod_ps = ctx.enter_context(nc.psum_tensor("mod_ps", [P, CONVS, SAMPLES], F32))
    var_ps = ctx.enter_context(nc.psum_tensor("var_ps", [P, CONVS, SAMPLES], F32))

    names = ("cond_t", "mod_w", "mod_b", "conv_b", "wq", "coeffs", "scales", "b0", "a0", "w0",
             "gate", "delta", "a2", "b2", "cw", "coef", "c2_blocks", "a1", "b1", "a3", "b3", "as2", "bs2")
    loaded = {n: sem(f"ld_{n}") for n in names}
    kept = sem("kept")
    mod_done, mod_ready, square_ready, wq_ready, var_done, var_ready, root_ready, chain, table_ready = (
        sem(n) for n in ("mod_done", "mod_ready", "square_ready", "wq_ready", "var_done", "var_ready",
                         "root_ready", "chain", "table_ready"))
    table_out, w0_out = sem("table_out"), sem("w0_out")
    zeroed = sem("zeroed")
    b3_zero = sem("b3_zero")
    mix_done = sem("mix_done")
    b0_ready = sem("b0_ready")
    w0_done = sem("w0_done")
    w0_ready = sem("w0_ready")
    gm_ready = sem("gm_ready")
    a2_done = sem("a2_done")
    b2_done = sem("b2_done")
    a2_hi, a2_lo, b2_hi, b2_lo = (sem(n) for n in ("a2_hi", "a2_lo", "b2_hi", "b2_lo"))
    small_hi, small_lo = sem("small_hi"), sem("small_lo")
    odd_ready, conv_hi = sem("odd_ready"), sem("conv_hi")
    blocks_dve, blocks_pool = sem("blocks_dve"), sem("blocks_pool")
    scratch_out = [sem(f"scratch_out{i}") for i in range(6)]

    S = slice(R2, 2 * R2)
    small = [
        ("a1", a1[:], [(keep["a1"][i][:]) for i in range(2)]),
        ("b1", b1[:], [(keep["b1"][i][:]) for i in range(2)]),
        ("a3", a3[:], [(keep["a3"][i][:]) for i in range(2)]),
        ("b3", b3[:], [(keep["b3"][i][:]) for i in range(2)]),
        ("as2", as2[:], [(keep["a2"][i][:, 0, :, S]) for i in range(2)]),
        ("as2", as2[:], [(keep["a2"][i][:, 1, :, S]) for i in range(2)]),
        ("bs2", bs2[S], [(keep["b2"][i][S, 0]) for i in range(2)]),
        ("bs2", bs2[S], [(keep["b2"][i][S, 1]) for i in range(2)]),
    ]

    with nc.Block() as block:

        @block.sync
        def _(sp):
            for name, dst, src in (
                ("cond_t", cond_t[:], io["cond_t"]), ("mod_w", mod_w[:], io["mod_w"]),
                ("cw", cw[:], io["cw"]), ("wq", wq[:], io["wq"]),
                ("coeffs", coeffs[:], io["coeffs"]), ("scales", scales[:], io["scales"]),
                ("b0", b0[:], io["b0"]), ("a0", a0[:], io["a0"]),
                ("w0", w0[:], io["w"][:, 0]), ("a2", a2[:], io["a2"]), ("b2", b2[:], io["b2"]),
            ):
                sp.dma_start(dst, src).then_inc(loaded[name], 16)
            sp.wait_ge(table_ready, 1)
            for l in range(LAYERS):
                sp.dma_start(scratch["tab"][:, :, l].rearrange("i c k b -> c i k b"),
                             table[CH * l:CH * (l + 1)]).then_inc(table_out, 16)
            sp.wait_ge(w0_ready, PH)
            sp.dma_start(scratch["w0"], w0[:]).then_inc(w0_out, 16)
            for i, done in ((0, b2_hi), (1, b2_lo)):
                sp.wait_ge(done, 2)
                for h in range(2):
                    sp.dma_start(scratch["b2"][i, 4 * h:4 * h + 4].rearrange("b r n -> (b r) n"),
                                 b2eff[i][:, h].bitcast(F32)).then_inc(scratch_out[2 + 2 * i + h], 16)
            for i, done in ((0, a2_hi), (1, a2_lo)):
                sp.wait_ge(done, PH)
                sp.dma_start(scratch["a2"][i], a2eff[i].bitcast(F32)).then_inc(scratch_out[i], 16)
            for s in scratch_out:
                sp.wait_ge(s, 16)
            sp.wait_ge(table_out, 16 * LAYERS)
            sp.wait_ge(w0_out, 16)

        @block.scalar
        def _(act):
            a = nc.scalar
            for name, dst, src in (
                ("coef", coef[:], io["coef"]), ("mod_b", mod_b[:], io["mod_b"]), ("conv_b", conv_b[:], io["conv_b"]),
                ("gate", gate_t[:], io["gate_t"]), ("delta", delta[:], io["delta"]),
                ("a1", a1[:], io["a1"]), ("b1", b1[:], io["b1"]), ("a3", a3[:], io["a3"]),
                ("as2", as2[:], io["as2"]), ("bs2", bs2[S], io["bs2"]),
            ):
                act.dma_start(dst, src).then_inc(loaded[name], 16)
            act.wait_ge(b3_zero, 1)
            act.dma_start(b3[0:E3 * R3], io["b3"]).then_inc(loaded["b3"], 16)
            n = 0
            for dst, src in (
                (keep["wp"][:, :, 0:C2_FIRST * CH], io["wp"][:, :, 0:C2_FIRST * CH]),
                (keep["wp"][:, :, C2_SIDES * CH:], io["wp"][:, :, C2_LAST * CH:]), (keep["ident"][:], io["ident"]), (keep["iota"][:], io["iota"]),
                (keep["ob"][:], io["ob"]), (keep["eb3"][:], io["eb3"]), (keep["cb3"][:], io["cb3"]),
            ):
                act.dma_start(dst, src).then_inc(kept, 16)
                n += 1
            act.dma_start(c2_blocks[:], io["wp"][:, :, C2_FIRST * CH:C2_LAST * CH]).then_inc(loaded["c2_blocks"], 16)
            act.wait_ge(loaded["mod_b"], 16)
            act.wait_ge(mod_done, 1)
            for k in range(CONVS):
                a.activation(mod[:, k], mod_ps[:, k], ACT.Identity, bias=mod_b[:, k:k + 1]).then_inc(mod_ready, 1)
            act.wait_ge(mod_ready, CONVS)
            a.activation(mod_sq[:], mod[:], ACT.Square).then_inc(square_ready, 1)
            act.wait_ge(var_ready, 1)
            a.activation(root[:], var[:], ACT.Sqrt).then_inc(root_ready, 1)

            act.wait_ge(blocks_dve, 5)
            for g, row in enumerate(LO_ODD):
                a.activation(up_blocks[CH * g:CH * (g + 1), :, NUP * CH:2 * NUP * CH],
                             up_blocks[CH * row:CH * (row + 1), :, 0:NUP * CH], ACT.Copy).then_inc(odd_ready, 1)
            act.wait_ge(loaded["c2_blocks"], 16)
            a.activation(keep["c2"][0][:], c2_blocks[:], ACT.Copy).then_inc(conv_hi, 1)
            act.wait_ge(odd_ready, PH)
            for u in range(2):
                mid = slice(u * NUP * CH, (u * NUP + UP_MID) * CH)
                side = slice((u * NUP + UP_MID) * CH, (u + 1) * NUP * CH)
                a.activation(keep["up"][u][0][:], up_blocks[:, :, mid], ACT.Copy).then_inc(conv_hi, 1)
                a.activation(keep["wm"][:, :, SIDES[u] * CH:(SIDES[u] + UP_SIDES) * CH], up_blocks[:, :, side], ACT.Copy)
            act.wait_ge(zeroed, 2)
            for name, v, pair in small:
                act.wait_ge(loaded[name], 16)
                a.activation(pair[0], v, ACT.Copy).then_inc(small_hi, 1)
            for h in range(2):
                act.wait_ge(b2_done, h + 1)
                a.activation(b2eff[0][:, h], ps[4 + h][:], ACT.Copy).then_inc(b2_hi, 1)
            for p in range(PH):
                act.wait_ge(a2_done, p + 1)
                a.activation(a2eff[0][:, :, p], ps[p][:, 0:256].rearrange("p (b r) -> p b r", r=R2),
                             ACT.Copy).then_inc(a2_hi, 1)
            act.wait_ge(kept, 16 * n)

        @block.gpsimd
        def _(pool):
            nc.gpsimd.memset(b3[:], 0.0).then_inc(b3_zero, 1)
            for i in range(2):
                nc.gpsimd.memset(keep["b2"][i][:].bitcast(F32), 0.0).then_inc(zeroed, 1)
            pool.wait_ge(loaded["cw"], 16)
            pool.wait_ge(loaded["coef"], 16)
            blocks_of(nc.gpsimd, pool, keep["wm"][:, :, DN * CH:(DN + NM - NUP) * CH], cw, coef, 1, NUP, NM,
                      tmp_pool, blocks_pool, 0)

        @block.vector
        def _(dve):
            v = nc.vector
            steps = 0

            def then(ins):
                nonlocal steps
                steps += 1
                ins.then_inc(chain, 1)
                dve.wait_ge(chain, steps)

            dve.wait_ge(loaded["wq"], 16)
            then(v.tensor_tensor(wq[:], wq[:], wq[:], ALU.mult))
            then(v.tensor_tensor(wq[:, :, 0], wq[:, :, 0], wq[:, :, 1], ALU.add))
            v.tensor_tensor(wq[:, :, 0], wq[:, :, 0], wq[:, :, 2], ALU.add).then_inc(wq_ready, 1)
            dve.wait_ge(loaded["coeffs"], 16)
            dve.wait_ge(loaded["scales"], 16)
            dve.wait_ge(loaded["b0"], 16)
            v.tensor_tensor(mix[:], coeffs[:], scales[:], ALU.mult).then_inc(mix_done, 1)
            dve.wait_ge(mix_done, 1)
            for kk in range(2):
                v.tensor_scalar(b0[:, kk], b0[:, kk], mix[:, kk:kk + 1], None, ALU.mult).then_inc(b0_ready, 1)
            dve.wait_ge(loaded["cw"], 16)
            dve.wait_ge(loaded["coef"], 16)
            blocks_of(v, dve, up_blocks[:, :, 0:NUP * CH], cw, coef, 0, 0, NUP, tmp_dve, blocks_dve, 0)
            dve.wait_ge(var_done, 1)
            v.tensor_scalar(var[:], var_ps[:], SCALE * SCALE, EPS, ALU.mult, ALU.add).then_inc(var_ready, 1)
            dve.wait_ge(loaded["gate"], 16)
            dve.wait_ge(loaded["delta"], 16)
            v.tensor_tensor(gmat[:], gate_t[:].unsqueeze(3).broadcast_to((P, 4, 8, R2)),
                            delta[:].unsqueeze(1).unsqueeze(1).broadcast_to((P, 4, 8, R2)),
                            ALU.mult).then_inc(gm_ready, 1)
            dve.wait_ge(root_ready, 1)
            then(v.reciprocal(demod[:], root[:]))
            then(v.tensor_tensor(root[:], demod[:], demod[:], ALU.mult))
            then(v.tensor_tensor(root[:], root[:], var[:], ALU.mult))
            then(v.tensor_scalar(root[:], root[:], -0.5, 1.5, ALU.mult, ALU.add))
            then(v.tensor_tensor(demod[:], demod[:], root[:], ALU.mult))
            dve.wait_ge(mod_ready, CONVS)

            def of(x, k):
                return x[:, k].rearrange("p (i b) -> p i b", i=ITERS)

            for k, left, right in ((0, demod, demod), (1, mod, mod), (2, demod, mod)):
                v.scalar_tensor_tensor(out=table[:, :, T_A + k], in0=of(left, k), scalar=SCALE, in1=of(right, k + 1),
                                       op0=ALU.mult, op1=ALU.mult)
            v.tensor_scalar(table[:, :, T_A + 3], of(demod, 3), SCALE, None, ALU.mult)
            dve.wait_ge(loaded["conv_b"], 16)
            for kind, k, right, c in ((T_B, 0, demod, 1.0), (T_B + 1, 1, mod, 2.0), (T_B + 2, 2, mod, 1.0),
                                      (T_D, 1, mod, -0.25)):
                v.tensor_scalar(table[:, :, kind], of(right, k + 1), conv_b[:, k:k + 1], c, ALU.mult, ALU.mult)
            v.tensor_copy(table[:, :, T_S], of(mod, 0)).then_inc(table_ready, 1)
            dve.wait_ge(conv_hi, 1)
            v.tensor_tensor(keep["c2"][1][:], c2_blocks[:], keep["c2"][0][:].bitcast(F32), ALU.subtract)
            dve.wait_ge(loaded["w0"], 16)
            for p in range(PH):
                dve.wait_ge(w0_done, p + 1)
                v.tensor_tensor(w0[:, p], ps[p][:], w0[:, p], ALU.add).then_inc(w0_ready, 1)
            for u in range(2):
                dve.wait_ge(conv_hi, 2 + u)
                v.tensor_tensor(keep["up"][u][1][:], up_blocks[:, :, u * NUP * CH:(u * NUP + UP_MID) * CH],
                                keep["up"][u][0][:].bitcast(F32), ALU.subtract)
            for k, (name, x, pair) in enumerate(small):
                dve.wait_ge(small_hi, k + 1)
                v.tensor_tensor(pair[1], x, pair[0].bitcast(F32), ALU.subtract).then_inc(small_lo, 1)
            for h in range(2):
                dve.wait_ge(b2_hi, h + 1)
                v.tensor_tensor(b2eff[1][:, h], ps[4 + h][:], b2eff[0][:, h].bitcast(F32),
                                ALU.subtract).then_inc(b2_lo, 1)
            for p in range(PH):
                dve.wait_ge(a2_hi, p + 1)
                v.tensor_tensor(a2eff[1][:, :, p], ps[p][:, 0:256].rearrange("p (b r) -> p b r", r=R2),
                                a2eff[0][:, :, p].bitcast(F32), ALU.subtract).then_inc(a2_lo, 1)

        @block.tensor
        def _(pe):
            pe.wait_ge(loaded["cond_t"], 16)
            pe.wait_ge(loaded["mod_w"], 16)
            for k in range(CONVS):
                last = pe.matmul(mod_ps[:, k], mod_w[:, k], cond_t[:], start=True, stop=True)
            last.then_inc(mod_done, 1)
            pe.wait_ge(wq_ready, 1)
            pe.wait_ge(square_ready, 1)
            for k in range(CONVS):
                last = pe.matmul(var_ps[:, k], wq[:, k, 0], mod_sq[:, k], start=True, stop=True)
            last.then_inc(var_done, 1)
            pe.wait_ge(b0_ready, 2)
            pe.wait_ge(loaded["a0"], 16)
            for p in range(PH):
                for kk in range(2):
                    last = pe.matmul(ps[p][:], a0[:, kk, p * Q:(p + 1) * Q], b0[:, kk], start=(kk == 0), stop=(kk == 1))
                last.then_inc(w0_done, 1)
            pe.wait_ge(gm_ready, 1)
            pe.wait_ge(loaded["a2"], 16)
            pe.wait_ge(loaded["b2"], 16)
            g2 = gmat[:].rearrange("p k b r -> p k (b r)")
            for h in range(2):
                for kk in range(4):
                    last = pe.matmul(ps[4 + h][:], g2[:, kk, h * P:(h + 1) * P], b2[:, kk], start=(kk == 0), stop=(kk == 3))
                last.then_inc(b2_done, 1)
            for p in range(PH):
                pe.wait_ge(w0_ready, p + 1)
                for kk in range(4):
                    last = pe.matmul(ps[p][:, 0:256], a2[:, kk, p * Q:(p + 1) * Q], g2[:, kk], start=(kk == 0), stop=(kk == 3))
                last.then_inc(a2_done, 1)


def main_program(nc, ctx, io, keep, scratch):

    def sb(name, shape, dt=F32):
        return ctx.enter_context(nc.sbuf_tensor(name, shape, dt))

    def sem(name):
        return ctx.enter_context(nc.semaphore(name))

    x = [sb(f"x{g}", [P, GROUP, Q]) for g in range(2)]
    tab = sb("tab", [P, LAYERS * KINDS * PAIR])
    xs = [sb(f"xs{t}", [P, TILE, HALO]) for t in range(TILES)]
    y0 = [sb(f"y0_{u}", [P, TILE, HALO]) for u in range(2)]
    y1 = [sb(f"y1_{u}", [P, 2, TILE, HALO]) for u in range(2)]
    y2 = [sb(f"y2_{u}", [P, 2, TILE, HALO]) for u in range(2)]
    y3 = [sb(f"y3_{u}", [P, TILE, Q]) for u in range(2)]
    y3t = [sb(f"y3t_{part}", [P, PH, GROUP * CH], F32R) for part in ("hi", "lo")]
    out_t = sb("out_t", [P, GROUP, PH, CH])
    z_raw = sb("z_raw", [P, GROUP * CH])
    logits = sb("logits", [E1, GROUP * CH])
    z = sb("z", [P, TILES, P])
    zt = [sb(f"zt_{part}", [P, GROUP * CH], F32R) for part in ("hi", "lo")]
    lg, r_a, r_b, oh, oh2, ex = (sb(n, [P, TILES, E1]) for n in ("lg", "r_a", "r_b", "oh", "oh2", "ex"))
    m1, m2, ix, den = (sb(n, [P, TILES]) for n in ("m1", "m2", "ix", "den"))
    y0_pair = [[sb(f"y0_{part}{u}", [P, TILE, Q], F32R) for part in ("hi", "lo")] for u in range(2)]
    y1_pair = [[sb(f"y1_{part}{u}", [P, 2, TILE, Q], F32R) for part in ("hi", "lo")] for u in range(2)]
    w_raw = sb("w_raw", [P, PH, LEN])
    w = [sb(f"w_{part}", [P, PH, LEN], F32R) for part in ("hi", "lo")]
    out_tiles = [sb(f"out_tile{u}", [P, TILE, Q]) for u in range(2)]
    ident = keep["ident"]

    conv_ps = [[ctx.enter_context(nc.psum_tensor(f"conv{u}{h}", [P, TILE, Q], F32)) for h in range(2)]
               for u in range(2)]
    tr_ps = ctx.enter_context(nc.psum_tensor("tr_ps", [P, TILE, PH, CH], F32))
    back_ps = ctx.enter_context(nc.psum_tensor("back_ps", [P, TILE, Q], F32))
    lin_ps = [ctx.enter_context(nc.psum_tensor(f"lin{h}", [P, 512], F32)) for h in range(2)]
    zt_ps = back_ps[:].rearrange("p b q -> p (b q)")
    turned_back = [back_ps[:]] + [ps[:].rearrange("p (b q) -> p b q", q=Q) for ps in lin_ps] + [back_ps[:]]

    z_ps, logit_ps = lin_ps

    x_loaded = [[sem(f"x_loaded{g}{t}") for t in range(TILES)] for g in range(2)]
    tab_loaded = [sem(f"tab_loaded{l}") for l in range(LAYERS)]
    a2_loaded = sem("a2_loaded")
    b2_loaded = sem("b2_loaded")
    w_loaded, w_hi, w_lo = (sem(n) for n in ("w_loaded", "w_hi", "w_lo"))
    stored = [[sem(f"stored{g}{t}") for t in range(TILES)] for g in range(2)]
    halos_zero = sem("halos_zero")
    xs_ready = sem("xs_ready")
    c0_done, up_done, c2_done, dn_done, tr_done = (sem(n) for n in ("c0_done", "up_done", "c2_done", "dn_done", "tr_done"))
    y0_raw, y0_hi, y0_lo = (sem(n) for n in ("y0_raw", "y0_hi", "y0_lo"))
    y1a_raw, y1b_raw, y1_ready, y1a_hi, y1b_hi, y1a_lo, y1b_lo = (
        sem(n) for n in ("y1a_raw", "y1b_raw", "y1_ready", "y1a_hi", "y1b_hi", "y1a_lo", "y1b_lo"))
    y2a_ready, y2b_ready, y3_ready, y3t_hi, y3t_ready = (
        sem(n) for n in ("y2a_ready", "y2b_ready", "y3_ready", "y3t_hi", "y3t_ready"))
    lin_done, out_ready, back_done, x_ready = (sem(n) for n in ("lin_done", "out_ready", "back_done", "x_ready"))
    z_done, z_raw_ready, z_turned, exp_in, exp_done, z_ready, zt_done, zt_hi, zt_ready, rchain = (
        sem(n) for n in ("z_done", "z_raw_ready", "z_turned", "exp_in", "exp_done", "z_ready", "zt_done", "zt_hi",
                         "zt_ready", "rchain"))

    PHASES = 2 * LAYERS
    GATE_STEPS = {1: 17, 3: 6}

    def turned_cols(part, t):
        return y3t[part][:, :, P * t:P * (t + 1)].rearrange("q p (b c) -> q p b c", c=CH)

    COUNT = TILES * PHASES
    TAB_DMAS, ADAPTER_DMAS = PH, 4

    FIRST = [(n, True, n > 0) for n in range(PHASES)]
    STEADY = [(n, True, True) for n in range(PHASES)]
    LAST = [(0, False, True)]

    def layer(n):
        return n % PHASES // 2

    def adapters_before(it, n, layers):
        return it * 2 * len(layers) + (sum(1 for i in range(n) if layer(i) in layers) if n >= 0
                                       else -1 if layer(n) in layers else 0)

    def gate_steps_before(it, n):
        return it * 2 * sum(GATE_STEPS.values()) + (sum(GATE_STEPS.get(layer(i), 0) for i in range(n)) if n >= 0
                                                    else -GATE_STEPS[layer(n)])

    def load_table(it, l, queue):
        for g in range(PH):
            at = table_column(l, 0, 0)
            queue.dma_start(tab[CH * g:CH * (g + 1), at:at + KINDS * PAIR],
                            scratch["tab"][it][:, l].rearrange("c k b -> c (k b)")).then_inc(tab_loaded[l], 16)

    with nc.Block() as block:

        @block.sync
        def _(sp):
            def load_x(it, g, t):
                sp.dma_start(x[g][:, TILE * t:TILE * (t + 1)],
                             io["x"][2 * it + g][:, TILE * t:TILE * (t + 1)]).then_inc(x_loaded[g][t], 16)

            def load_adapters(it):
                for i in range(2):
                    for g in range(2):
                        sp.dma_start(keep["a2"][i][:, g, :, 0:R2].bitcast(F32),
                                     scratch["a2"][i][:, 2 * it + g]).then_inc(a2_loaded, 16)
                        sp.dma_start(keep["b2"][i][0:R2, g].bitcast(F32),
                                     scratch["b2"][i][2 * it + g]).then_inc(b2_loaded, 16)

            def load_weights(it, l):
                if l or not isinstance(it, int):
                    sp.wait_ge(w_lo, (it * LAYERS + l) * PH)
                sp.dma_start(w_raw[:], io["w"][:, l] if l else scratch["w0"]).then_inc(w_loaded, 16)

            def result_ready(it, g, t):
                sp.wait_ge(x_ready, it * COUNT + TILES * (PHASES - 2 + g) + t + 1)

            def store(it, g, t):
                sp.dma_start(io["out"][2 * it + g][:, TILE * t:TILE * (t + 1)], out_tiles[t % 2][:]).then_inc(stored[g][t], 16)

            for g in range(2):
                for t in range(TILES):
                    load_x(0, g, t)
            for l in range(1, LAYERS):
                load_table(0, l, sp)
            load_weights(0, 0)
            load_adapters(0)
            with sp.Fori(1, ITERS) as it:
                last = it - 1
                for l in range(LAYERS):
                    if l < LAYERS - 1:
                        load_weights(last, l + 1)
                        sp.wait_ge(y3_ready, last * COUNT + TILES * 2 * (l + 1))
                        load_table(it, l, sp)
                    if l == 2:
                        sp.wait_ge(lin_done, last * COUNT + PH * 2 * (l + 1))
                        load_adapters(it)
                load_weights(it, 0)
                for g in range(2):
                    for t in range(TILES):
                        result_ready(last, g, t)
                        load_x(it, g, t)
                        store(last, g, t)
                    if g == 0:
                        sp.wait_ge(y3_ready, it * COUNT)
                        load_table(it, LAYERS - 1, sp)
            for l in range(1, LAYERS):
                load_weights(ITERS - 1, l)
            for g in range(2):
                for t in range(TILES):
                    result_ready(ITERS - 1, g, t)
                    store(ITERS - 1, g, t)
            for g in range(2):
                for t in range(TILES):
                    sp.wait_ge(stored[g][t], ITERS * 16)

        @block.gpsimd
        def _(pool):
            def scale_x(it, n, t):
                l, g = layer(n), n % 2
                if n or type(it) is not int:
                    pool.wait_ge(c0_done, it * COUNT + TILES * (n - 1) + t + 1)
                lo = table_column(l, T_S, GROUP * g + TILE * t)
                nc.gpsimd.tensor_tensor(
                    xs[t][:, :, 1:Q + 1], x[g][:, TILE * t:TILE * (t + 1)],
                    tab[:, lo:lo + TILE].unsqueeze(2).broadcast_to((P, TILE, Q)), ALU.mult).then_inc(xs_ready, 1)

            def rest(lo, value, hi):
                return nc.gpsimd.tensor_tensor(lo, value, hi.bitcast(F32), ALU.subtract)

            def y0_rest(it, n, t):
                hi, lo = y0_pair[t % 2]
                pool.wait_ge(y0_hi, it * COUNT + TILES * n + t + 1)
                rest(lo[:], y0[t % 2][:, :, 1:Q + 1], hi[:]).then_inc(y0_lo, 1)

            def y1a_rest(it, n, t):
                hi, lo = (part[:, 0] for part in y1_pair[t % 2])
                pool.wait_ge(y1a_hi, it * COUNT + TILES * n + t + 1)
                rest(lo, y1[t % 2][:, 0, :, 1:Q + 1], hi).then_inc(y1a_lo, 1)

            def weights_rest(it, n, k):
                pool.wait_ge(w_hi, (it * LAYERS + n // 2) * PH + k + 1)
                rest(w[1][:, k], w_raw[:, k], w[0][:, k]).then_inc(w_lo, 1)

            def iteration(it):
                for n in range(PHASES):
                    if n % 2 == 0:
                        pool.wait_ge(tab_loaded[layer(n)], (it + 1) * (16 * TAB_DMAS))
                    for t in range(TILES):
                        if n < 2:
                            pool.wait_ge(x_loaded[n][t], (it + 1) * 16)
                        else:
                            pool.wait_ge(x_ready, it * COUNT + TILES * (n - 2) + t + 1)
                        scale_x(it, n, t)
                    for t in range(2):
                        y0_rest(it, n, t)
                    for t in range(2):
                        y1a_rest(it, n, t)
                    if n % 2 == 1:
                        weights_rest(it, n, 2)
                        weights_rest(it, n, 3)
                    for t in range(2):
                        y0_rest(it, n, 2 + t)
                    if n % 2 == 0:
                        weights_rest(it, n, 0)
                        weights_rest(it, n, 1)
                    for t in range(2):
                        y1a_rest(it, n, 2 + t)

            iteration(0)
            with pool.Fori(1, ITERS) as it:
                iteration(it)

        @block.scalar
        def _(act):
            a = nc.scalar

            def iteration(it, phases):
                start = it * COUNT
                later = not (isinstance(it, int) and it == 0)

                def tiles(n, t):
                    return start + TILES * n + t

                def products(n, p):
                    return start + PH * n + p

                def factors(l, k, n, t, b):
                    sample = GROUP * (n % 2) + TILE * t + b
                    at, bias_at = table_column(l, T_A + k, sample), table_column(l, T_B + k, sample)
                    return tab[:, at:at + 1], tab[:, bias_at:bias_at + 1]

                def half(n, t, k, y, done, ready):
                    act.wait_ge(done, tiles(n, t + 1))
                    for b in range(TILE):
                        s, c = factors(layer(n), k, n, t, b)
                        ins = a.activation(y[t % 2][:, 0, b, 1:Q + 1], conv_ps[t % 2][0][:, b], ACT.Identity,
                                           bias=c, scale=s)
                    ins.then_inc(ready, 1)

                def up(n, t):
                    half(n, t, 1, y1, up_done, y1a_raw)
                    act.wait_ge(y1_ready, tiles(n, t + 1))
                    a.activation(y1_pair[t % 2][0][:, 0], y1[t % 2][:, 0, :, 1:Q + 1], ACT.Copy).then_inc(y1a_hi, 1)

                def third(n, t):
                    half(n, t, 2, y2, c2_done, y2a_ready)

                def first(n, t):
                    act.wait_ge(c0_done, tiles(n, t + 1))
                    for b in range(TILE):
                        s, c = factors(layer(n), 0, n, t, b)
                        ins = a.activation(y0[t % 2][:, b, 1:Q + 1], conv_ps[t % 2][1][:, b], ACT.Identity,
                                           bias=c, scale=s)
                    ins.then_inc(y0_raw, 1)
                    act.wait_ge(y0_raw, tiles(n, t + 1))
                    a.activation(y0_pair[t % 2][0][:], y0[t % 2][:, :, 1:Q + 1], ACT.Copy).then_inc(y0_hi, 1)

                def weights_hi(n, k):
                    if n % 2 == 0:
                        act.wait_ge(w_loaded, (it * LAYERS + n // 2 + 1) * 16)
                        a.activation(w[0][:, k], w_raw[:, k], ACT.Copy).then_inc(w_hi, 1)

                def turned(n, t):
                    act.wait_ge(tr_done, tiles(n, t + 1))
                    a.activation(turned_cols(0, t), tr_ps[:].rearrange("q b p c -> q p b c"), ACT.Copy).then_inc(y3t_hi, 1)

                def adapter(n):
                    l = layer(n)
                    if l:
                        act.wait_ge(z_done, adapters_before(it, n, (1, 2, 3)) + 1)
                    if l == 1:
                        a.activation(z_raw[:], z_ps[:], ACT.Copy)
                        a.activation(logits[:], logit_ps[0:E1], ACT.Copy).then_inc(z_raw_ready, 1)
                    elif l == 2:
                        a.activation(zt[0][0:Z23], z_ps[0:Z23], ACT.Copy).then_inc(zt_hi, 1)
                    elif l == 3:
                        a.activation(z_raw[0:Z23], z_ps[0:Z23], ACT.Copy).then_inc(z_raw_ready, 1)

                def exponentials(n):
                    if layer(n) == 1:
                        act.wait_ge(exp_in, adapters_before(it, n, (1,)) + 1)
                        a.activation(ex[:], r_a[:], ACT.Exp).then_inc(exp_done, 1)

                def adapter_turned(n):
                    if layer(n) in (1, 3):
                        rows = E1 * R1 if layer(n) == 1 else E3 * R3
                        act.wait_ge(zt_done, adapters_before(it, n, (1, 3)) + 1)
                        a.activation(zt[0][0:rows], zt_ps[0:rows], ACT.Copy).then_inc(zt_hi, 1)

                def linear_out(n):
                    l = layer(n)
                    for p in range(PH):
                        act.wait_ge(lin_done, products(n, p + 1))
                        src = lin_ps[p % 2][:].rearrange("q (b c) -> q b c", c=CH)
                        if l < 3:
                            ins = a.activation(out_t[:, :, p], src, ACT.Identity,
                                               bias=keep["ob"][:, PH * l + p:PH * l + p + 1])
                        else:
                            ins = a.activation(out_t[:, :, p], src, ACT.Copy)
                        ins.then_inc(out_ready, 1)

                for n, convolve, linear in phases:
                    m = n - 1
                    if convolve:
                        if n % 2 == 0:
                            act.wait_ge(tab_loaded[layer(n)], (it + 1) * (16 * TAB_DMAS))
                        first(n, 0)
                        first(n, 1)
                        up(n, 0)
                        up(n, 1)
                    if linear:
                        turned(m, 3)
                    if convolve:
                        third(n, 0)
                        third(n, 1)
                    if linear:
                        adapter(m)
                        exponentials(m)
                    if convolve:
                        first(n, 2)
                    if linear:
                        adapter_turned(m)
                    if convolve:
                        first(n, 3)
                    if linear:
                        linear_out(m)
                    if convolve:
                        weights_hi(n, 0)
                        turned(n, 0)
                        weights_hi(n, 1)
                        up(n, 2)
                        weights_hi(n, 2)
                        turned(n, 1)
                        up(n, 3)
                        weights_hi(n, 3)
                        third(n, 2)
                        third(n, 3)

            load_table(0, 0, act)
            iteration(0, FIRST)
            with act.Fori(1, ITERS) as it:
                iteration(it, STEADY)
            iteration(ITERS, LAST)

        @block.vector
        def _(dve):
            v = nc.vector
            for u in range(2):
                v.memset(y0[u][:, :, 0:HALO:HALO - 1], 0.0)
                for y in (y1[u], y2[u]):
                    v.memset(y[:, :, :, 0:HALO:HALO - 1], 0.0)
            for t in range(TILES):
                ins = v.memset(xs[t][:, :, 0:HALO:HALO - 1], 0.0)
            ins.then_inc(halos_zero, 1)
            def iteration(it, phases):
                start = it * COUNT
                later = not (isinstance(it, int) and it == 0)

                def tiles(n, t):
                    return start + TILES * n + t

                def products(n, p):
                    return start + PH * n + p

                steps, gates_start = 0, 0

                def then(ins):
                    nonlocal steps
                    steps += 1
                    ins.then_inc(rchain, 1)
                    dve.wait_ge(rchain, gates_start + steps)

                def evacuate(n, t, k, dst, src, done, ready):
                    l = layer(n)
                    dve.wait_ge(done, tiles(n, t + 1))
                    for b in range(TILE):
                        sample = GROUP * (n % 2) + TILE * t + b
                        at, bias_at = table_column(l, T_A + k, sample), table_column(l, T_B + k, sample)
                        c = tab[:, bias_at:bias_at + 1] if k < 3 else keep["cb3"][:, l:l + 1]
                        ins = v.tensor_scalar(dst[:, b], src[:, b], tab[:, at:at + 1], c,
                                              ALU.mult, ALU.add)
                    ins.then_inc(ready, 1)

                def up(n, t):
                    evacuate(n, t, 1, y1[t % 2][:, 1, :, 1:Q + 1], conv_ps[t % 2][1], up_done, y1b_raw)
                    at = table_column(layer(n), T_D, GROUP * (n % 2) + TILE * t)
                    for half, q, group, raw in ((0, 1, HI_A.index(0), y1a_raw), (1, Q, HI_B.index(7), y1b_raw)):
                        rows = slice(CH * group, CH * (group + 1))
                        end = y1[t % 2][rows, half, :, q]
                        dve.wait_ge(raw, tiles(n, t + 1))
                        ins = v.tensor_tensor(end, end, tab[rows, at:at + TILE], ALU.add)
                    ins.then_inc(y1_ready, 1)
                    dve.wait_ge(y1_ready, tiles(n, t + 1))
                    hi, lo = (part[:, 1] for part in y1_pair[t % 2])
                    v.tensor_copy(hi, y1[t % 2][:, 1, :, 1:Q + 1]).then_inc(y1b_hi, 1)
                    dve.wait_ge(y1b_hi, tiles(n, t + 1))
                    v.tensor_tensor(lo, y1[t % 2][:, 1, :, 1:Q + 1], hi.bitcast(F32), ALU.subtract).then_inc(y1b_lo, 1)

                def third(n, t):
                    evacuate(n, t, 2, y2[t % 2][:, 1, :, 1:Q + 1], conv_ps[t % 2][1], c2_done, y2b_ready)

                def down(n, t):
                    evacuate(n, t, 3, y3[t % 2][:], conv_ps[t % 2][0], dn_done, y3_ready)

                def residual(n, t):
                    xt, result = x[n % 2][:, TILE * t:TILE * (t + 1)], x[n % 2][:, TILE * t:TILE * (t + 1)]
                    if layer(n) == LAYERS - 1:
                        result = out_tiles[t % 2][:]
                        if t >= 2:
                            dve.wait_ge(stored[n % 2][t - 2], (it + n // PHASES + 1) * 16)
                        elif n % 2:
                            dve.wait_ge(stored[0][t + 2], (it + n // PHASES + 1) * 16)
                        elif later:
                            dve.wait_ge(stored[1][t + 2], it * 16)
                    dve.wait_ge(back_done, tiles(n, t + 1))
                    v.tensor_tensor(result, turned_back[t], xt, ALU.add).then_inc(x_ready, 1)

                def turned(n, t):
                    tile = tr_ps[:].rearrange("q b p c -> q p b c")
                    if t == 2:
                        dve.wait_ge(tr_done, tiles(n, t + 1))
                        v.tensor_copy(turned_cols(0, t), tile).then_inc(y3t_hi, 1)
                    dve.wait_ge(y3t_hi, tiles(n, t + 1))
                    v.tensor_tensor(turned_cols(1, t), tile, turned_cols(0, t).bitcast(F32),
                                    ALU.subtract).then_inc(y3t_ready, 1)

                def wide(small, e):
                    return small[:].unsqueeze(2).broadcast_to((P, TILES, e))

                def best(scores, e, mask, top):
                    iota = keep["iota"][:, 0:e].unsqueeze(1).broadcast_to((P, TILES, e))
                    then(v.tensor_reduce(top[:], scores, AX.X, ALU.max))
                    then(v.tensor_tensor(r_b[:, :, 0:e], scores, wide(top, e), ALU.is_equal))
                    then(v.tensor_tensor(r_b[:, :, 0:e], r_b[:, :, 0:e], iota, ALU.mult))
                    then(v.tensor_reduce(ix[:], r_b[:, :, 0:e], AX.X, ALU.min))
                    then(v.tensor_tensor(mask[:, :, 0:e], wide(ix, e), iota, ALU.is_equal))

                def gated(n):
                    nonlocal steps, gates_start
                    l = layer(n)
                    if l not in (1, 3):
                        return
                    steps, gates_start = 0, gate_steps_before(it, n)
                    e, r = (E1, R1) if l == 1 else (E3, R3)
                    dve.wait_ge(z_turned, adapters_before(it, n, (1, 3)) + 1)
                    if l == 1:
                        then(v.tensor_copy(lg[:], logit_ps[:, 0:TILES * E1].rearrange("p (t e) -> p t e", e=E1)))
                    else:
                        then(v.tensor_tensor(lg[:, :, 0:e], z_ps[:].rearrange("p (t c) -> p t c", c=P)
                                             [:, :, e * r:e * r + e],
                                             keep["eb3"][:].unsqueeze(1).broadcast_to((P, TILES, e)), ALU.add))
                    best(lg[:, :, 0:e], e, oh, m1)
                    if l == 1:
                        v.tensor_tensor(r_a[:], lg[:], wide(m1, e), ALU.subtract).then_inc(exp_in, 1)
                        then(v.scalar_tensor_tensor(out=lg[:], in0=oh[:], scalar=LOWEST, in1=lg[:],
                                                    op0=ALU.mult, op1=ALU.add))
                        best(lg[:], e, oh2, m2)
                        then(v.tensor_tensor(oh[:], oh[:], oh2[:], ALU.add))
                        dve.wait_ge(exp_done, adapters_before(it, n, (1,)) + 1)
                        then(v.tensor_tensor(oh[:], oh[:], ex[:], ALU.mult))
                        then(v.tensor_reduce(den[:], oh[:], AX.X, ALU.add))
                        then(v.reciprocal(den[:], den[:]))
                        then(v.scalar_tensor_tensor(out=oh[:], in0=oh[:], scalar=LORA1_SCALE, in1=wide(den, e),
                                                    op0=ALU.mult, op1=ALU.mult))
                    assert steps == GATE_STEPS[l]
                    for t in range(TILES):
                        ins = v.tensor_tensor(
                            z[:, t, 0:e * r].rearrange("p (e r) -> p e r", r=r),
                            z_ps[:, P * t:P * t + e * r].rearrange("p (e r) -> p e r", r=r),
                            oh[:, t, 0:e].unsqueeze(2).broadcast_to((P, e, r)), ALU.mult)
                    ins.then_inc(z_ready, 1)

                def adapter_turned(n, layers):
                    l = layer(n)
                    if l in layers:
                        rows = (0, E1 * R1, Z23, E3 * R3)[l]
                        src = z_ps if l == 2 else zt_ps
                        dve.wait_ge(zt_hi, adapters_before(it, n, (1, 2, 3)) + 1)
                        v.tensor_tensor(zt[1][0:rows], src[0:rows], zt[0][0:rows].bitcast(F32),
                                        ALU.subtract).then_inc(zt_ready, 1)

                for n, convolve, linear in phases:
                    m = n - 1
                    if convolve:
                        if n % 2 == 0:
                            dve.wait_ge(tab_loaded[layer(n)], (it + 1) * (16 * TAB_DMAS))
                    if linear:
                        down(m, 3)
                        turned(m, 2)
                    if convolve:
                        up(n, 0)
                        up(n, 1)
                    if linear:
                        turned(m, 3)
                    if convolve:
                        third(n, 0)
                        third(n, 1)
                    if linear:
                        adapter_turned(m, (2,))
                        gated(m)
                    if convolve:
                        down(n, 0)
                        down(n, 1)
                    if linear:
                        adapter_turned(m, (1, 3))
                    if convolve:
                        turned(n, 0)
                        up(n, 2)
                    if linear:
                        residual(m, 0)
                        residual(m, 1)
                    if convolve:
                        turned(n, 1)
                        up(n, 3)
                        third(n, 2)
                    if linear:
                        residual(m, 2)
                    if convolve:
                        third(n, 3)
                    if linear:
                        residual(m, 3)
                    if convolve:
                        down(n, 2)

            iteration(0, FIRST)
            with dve.Fori(1, ITERS) as it:
                iteration(it, STEADY)
            iteration(ITERS, LAST)

        @block.tensor
        def _(pe):
            def iteration(it, phases):
                start = it * COUNT
                later = not (isinstance(it, int) and it == 0)

                def tiles(n, t):
                    return start + TILES * n + t

                def products(n, p):
                    return start + PH * n + p

                def mm(out, weights, l, first_block, blocks, rhs, start, stop):
                    return pe.matmul(out, weights[:, l, first_block * CH:(first_block + blocks) * CH], rhs,
                                     start=start, stop=stop, skip_group_check=True)

                wp, wm = keep["wp"], keep["wm"]

                def conv0_pair(n, t):
                    l = layer(n)
                    both = (t, t + 1)
                    for t in both:
                        u = t % 2
                        pe.wait_ge(xs_ready, tiles(n, t + 1))
                        if later or TILES * n + t >= 2:
                            pe.wait_ge(y2b_ready, tiles(n, t - 1))
                        mm(conv_ps[u][1][:], wp, l, C0_MID[u], 4, xs[t][:, :, 1:Q + 1], True, False)
                    for t in both:
                        u = t % 2
                        ps, xt = conv_ps[u][1], xs[t]
                        left, right = ((0, 3), (1, 2))[u]
                        mm(ps[left * CH:(left + 1) * CH], wp, l, C0_LEFT, 1, xt[:, :, 0:Q], False, True)
                        mm(ps[right * CH:(right + 1) * CH], wp, l, C0_RIGHT, 1, xt[:, :, 2:Q + 2],
                           False, True).then_inc(c0_done, 1)

                def middle(ps, weights, l, first_block, y, passes, start, stop):
                    for i, (wi, yi) in enumerate(passes):
                        ins = mm(ps, weights[wi], l, first_block, HALF, y[yi], start and i == 0, stop)
                    return ins

                def conv_up(n, t):
                    l, u = layer(n), t % 2
                    y, weights, parts = y0[u], keep["up"][u], [part[:] for part in y0_pair[u]]
                    pe.wait_ge(y0_hi, tiles(n, t + 1))
                    if later or TILES * n + t >= 2:
                        pe.wait_ge(y3_ready, tiles(n, t - 1))
                    for half in range(2):
                        middle(conv_ps[u][half][:], weights, l, HALF * half, parts, HIGH_INPUT, True, False)
                    mm(conv_ps[u][0][0:2 * CH], wm, l, SIDES[u], 2, y[:, :, 0:Q], False, False)
                    mm(conv_ps[u][1][2 * CH:P], wm, l, SIDES[u] + 2, 2, y[:, :, 2:Q + 2], False, False)
                    pe.wait_ge(y0_lo, tiles(n, t + 1))
                    for half in range(2):
                        ins = middle(conv_ps[u][half][:], weights, l, HALF * half, parts, LOW_INPUT, False, True)
                    ins.then_inc(up_done, 1)

                def conv2(n, t):
                    l, u = layer(n), t % 2
                    ya, yb = y1[u][:, 0], y1[u][:, 1]
                    pa, pb = conv_ps[u]
                    parts = [[part[:, half] for part in y1_pair[u]] for half in range(2)]
                    for half, ready in ((1, y1b_hi), (0, y1a_hi)):
                        pe.wait_ge(ready, tiles(n, t + 1))
                        middle(conv_ps[u][half][:], keep["c2"], l, HALF * half, parts[half], HIGH_INPUT, True, False)
                    pe.wait_ge(y1_ready, tiles(n, t + 1))
                    mm(pa[0:CH], wp, l, C2_SIDES, 1, yb[:, :, 0:Q], False, False)
                    mm(pa[3 * CH:P], wp, l, C2_SIDES + 1, 1, yb[:, :, 1:Q + 1], False, False)
                    mm(pb[CH:2 * CH], wp, l, C2_SIDES + 2, 1, ya[:, :, 1:Q + 1], False, False)
                    mm(pb[2 * CH:3 * CH], wp, l, C2_SIDES + 3, 1, ya[:, :, 2:Q + 2], False, False)
                    for half, ready in ((1, y1b_lo), (0, y1a_lo)):
                        pe.wait_ge(ready, tiles(n, t + 1))
                        ins = middle(conv_ps[u][half][:], keep["c2"], l, HALF * half, parts[half], LOW_INPUT, False, True)
                    ins.then_inc(c2_done, 1)

                def conv_down(n, t):
                    l, u = layer(n), t % 2
                    pe.wait_ge(y2a_ready, tiles(n, t + 1))
                    pe.wait_ge(y2b_ready, tiles(n, t + 1))
                    ya, yb = y2[u][:, 0], y2[u][:, 1]
                    ps = conv_ps[u][0]
                    for o in LO:
                        mm(ps[CH * o:CH * (o + 1)], wm, l, DN + o, 1, ya[:, :, 1:Q + 1] if o < 3 else ya[:, :, 2:Q + 2], True, False)
                    for o in LO:
                        ins = mm(ps[CH * o:CH * (o + 1)], wm, l, DN + 4 + o, 1, yb[:, :, 0:Q] if o == 0 else yb[:, :, 1:Q + 1], False, True)
                    ins.then_inc(dn_done, 1)

                def turn(n, t):
                    pe.wait_ge(y3_ready, tiles(n, t + 1))
                    if later or TILES * n + t:
                        pe.wait_ge(y3t_ready, tiles(n, t))
                    for b in range(TILE):
                        ins = pe.transpose(tr_ps[:, b].rearrange("q p c -> q (p c)"), y3[t % 2][:, b], ident[:])
                    ins.then_inc(tr_done, 1)

                def adapter(n):
                    l, g = layer(n), n % 2
                    if l == 0:
                        return
                    pe.wait_ge(y3t_ready, tiles(n, TILES))
                    pe.wait_ge(x_ready, tiles(n, 0))
                    if l == 2:
                        pe.wait_ge(a2_loaded, (it + 1) * (16 * ADAPTER_DMAS))
                    a_l = (None, keep["a1"], [a[:, g] for a in keep["a2"]], keep["a3"])[l]
                    parts = [(z_ps, 0, P), (logit_ps, P, E1)] if l == 1 else [(z_ps, 0, Z23)]
                    for ps, col, rows in parts:
                        for p in range(PH):
                            for i, (ai, yi) in enumerate(PASSES):
                                ins = pe.matmul(ps[0:rows], a_l[ai][:, p, col:col + rows], y3t[yi][:, p],
                                                start=(p == 0 and i == 0), stop=(p == PH - 1 and i == 2))
                    ins.then_inc(z_done, 1)

                def to_tokens(n):
                    l = layer(n)
                    if l not in (1, 3):
                        return
                    pe.wait_ge(z_raw_ready, adapters_before(it, n, (1, 3)) + 1)
                    for t in range(TILES):
                        tokens = slice(P * t, P * (t + 1))
                        ins = pe.transpose(z_ps[:, tokens], z_raw[:, tokens], ident[:])
                        if l == 1:
                            ins = pe.transpose(logit_ps[:, E1 * t:E1 * (t + 1)], logits[:, tokens], ident[0:E1, 0:E1])
                    ins.then_inc(z_turned, 1)

                def adapter_turn(n):
                    l = layer(n)
                    if l not in (1, 3):
                        return
                    rows = E1 * R1 if l == 1 else E3 * R3
                    pe.wait_ge(z_ready, adapters_before(it, n, (1, 3)) + 1)
                    pe.wait_ge(x_ready, tiles(n, 0))
                    for t in range(TILES):
                        ins = pe.transpose(zt_ps[0:rows, P * t:P * (t + 1)], z[:, t, 0:rows], ident[:])
                    ins.then_inc(zt_done, 1)

                def linear_layer(n):
                    l, g = layer(n), n % 2
                    pe.wait_ge(y3t_ready, tiles(n, TILES))
                    if later or n:
                        pe.wait_ge(x_ready, tiles(n, 0))
                    pe.wait_ge(w_lo, (it * LAYERS + n // 2 + 1) * PH)
                    if l == 2:
                        pe.wait_ge(b2_loaded, (it + 1) * (16 * ADAPTER_DMAS))
                        pe.wait_ge(zt_ready, adapters_before(it, n, (1, 2, 3)) + 1)
                    b_l = (None, keep["b1"], [b[:, g] for b in keep["b2"]], keep["b3"])[l]
                    for p in range(PH):
                        if later or PH * n + p >= 2:
                            pe.wait_ge(out_ready, products(n, p - 1))
                        ps = lin_ps[p % 2]
                        for k in range(PH):
                            for i, (wi, yi) in enumerate(PASSES):
                                ins = pe.matmul(ps[:], w[wi][:, k, p * Q:(p + 1) * Q], y3t[yi][:, k],
                                                start=(k == 0 and i == 0), stop=(k == PH - 1 and i == 2 and l == 0))
                        if l:
                            if p == 0 and l != 2:
                                pe.wait_ge(zt_ready, adapters_before(it, n, (1, 2, 3)) + 1)
                            for i, (bi, zi) in enumerate(PASSES):
                                ins = pe.matmul(ps[:], b_l[bi][:, p * Q:(p + 1) * Q], zt[zi][:], start=False, stop=(i == 2))
                        ins.then_inc(lin_done, 1)

                def turn_back(n, t):
                    if t == 0:
                        pe.wait_ge(out_ready, products(n, PH))
                    elif t == TILES - 1:
                        pe.wait_ge(x_ready, tiles(n, 1))
                    for b in range(TILE):
                        ins = pe.transpose(turned_back[t][:, b], out_t[:, TILE * t + b].rearrange("q p c -> q (p c)"), ident[:])
                    ins.then_inc(back_done, 1)

                for n, convolve, linear in phases:
                    m = n - 1
                    if convolve:
                        conv0_pair(n, 0)
                    if linear:
                        conv_down(m, 3)
                        turn(m, 2)
                    if convolve:
                        conv_up(n, 0)
                    if linear:
                        turn(m, 3)
                    if convolve:
                        conv_up(n, 1)
                        conv2(n, 0)
                        conv2(n, 1)
                    if linear:
                        adapter(m)
                    if convolve:
                        conv_down(n, 0)
                    if linear:
                        to_tokens(m)
                    if convolve:
                        conv0_pair(n, 2)
                        conv_down(n, 1)
                    if linear:
                        adapter_turn(m)
                        linear_layer(m)
                    if convolve:
                        turn(n, 0)
                        conv_up(n, 2)
                    if linear:
                        turn_back(m, 0)
                        turn_back(m, 1)
                    if convolve:
                        turn(n, 1)
                        conv_up(n, 3)
                    if linear:
                        turn_back(m, 2)
                    if convolve:
                        conv2(n, 2)
                    if linear:
                        turn_back(m, 3)
                    if convolve:
                        conv2(n, 3)
                        conv_down(n, 2)

            pe.wait_ge(halos_zero, 1)
            iteration(0, FIRST)
            with pe.Fori(1, ITERS) as it:
                iteration(it, STEADY)
            iteration(ITERS, LAST)


def build(nc, io):
    with ExitStack() as ctx:
        def sb(name, shape, dt=F32):
            return ctx.enter_context(nc.sbuf_tensor(name, shape, dt))

        def pair(name, shape):
            return [sb(f"{name}_{part}", shape, F32R) for part in ("hi", "lo")]

        keep = {
            "wp": sb("w_placed", [P, LAYERS, (NP - NC2) * CH]),
            "wm": sb("w_mixed", [P, LAYERS, (NM - NUP + 2 * UP_SIDES) * CH]),
            "c2": pair("w_c2", [P, LAYERS, NC2 * CH]),
            "up": [pair(f"w_up{u}", [P, LAYERS, UP_MID * CH]) for u in range(2)],
            "ob": sb("ob", [P, 3 * PH]),
            "ident": sb("ident", [P, P]),
            "iota": sb("iota", [P, 8]),
            "a1": pair("a1", [P, PH, Z1]),
            "b1": pair("b1", [P, LEN]),
            "a2": pair("a2_cur", [P, 2, PH, Z23]),
            "b2": pair("b2_cur", [P, 2, LEN]),
            "eb3": sb("eb3", [P, E3]),
            "cb3": sb("cb3", [P, LAYERS]),
            "a3": pair("a3", [P, PH, Z23]),
            "b3": pair("b3", [P, LEN]),
        }
        scratch = {
            "tab": nc.dram_tensor("tab_scratch", [ITERS, CH, LAYERS, KINDS, PAIR], F32).ap(),
            "w0": nc.dram_tensor("w0_scratch", [P, PH, LEN], F32).ap(),
            "a2": nc.dram_tensor("a2_scratch", [2, P, 8, PH, R2], F32).ap(),
            "b2": nc.dram_tensor("b2_scratch", [2, 8, R2, LEN], F32).ap(),
        }
        with ExitStack() as inner:
            setup_program(nc, inner, io, keep, scratch)
        with ExitStack() as inner:
            main_program(nc, inner, io, keep, scratch)


def placed_blocks(cw_in):
    where = block_coefficients(PLACED)
    out = np.zeros((PH, CH, LAYERS, NP, CH), np.float32)
    for g, t, n in zip(*np.nonzero(where)):
        out[g, :, :, n] = cw_in[:, :, PLACED[n][0], t]
    return out.reshape(P, LAYERS, NP * CH)


def host_layout(i):
    c = np.ascontiguousarray

    def cols(a):
        return c(a.reshape(a.shape[:-1] + (Q, PH)).swapaxes(-1, -2).reshape(a.shape))

    def rows(a):
        return c(a.reshape((Q, PH) + a.shape[1:]))

    def rep(a):
        return c(np.tile(a, (PH,) + (1,) * (a.ndim - 1)))

    def every(a):
        return c(np.tile(a[None], (P, 1)))

    cw_oikt = np.stack([i[f"L{l}_cond_weights"] for l in range(LAYERS)])
    cw_in = cw_oikt.transpose(3, 0, 1, 4, 2).copy()
    cw_in[:, :, 1] = cw_oikt[:, 1].transpose(1, 0, 3, 2)
    mod_w = np.stack([i[f"L{l}_cond_mod_w"] for l in range(LAYERS)])
    mod_b = np.stack([i[f"L{l}_cond_mod_b"] for l in range(LAYERS)])
    bias = np.stack([i[f"L{l}_cond_biases"] for l in range(LAYERS)])
    wq = np.zeros((LAYERS, CH, CONVS, TAPS, LAYERS, CH), np.float32)
    for l in range(LAYERS):
        wq[l, :, :, :, l] = cw_oikt[l].transpose(2, 0, 3, 1)
    w_do = [i["L0_ffn_W"].T, i["L1_ffn_W_base"].T, i["L2_ffn_kernel"], i["L3_ffn_W_up"].T]
    w = np.stack([rows(cols(c(m))) for m in w_do], axis=1)
    ob = np.stack([rows(i[k]) for k in ("L0_ffn_bias", "L1_ffn_b_base", "L2_ffn_bias")], axis=1)
    a0 = cols(i["L0_ffn_A"].reshape(256, LEN)).reshape(2, P, LEN).transpose(1, 0, 2)
    b0 = cols(c(i["L0_ffn_Bf"].transpose(0, 2, 1)).reshape(256, LEN)).reshape(2, P, LEN).transpose(1, 0, 2)
    a2 = cols(i["L2_ffn_lora_A"].reshape(512, LEN)).reshape(4, P, LEN).transpose(1, 0, 2)
    b2 = cols(c(i["L2_ffn_lora_B"].transpose(0, 2, 1)).reshape(512, LEN)).reshape(4, P, LEN).transpose(1, 0, 2)
    x = i["x"].reshape(2 * ITERS, GROUP, CH, Q, PH).transpose(0, 4, 2, 1, 3).reshape(2 * ITERS, P, GROUP, Q)
    return {k: c(a) for k, a in {
        "x": x,
        "cond_t": i["cond_512"].T,
        "mod_w": mod_w.transpose(3, 1, 0, 2).reshape(STYLE, CONVS, P),
        "mod_b": mod_b.transpose(0, 2, 1).reshape(P, CONVS),
        "conv_b": bias.transpose(0, 2, 1).reshape(P, CONVS),
        "cb3": rep(bias[:, 3].T),
        "wq": wq.reshape(P, CONVS, TAPS, P),
        "cw": rep(cw_in[:, :, 1::2]),
        "coef": np.repeat(block_coefficients(MIXED), CH, axis=0),
        "wp": placed_blocks(cw_in),
        "w": w, "ob": ob.reshape(P, 3 * PH),
        "a0": a0, "b0": b0,
        "coeffs": np.repeat(i["L0_ffn_coeffs"], 16).reshape(2, P).T,
        "scales": np.repeat(i["L0_ffn_scales"], 16).reshape(2, P).T,
        "ident": np.eye(P, dtype=np.float32),
        "iota": np.tile(np.arange(8, dtype=np.float32) - 8.0, (P, 1)),
        "a1": np.concatenate([rows(i["L1_ffn_lora_A"].reshape(E1 * R1, LEN).T), rows(i["L1_ffn_W_router"].T)], axis=2),
        "b1": cols(c(i["L1_ffn_lora_B"].transpose(0, 2, 1)).reshape(E1 * R1, LEN)),
        "a2": a2, "b2": b2,
        "gate_t": np.repeat(i["L2_ffn_gate"].T, R2, axis=0).reshape(4, P, 8).transpose(1, 0, 2),
        "delta": np.tile(np.eye(R2, dtype=np.float32), (PH, 1)),
        "as2": rows(i["L2_ffn_lora_A_shared"].T),
        "bs2": cols(c(i["L2_ffn_lora_B_shared"].T)),
        "eb3": every(i["L3_ffn_expert_bias"]),
        "a3": np.concatenate([rows(i["L3_ffn_lora_A"].reshape(E3 * R3, LEN).T), rows(i["L3_ffn_gate_w"].T),
                              np.zeros((Q, PH, Z23 - E3 * R3 - E3), np.float32)], axis=2),
        "b3": cols(c(i["L3_ffn_lora_B"].transpose(0, 2, 1)).reshape(E3 * R3, LEN)),
    }.items()}


def kernel(**inputs):
    import concourse.bacc as bacc
    from concourse.bass_utils import run_bass_kernel_spmd

    arrays = host_layout({k: np.asarray(v) for k, v in inputs.items()})
    nc = bacc.Bacc("TRN2", target_bir_lowering=False, num_devices=1)
    io = {k: nc.dram_tensor(f"in_{k}", a.shape, mybir.dt.from_np(a.dtype), kind="ExternalInput").ap()
          for k, a in arrays.items()}
    io["out"] = nc.dram_tensor("out_x", arrays["x"].shape, F32, kind="ExternalOutput").ap()
    build(nc, io)
    r = run_bass_kernel_spmd(nc, [{f"in_{k}": a for k, a in arrays.items()}], core_ids=[0])
    y = r.results[0]["out_x"].reshape(2 * ITERS, PH, CH, GROUP, Q)
    return np.ascontiguousarray(y.transpose(0, 3, 2, 4, 1)).reshape(SAMPLES, CH, LEN)
```
